# Optimizing a Trainium2 kernel written in Bass

```python
import numpy as np
import jax
import jax.numpy as jnp

def _softmax(x, axis=-1):
    return jax.nn.softmax(x, axis=axis)

def _gelu(x):
    return jax.nn.gelu(x, approximate=True)

def _silu(x):
    return jax.nn.silu(x)

def _sigmoid(x):
    return jax.nn.sigmoid(x)

def _layernorm(x, axis=-1, eps=1e-05):
    m = jnp.mean(x, axis=axis, keepdims=True)
    v = jnp.var(x, axis=axis, keepdims=True)
    return (x - m) / jnp.sqrt(v + eps)

def _scatter_add(tgt, idx, src, axis=0):
    return tgt.at[idx].add(src)

def _segment_sum(src, seg, n):
    return jax.ops.segment_sum(src, seg, n)
kernel_name = 'mk_gnn_preln_d4_gnn_r32_8385ec'

def setup_inputs(seed: int=0):
    np.random.seed(seed)
    _w = jnp.asarray

    def _rec_inputs():
        import jax
        import jax.numpy as jnp
        _gk = jax.random.key(seed)
        x = -0.0002117 + 1 * jax.random.normal(jax.random.fold_in(_gk, 1), (3125, 256), jnp.float32)
        src = jax.random.randint(jax.random.fold_in(_gk, 2), (50000,), 0, 3125, jnp.int32)
        dst = jax.random.randint(jax.random.fold_in(_gk, 3), (50000,), 0, 3125, jnp.int32)
        _o = jnp.argsort(dst, stable=True)
        src = src[_o]
        dst = dst[_o]
        edge_weight = jax.random.uniform(jax.random.fold_in(_gk, 13), (50000,), jnp.float32, 0.0, 1)
        return (x, src, dst, edge_weight)
    x, src, dst, edge_weight = _rec_inputs()

    def _L0_gnn_setup():
        import jax, jax.numpy as jnp
        import numpy as np
        N_NODES = 3125
        N_EDGES = 100000
        IN_F = 256
        OUT_F = 256
        key = jax.random.key(seed)
        k1, k2, k3, k4, k5, k6 = jax.random.split(key, 6)
        stdv = 1.0 / np.sqrt(IN_F)
        return {'x': jax.random.normal(k1, (N_NODES, IN_F), dtype=jnp.float32), 'edge_row': jax.random.randint(k2, (N_EDGES,), 0, N_NODES, dtype=jnp.int32), 'edge_col': jax.random.randint(k3, (N_EDGES,), 0, N_NODES, dtype=jnp.int32), 'adj_val': jax.random.uniform(k4, (N_EDGES,), dtype=jnp.float32), 'weight': jax.random.normal(k5, (IN_F, OUT_F), dtype=jnp.float32) * stdv, 'bias': jax.random.normal(k6, (OUT_F,), dtype=jnp.float32)}
    _L0_gnn_all = _L0_gnn_setup()
    _L0_gnn_in = {k: v for k, v in _L0_gnn_all.items() if k in ('weight', 'bias')}
    del _L0_gnn_all

    def _L1_gnn_setup():
        import jax, jax.numpy as jnp
        import numpy as np
        N_NODES = 10000
        N_EDGES = 5000
        N_IN, N_H, N_OUT = (256, 512, 256)
        EPS = 1e-05

        def layer_norm(x, gamma, beta):
            mu = jnp.mean(x, axis=-1, keepdims=True)
            var = jnp.var(x, axis=-1, keepdims=True)
            return (x - mu) * jax.lax.rsqrt(var + EPS) * gamma + beta

        def gcn_conv(x, edge_index, W, b):
            n = x.shape[0]
            xw = x @ W
            loop = jnp.arange(n, dtype=edge_index.dtype)
            src = jnp.concatenate([edge_index[0], loop])
            dst = jnp.concatenate([edge_index[1], loop])
            ones = jnp.ones(src.shape[0], dtype=x.dtype)
            deg = jax.ops.segment_sum(ones, dst, num_segments=n)
            dis = jnp.where(deg > 0, jax.lax.rsqrt(deg), 0.0)
            norm = dis[src] * dis[dst]
            msg = xw[src] * norm[:, None]
            out = jax.ops.segment_sum(msg, dst, num_segments=n)
            return out + b
        key = jax.random.key(seed)
        ks = jax.random.split(key, 12)
        s_in = 1.0 / np.sqrt(N_IN)
        s_h = 1.0 / np.sqrt(N_H)
        return {'x': jax.random.normal(ks[0], (N_NODES, N_IN), dtype=jnp.float32), 'edge_index': jax.random.randint(ks[1], (2, N_EDGES), 0, N_NODES, dtype=jnp.int64), 'gamma1': jnp.ones((N_IN,), jnp.float32), 'beta1': jnp.zeros((N_IN,), jnp.float32), 'gamma2': jnp.ones((N_H,), jnp.float32), 'beta2': jnp.zeros((N_H,), jnp.float32), 'Wm1': jax.random.normal(ks[2], (N_IN, N_H), jnp.float32) * s_in, 'bm1': jnp.zeros((N_H,), jnp.float32), 'W1': jax.random.normal(ks[3], (N_H, N_H), jnp.float32) * s_h, 'b1': jnp.zeros((N_H,), jnp.float32), 'W2': jax.random.normal(ks[4], (N_H, N_H), jnp.float32) * s_h, 'b2': jnp.zeros((N_H,), jnp.float32), 'Wm2': jax.random.normal(ks[5], (N_H, N_OUT), jnp.float32) * s_h, 'bm2': jnp.zeros((N_OUT,), jnp.float32), 'Ws': jax.random.normal(ks[6], (N_IN, N_OUT), jnp.float32) * s_in, 'bs': jnp.zeros((N_OUT,), jnp.float32)}
    _L1_gnn_all = _L1_gnn_setup()
    _L1_gnn_in = {k: v for k, v in _L1_gnn_all.items() if k in ('gamma1', 'beta1', 'gamma2', 'beta2', 'Wm1', 'bm1', 'W1', 'b1', 'W2', 'b2', 'Wm2', 'bm2', 'Ws', 'bs')}
    del _L1_gnn_all

    def _L2_gnn_setup():
        import jax, jax.numpy as jnp
        import numpy as np
        N_NODES = 50000
        NEG_SLOPE = 0.01

        def gcn_conv(x, src, dst, ew, W, b):
            n = x.shape[0]
            h = x @ W
            loop = jnp.arange(n, dtype=src.dtype)
            src_f = jnp.concatenate([src, loop])
            dst_f = jnp.concatenate([dst, loop])
            ew_f = jnp.concatenate([ew, jnp.ones((n,), dtype=ew.dtype)])
            deg = jax.ops.segment_sum(ew_f, dst_f, num_segments=n)
            dis = jnp.where(deg > 0, jax.lax.rsqrt(jnp.where(deg > 0, deg, 1.0)), 0.0)
            norm = dis[src_f] * ew_f * dis[dst_f]
            msg = h[src_f] * norm[:, None]
            out = jax.ops.segment_sum(msg, dst_f, num_segments=n)
            return out + b
        key = jax.random.key(seed)
        k = jax.random.split(key, 6)
        nfeat, nhid, E = (256, 256, 15625)
        x = jax.random.normal(k[0], (N_NODES, nfeat), dtype=jnp.float32)
        edge_index = jax.random.randint(k[1], (2, E), 0, N_NODES, dtype=jnp.int64)
        edge_weight = jax.random.uniform(k[2], (E,), dtype=jnp.float32)
        s1 = 1.0 / np.sqrt(nfeat)
        s2 = 1.0 / np.sqrt(nhid)
        W1 = jax.random.normal(k[3], (nfeat, nhid), dtype=jnp.float32) * s1
        b1 = jnp.zeros((nhid,), dtype=jnp.float32)
        W2 = jax.random.normal(k[4], (nhid, nhid), dtype=jnp.float32) * s2
        b2 = jnp.zeros((nhid,), dtype=jnp.float32)
        return {'x': x, 'edge_index': edge_index, 'edge_weight': edge_weight, 'W1': W1, 'b1': b1, 'W2': W2, 'b2': b2}
    _L2_gnn_all = _L2_gnn_setup()
    _L2_gnn_in = {k: v for k, v in _L2_gnn_all.items() if k in ('W1', 'b1', 'W2', 'b2')}
    del _L2_gnn_all

    def _L3_gnn_setup():
        import jax, jax.numpy as jnp
        import numpy as np
        N_NODES = 10000
        N_EDGES = 10000
        D_IN = 256
        D_OUT = 256
        NEG_SLOPE = 0.2
        key = jax.random.key(seed)
        ks = jax.random.split(key, 8)
        feature = jax.random.normal(ks[0], (N_NODES, D_IN), dtype=jnp.float32)
        src = jax.random.randint(ks[1], (N_EDGES,), 0, N_NODES, dtype=jnp.int32)
        dst = jax.random.randint(ks[2], (N_EDGES,), 0, N_NODES, dtype=jnp.int32)
        s = 1.0 / np.sqrt(D_IN)
        W_s = jax.random.normal(ks[3], (D_OUT, D_IN), dtype=jnp.float32) * s
        W_t = jax.random.normal(ks[4], (D_OUT, D_IN), dtype=jnp.float32) * s
        W_attn = jax.random.normal(ks[5], (1, D_OUT), dtype=jnp.float32) * (1.0 / np.sqrt(D_OUT))
        W_fc = jax.random.normal(ks[6], (D_OUT, D_IN), dtype=jnp.float32) * s
        b_fc = jnp.zeros((D_OUT,), dtype=jnp.float32)
        return {'feature': feature, 'src': src, 'dst': dst, 'W_s': W_s, 'W_t': W_t, 'W_attn': W_attn, 'W_fc': W_fc, 'b_fc': b_fc}
    _L3_gnn_all = _L3_gnn_setup()
    _L3_gnn_in = {k: v for k, v in _L3_gnn_all.items() if k in ('W_s', 'W_t', 'W_attn', 'W_fc', 'b_fc')}
    del _L3_gnn_all
    return {'x': x, 'src': src, 'dst': dst, 'edge_weight': edge_weight, 'L0_gnn_weight': _L0_gnn_in['weight'], 'L0_gnn_bias': _L0_gnn_in['bias'], 'L1_gnn_gamma1': _L1_gnn_in['gamma1'], 'L1_gnn_beta1': _L1_gnn_in['beta1'], 'L1_gnn_gamma2': _L1_gnn_in['gamma2'], 'L1_gnn_beta2': _L1_gnn_in['beta2'], 'L1_gnn_Wm1': _L1_gnn_in['Wm1'], 'L1_gnn_bm1': _L1_gnn_in['bm1'], 'L1_gnn_W1': _L1_gnn_in['W1'], 'L1_gnn_b1': _L1_gnn_in['b1'], 'L1_gnn_W2': _L1_gnn_in['W2'], 'L1_gnn_b2': _L1_gnn_in['b2'], 'L1_gnn_Wm2': _L1_gnn_in['Wm2'], 'L1_gnn_bm2': _L1_gnn_in['bm2'], 'L1_gnn_Ws': _L1_gnn_in['Ws'], 'L1_gnn_bs': _L1_gnn_in['bs'], 'L2_gnn_W1': _L2_gnn_in['W1'], 'L2_gnn_b1': _L2_gnn_in['b1'], 'L2_gnn_W2': _L2_gnn_in['W2'], 'L2_gnn_b2': _L2_gnn_in['b2'], 'L3_gnn_W_s': _L3_gnn_in['W_s'], 'L3_gnn_W_t': _L3_gnn_in['W_t'], 'L3_gnn_W_attn': _L3_gnn_in['W_attn'], 'L3_gnn_W_fc': _L3_gnn_in['W_fc'], 'L3_gnn_b_fc': _L3_gnn_in['b_fc']}

def reference(x, src, dst, edge_weight, L0_gnn_weight, L0_gnn_bias, L1_gnn_gamma1, L1_gnn_beta1, L1_gnn_gamma2, L1_gnn_beta2, L1_gnn_Wm1, L1_gnn_bm1, L1_gnn_W1, L1_gnn_b1, L1_gnn_W2, L1_gnn_b2, L1_gnn_Wm2, L1_gnn_bm2, L1_gnn_Ws, L1_gnn_bs, L2_gnn_W1, L2_gnn_b1, L2_gnn_W2, L2_gnn_b2, L3_gnn_W_s, L3_gnn_W_t, L3_gnn_W_attn, L3_gnn_W_fc, L3_gnn_b_fc):
    import jax
    import jax.numpy as jnp

    def _L0_gnn_ref(x, edge_row, edge_col, adj_val, weight, bias):
        import jax, jax.numpy as jnp
        import numpy as np
        N_NODES = 3125
        N_EDGES = 100000
        IN_F = 256
        OUT_F = 256
        support = x @ weight
        msgs = adj_val[:, None] * support[edge_col]
        output = jax.ops.segment_sum(msgs, edge_row, num_segments=x.shape[0])
        return output + bias

    def _L1_gnn_ref(x, edge_index, gamma1, beta1, gamma2, beta2, Wm1, bm1, W1, b1, W2, b2, Wm2, bm2, Ws, bs):
        import jax, jax.numpy as jnp
        import numpy as np
        N_NODES = 10000
        N_EDGES = 5000
        N_IN, N_H, N_OUT = (256, 512, 256)
        EPS = 1e-05

        def layer_norm(x, gamma, beta):
            mu = jnp.mean(x, axis=-1, keepdims=True)
            var = jnp.var(x, axis=-1, keepdims=True)
            return (x - mu) * jax.lax.rsqrt(var + EPS) * gamma + beta

        def gcn_conv(x, edge_index, W, b):
            n = x.shape[0]
            xw = x @ W
            loop = jnp.arange(n, dtype=edge_index.dtype)
            src = jnp.concatenate([edge_index[0], loop])
            dst = jnp.concatenate([edge_index[1], loop])
            ones = jnp.ones(src.shape[0], dtype=x.dtype)
            deg = jax.ops.segment_sum(ones, dst, num_segments=n)
            dis = jnp.where(deg > 0, jax.lax.rsqrt(deg), 0.0)
            norm = dis[src] * dis[dst]
            msg = xw[src] * norm[:, None]
            out = jax.ops.segment_sum(msg, dst, num_segments=n)
            return out + b
        gelu = lambda t: jax.nn.gelu(t, approximate=False)
        x_copy = x
        h = layer_norm(x, gamma1, beta1)
        h = h @ Wm1 + bm1
        h = gcn_conv(h, edge_index, W1, b1)
        h = gelu(h)
        y = gcn_conv(h, edge_index, W2, b2)
        y = layer_norm(gelu(y), gamma2, beta2)
        y = y @ Wm2 + bm2
        z = x_copy @ Ws + bs + y
        return z

    def _L2_gnn_ref(x, edge_index, edge_weight, W1, b1, W2, b2):
        import jax, jax.numpy as jnp
        import numpy as np
        N_NODES = 50000
        NEG_SLOPE = 0.01

        def gcn_conv(x, src, dst, ew, W, b):
            n = x.shape[0]
            h = x @ W
            loop = jnp.arange(n, dtype=src.dtype)
            src_f = jnp.concatenate([src, loop])
            dst_f = jnp.concatenate([dst, loop])
            ew_f = jnp.concatenate([ew, jnp.ones((n,), dtype=ew.dtype)])
            deg = jax.ops.segment_sum(ew_f, dst_f, num_segments=n)
            dis = jnp.where(deg > 0, jax.lax.rsqrt(jnp.where(deg > 0, deg, 1.0)), 0.0)
            norm = dis[src_f] * ew_f * dis[dst_f]
            msg = h[src_f] * norm[:, None]
            out = jax.ops.segment_sum(msg, dst_f, num_segments=n)
            return out + b
        src, dst = (edge_index[0], edge_index[1])
        h = gcn_conv(x, src, dst, edge_weight, W1, b1)
        h = jnp.where(h >= 0, h, NEG_SLOPE * h)
        out = gcn_conv(h, src, dst, edge_weight, W2, b2)
        return out

    def _L3_gnn_ref(feature, src, dst, W_s, W_t, W_attn, W_fc, b_fc):
        import jax, jax.numpy as jnp
        import numpy as np
        N_NODES = 10000
        N_EDGES = 10000
        D_IN = 256
        D_OUT = 256
        NEG_SLOPE = 0.2
        n = feature.shape[0]
        proj_s = feature @ W_s.T
        proj_t = feature @ W_t.T
        z = proj_s[src] + proj_t[dst]
        z = jnp.where(z >= 0, z, NEG_SLOPE * z)
        e = (z @ W_attn.T)[:, 0]
        m = jax.ops.segment_max(e, src, num_segments=n)
        m = jnp.where(jnp.isfinite(m), m, 0.0)
        e_exp = jnp.exp(e - m[src])
        denom = jax.ops.segment_sum(e_exp, src, num_segments=n)
        alpha = e_exp / denom[src]
        msg = feature[src] * alpha[:, None]
        agg = jax.ops.segment_sum(msg, dst, num_segments=n)
        return agg @ W_fc.T + b_fc
    edge_index = jnp.stack([src, dst])
    h = jnp.maximum(_layernorm(x, axis=-1), 0.0)
    x = x + _L0_gnn_ref(h, src, dst, edge_weight, L0_gnn_weight, L0_gnn_bias)
    h = jnp.maximum(_layernorm(x, axis=-1), 0.0)
    x = x + _L1_gnn_ref(h, edge_index, L1_gnn_gamma1, L1_gnn_beta1, L1_gnn_gamma2, L1_gnn_beta2, L1_gnn_Wm1, L1_gnn_bm1, L1_gnn_W1, L1_gnn_b1, L1_gnn_W2, L1_gnn_b2, L1_gnn_Wm2, L1_gnn_bm2, L1_gnn_Ws, L1_gnn_bs)
    h = jnp.maximum(_layernorm(x, axis=-1), 0.0)
    x = x + _L2_gnn_ref(h, edge_index, edge_weight, L2_gnn_W1, L2_gnn_b1, L2_gnn_W2, L2_gnn_b2)
    h = jnp.maximum(_layernorm(x, axis=-1), 0.0)
    x = x + _L3_gnn_ref(h, src, dst, L3_gnn_W_s, L3_gnn_W_t, L3_gnn_W_attn, L3_gnn_W_fc, L3_gnn_b_fc)
    return x

_drawn_inputs = setup_inputs


def setup_inputs(seed=0):
    import zlib

    import numpy as np

    out = dict(_drawn_inputs(seed))
    spreads = {'L1_gnn_gamma1': (1.0, 0.2),
     'L1_gnn_beta1': (0.0, 0.1),
     'L1_gnn_gamma2': (1.0, 0.2),
     'L1_gnn_beta2': (0.0, 0.337),
     'L1_gnn_bm1': (0.0, 0.1),
     'L1_gnn_b1': (0.0, 0.267),
     'L1_gnn_b2': (0.0, 0.1),
     'L1_gnn_bm2': (0.0, 0.326),
     'L1_gnn_bs': (0.0, 0.356),
     'L2_gnn_b1': (0.0, 0.547),
     'L2_gnn_b2': (0.0, 0.391),
     'L3_gnn_b_fc': (0.0, 0.384)}
    factors = {'L3_gnn_W_s': 16.597}
    for name, (base, spread) in spreads.items():
        noise = np.random.default_rng([zlib.crc32(name.encode()), seed]).standard_normal(out[name].shape)
        drawn = base * np.exp(spread * noise) if base else spread * noise
        out[name] = jnp.asarray(drawn.astype(out[name].dtype))
    for name, factor in factors.items():
        out[name] = (out[name] * factor).astype(out[name].dtype)
    return out
```

```python
import concourse.bass as bass
from concourse import mybir
from contextlib import ExitStack

F32 = mybir.dt.float32
I32 = mybir.dt.int32
ALU = mybir.AluOpType
ACT = mybir.ActivationFunctionType
AX = mybir.AxisListType

NODES = 3125
EDGES = 50000
D = 256
H = 512
P = 125
TILES = NODES // P
COLS = EDGES // P
SLOTS = 128
GROUP = 16
HALF = GROUP // 2
CHUNKS = -(-(EDGES // SLOTS + TILES) // GROUP) * GROUP
STEPS = CHUNKS // GROUP
NPS = 4
REC = 4
EPS = 1e-5
ROUND = 12582912.0
LOW = -float(2 ** 100)
SKIP = 100000.0


def wait_if(eng, sem, value):
    if not isinstance(value, int) or value > 0:
        eng.wait_ge(sem, value)


def peeled(eng, n, body):
    body(0)
    with eng.Fori(1, n - 1) as i:
        body(i)
    body(n - 1)


def over_tiles(eng, body):
    body(0, 0)
    body(1, 1)
    with eng.Fori(1, TILES // 2) as i:
        body(i * 2, 0)
        body(i * 2 + 1, 1)
    body(TILES - 1, 0)


def at(buf, i, lo, hi, parts=P):
    if isinstance(i, int):
        return buf[0:parts, i, lo:hi]
    return buf[0:parts, bass.ds(i, 1), lo:hi].rearrange("p a f -> p (a f)")


def col(buf, i, n=1, parts=P):
    if isinstance(i, int):
        return buf[0:parts, i:i + n]
    return buf[0:parts, bass.ds(i, n)]


def gnn(nc, x_in, src_in, dst_in, ew_in, L0_W, L0_b, g1, be1, g2, be2, Wm1, bm1, W1, b1, W2, b2, Wm2, bm2,
        Ws, bs, L2_W1, L2_b1, L2_W2, L2_b2, L3_Ws, L3_Wt, L3_wa, L3_Wfc, L3_bfc, out):
    ctx = ExitStack()
    with ctx:
        def sb(name, shape, dt=F32):
            return ctx.enter_context(nc.sbuf_tensor(name, shape, dt))

        def sem(name):
            return ctx.enter_context(nc.semaphore(name))

        def dram(name, shape):
            return nc.dram_tensor(name, shape, F32, kind="Internal").ap()

        bank = [ctx.enter_context(nc.psum_tensor(f"bank{i}", [128, 512], F32)) for i in range(8)]

        table0 = dram("table0", (NODES, D))
        table1 = dram("table1", (NODES, D + 1))
        table2 = dram("table2", (NODES, H))
        table3 = dram("table3", (NODES, D))
        table4 = dram("table4", (NODES, D))
        table_ps = dram("table_ps", (NODES, D + 1))
        table_h3 = dram("table_h3", (NODES, D + 2))
        records_d = dram("records_d", (SLOTS * CHUNKS, REC))
        records_s = dram("records_s", (SLOTS * CHUNKS, REC))
        scores = dram("scores", (SLOTS * CHUNKS, 1))

        x = sb("x", [128, TILES, D])
        acc = sb("acc", [128, TILES, H])
        hbuf = sb("hbuf", [128, TILES, D + 1])
        G = sb("G", [128, GROUP, H])
        flat = G[:, :, :].rearrange("p a b -> p (a b)")
        hflat = hbuf[:, :, :].rearrange("p a b -> p (a b)")
        aflat = acc[:, :, :].rearrange("p a b -> p (a b)")
        sel = sb("sel", [128, NPS, P])
        rec = sb("rec", [128, CHUNKS, REC])
        src_idx = sb("src_idx", [128, CHUNKS], I32)
        src_adr = sb("src_adr", [128, CHUNKS], I32)
        dst_loc = sb("dst_loc", [128, CHUNKS])
        ew = sb("ew", [128, CHUNKS])
        src_loc = sb("src_loc", [128, CHUNKS])
        src_tile_i = sb("src_tile_i", [1, CHUNKS], I32)
        dst_idx = hflat[:, 0:CHUNKS].bitcast(I32)
        ew_s = hflat[:, CHUNKS:2 * CHUNKS]
        escore = sb("escore", [128, CHUNKS])
        dst_tile = flat[:, 7680:7680 + CHUNKS]
        dst_tile_i = sb("dst_tile_i", [1, CHUNKS], I32)
        src_tile = sb("src_tile", [128, CHUNKS])
        stage = sb("stage", [128, 2, HALF], I32)
        stage_rec = sb("stage_rec", [128, 2, HALF * REC])
        iota_n = sb("iota_n", [128, CHUNKS])
        ident = sb("ident", [128, 128])
        ones = sb("ones", [128, 128])
        upper = sb("upper", [128, 128])
        stats = sb("stats", [128, TILES, 6])
        cell = sb("cell", [128, GROUP])
        small = sb("small", [128, 12, TILES])
        rstd, nmr, dis1, dis2, deg, mean = (small[0:P, k, :] for k in (0, 1, 2, 3, 4, 11))
        m_rden = sb("m_rden", [128, TILES, 2])
        alpha = sb("alpha", [128, 2, NPS])
        w0 = sb("w0", [128, 2, D])
        wsk = sb("wsk", [128, 2, D])
        w11 = sb("w11", [128, 2, H])
        w2 = sb("w2", [128, 4, H])
        wm2 = sb("wm2", [128, 4, D])
        l2w1 = sb("l2w1", [128, 2, D])
        l2w2 = sb("l2w2", [128, 2, D])
        wst = sb("wst", [128, 2, 2 * D])
        wfc = sb("wfc", [128, 2, D])
        wa_b = sb("wa_b", [128, D + 1])
        wlin = sb("wlin", [128, 2, 2])
        lin = sb("lin", [128, TILES, 2])
        b0_r = sb("b0_r", [1, D])
        bs_r = sb("bs_r", [1, D])
        b11_r = sb("b11_r", [2, H])
        b2_r = sb("b2_r", [1, H])
        bm2_r = sb("bm2_r", [1, D])
        l2b1_r = sb("l2b1_r", [1, D])
        l2b2_r = sb("l2b2_r", [1, D])
        bfc_r = sb("bfc_r", [1, D])
        cols = sb("cols", [128, 24])

        arrived = [sem(f"arrived{r}") for r in range(GROUP)]
        passes = [0]

        def node_rows(table, t, lo, hi):
            if isinstance(t, int):
                return table[t * P:(t + 1) * P, lo:hi]
            return table[bass.ds(t * P, P), lo:hi]

        wm1_raw = aflat[:, 0:1024].rearrange("p (k n) -> p k n", k=2)
        w1_raw = aflat[:, 1024:3072].rearrange("p (k n) -> p k n", k=4)
        wm1_t = aflat[:, 3072:4096].rearrange("p (k n) -> p k n", k=4)
        w3_raw = aflat[:, 4096:5632].rearrange("p (m k n) -> p m k n", m=3, k=2)
        g1_c, be1_c, g2_c, be2_c, bm1_c = cols[:, 0:2], cols[:, 2:4], cols[:, 4:8], cols[:, 8:12], cols[:, 12:16]
        wa_c = cols[:, 20:22]
        dst_i = flat[0:P, 0:400].bitcast(I32)
        src_i = flat[0:P, 400:800].bitcast(I32)
        wgt = flat[0:P, 800:1200]
        node_f = flat[0:P, 1200:1600]
        hi = flat[0:P, 1600:2000]
        tmp = flat[0:P, 2000:2400]
        mask = flat[0:P, 2400:2800]
        rank = flat[0:P, 2800:3200]
        slot = flat[0:P, 3200:3600]
        rec_in_s = aflat[0:P, 6000:7600].rearrange("p (c k) -> p c k", k=REC)
        adr_s = aflat[0:P, 7600:8000].bitcast(I32)
        hot_node = aflat[0:P, 8000:8000 + NPS * P].rearrange("p (a b) -> p a b", a=NPS)
        hot_tile = aflat[0:P, 8600:8600 + NPS * 2 * TILES].rearrange("p (a b) -> p a b", a=NPS)
        adr_d = flat[0:P, 3600:4000].bitcast(I32)
        rec_in = flat[0:P, 4000:5600].rearrange("p (c k) -> p c k", k=REC)
        ones_e = flat[0:P, 5600:6000]
        rec_pad = flat[:, 6000:6000 + 1664].rearrange("p (c k) -> p c k", k=REC)
        count = small[0:P, 5, :]
        start = small[0:P, 6, :]
        bucket_c = small[0:TILES, 7, 0:1]
        first_c = small[0:TILES, 8, 0:1]
        diag = small[0:TILES, 9, 0:TILES]
        atleast = rec[0:TILES, :, 0]

        loaded_x, loaded_e, loaded_w = sem("loaded_x"), sem("loaded_e"), sem("loaded_w")
        const_ready, pad_ready, pad_stored = sem("const_ready"), sem("pad_ready"), sem("pad_stored")
        setup_tr, setup_tc, setup_mm, setup_w = sem("setup_tr"), sem("setup_tc"), sem("setup_mm"), sem("setup_w")

        weights = [(w0, L0_W, 2), (wsk, Ws, 2), (w2, W2, 4), (wm2, Wm2, 4), (l2w1, L2_W1, 2), (l2w2, L2_W2, 2),
                   (wm1_raw, Wm1, 2), (w1_raw, W1, 4), (w3_raw[:, 0, :, :], L3_Ws, 2), (w3_raw[:, 1, :, :], L3_Wt, 2),
                   (w3_raw[:, 2, :, :], L3_Wfc, 2)]
        rows = [(b0_r[0:1, :], L0_b), (bs_r[0:1, :], bs), (b11_r[1:2, :], b1), (b2_r[0:1, :], b2), (bm2_r[0:1, :], bm2),
                (l2b1_r[0:1, :], L2_b1), (l2b2_r[0:1, :], L2_b2), (bfc_r[0:1, :], L3_bfc)]
        columns = [(g1_c, g1), (be1_c, be1), (g2_c, g2), (be2_c, be2), (bm1_c, bm1), (wa_c, L3_wa.rearrange("a n -> (a n)"))]
        n_loads = len(weights) + len(rows) + len(columns) + 1

        with nc.Block() as block:
            @block.sync
            def _(sp):
                sp.dma_start(dst_i, dst_in.rearrange("(p c) -> p c", p=P)).then_inc(loaded_e, 16)
                sp.dma_start(src_i, src_in.rearrange("(p c) -> p c", p=P)).then_inc(loaded_e, 16)
                sp.dma_start(wgt, ew_in.rearrange("(p c) -> p c", p=P)).then_inc(loaded_e, 16)
                sp.dma_start(x[0:P, :, :], x_in.rearrange("(t p) f -> p t f", p=P)).then_inc(loaded_x, 16)
                for tile, w, k in weights:
                    sp.dma_start(tile[:, :, :], w.rearrange("(k p) n -> p k n", k=k)).then_inc(loaded_w, 16)
                sp.wait_ge(pad_ready, REC)
                for records in (records_s, records_d):
                    sp.dma_start(records.rearrange("(p c) k -> p c k", p=SLOTS), rec_pad).then_inc(pad_stored, 16)
                sp.wait_ge(pad_stored, 32)
                sp.wait_ge(loaded_x, 16)
                sp.wait_ge(loaded_e, 48)
                sp.wait_ge(loaded_w, 16 * n_loads)

            @block.scalar
            def _(act):
                for tile, b in rows:
                    act.dma_start(tile, b.rearrange("(a n) -> a n", a=1)).then_inc(loaded_w, 16)
                for tile, b in columns:
                    act.dma_start(tile, b.rearrange("(k p) -> p k", p=128),
                                  allow_slow_non_contiguous=True).then_inc(loaded_w, 16)
                act.dma_start(wa_b[:, 0:D], L3_wa.broadcast_to([128, D])).then_inc(loaded_w, 16)

            @block.gpsimd
            def _(pool):
                nc.gpsimd.iota(iota_n[:, :], [[1, CHUNKS]], base=0, channel_multiplier=0,
                               allow_small_or_imprecise_dtypes=True).then_inc(const_ready, 1)
                nc.gpsimd.memset(ones[:, :], 1.0).then_inc(const_ready, 1)
                nc.gpsimd.memset(ones_e, 1.0).then_inc(const_ready, 1)
                pool.wait_ge(const_ready, 3)
                nc.gpsimd.affine_select(out=ident[:, :], in_=ones[:, :], compare_op=ALU.is_equal, fill=0.0,
                                        base=0, pattern=[[-1, 128]], channel_multiplier=1).then_inc(const_ready, 1)
                nc.gpsimd.affine_select(out=upper[:, :], in_=ones[:, :], compare_op=ALU.is_gt, fill=0.0,
                                        base=0, pattern=[[1, 128]], channel_multiplier=-1).then_inc(const_ready, 1)

            @block.vector
            def _(dve):
                for k, value in enumerate((0.0, -1.0, 0.0, SKIP)):
                    nc.vector.memset(rec_pad[:, :, k], value).then_inc(pad_ready, 1)

        bm_c = cols[:, 16:20]
        lhs_b = flat[:, 0:8]
        with nc.Block() as block:
            blocks = [(wm1_raw[:, i, 128 * j:128 * (j + 1)], wm1_t[:, j, 128 * i:128 * (i + 1)])
                      for j in range(4) for i in range(2)]
            for m, (dest, off) in enumerate(((wst, D), (wst, 0), (wfc, 0))):
                blocks += [(w3_raw[:, m, i, 128 * j:128 * (j + 1)], dest[:, j, off + 128 * i:off + 128 * (i + 1)])
                           for i in range(2) for j in range(2)]
            nb = len(blocks)

            @block.tensor
            def _(pe):
                for n, (a, _o) in enumerate(blocks):
                    wait_if(pe, setup_tc, n - 1)
                    nc.tensor.transpose(bank[n % 2][:, 0:128], a, ident[:, :]).then_inc(setup_tr, 1)
                pe.wait_ge(setup_tc, nb)
                for i in range(2):
                    for j in range(4):
                        last = nc.tensor.matmul(bank[2 + i][:, :], wm1_t[:, j, 128 * i:128 * (i + 1)], w1_raw[:, j, :],
                                                start=(j == 0), stop=(j == 3))
                last.then_inc(setup_mm, 1)
                for j in range(4):
                    for i in range(2):
                        last = nc.tensor.matmul(bank[4][:, j:j + 1], wm1_raw[:, i, 128 * j:128 * (j + 1)],
                                                be1_c[:, i:i + 1], start=(i == 0), stop=(i == 1))
                last.then_inc(setup_mm, 1)
                for j in range(4):
                    last = nc.tensor.matmul(bank[5][0:1, 0:D], be2_c[:, j:j + 1], wm2[:, j, :],
                                            start=(j == 0), stop=(j == 3))
                last.then_inc(setup_mm, 1)
                for m in range(2):
                    for i in range(2):
                        for j in range(2):
                            last = nc.tensor.matmul(bank[7][:, 2 * i + m:2 * i + m + 1],
                                                    w3_raw[:, 1 - m, j, 128 * i:128 * (i + 1)],
                                                    wa_c[:, j:j + 1], start=(j == 0), stop=(j == 1))
                last.then_inc(setup_mm, 1)
                pe.wait_ge(setup_w, 3)
                for j in range(4):
                    last = nc.tensor.matmul(bank[6][0:1, :], bm_c[:, j:j + 1], w1_raw[:, j, :],
                                            start=(j == 0), stop=(j == 3))
                last.then_inc(setup_mm, 1)

            @block.vector
            def _(dve):
                for n, (_a, o) in enumerate(blocks):
                    dve.wait_ge(setup_tr, n + 1)
                    nc.vector.tensor_copy(o, bank[n % 2][:, 0:128]).then_inc(setup_tc, 1)
                dve.wait_ge(setup_mm, 2)
                for i in range(2):
                    nc.vector.tensor_scalar(w11[:, i, :], bank[2 + i][:, :], g1_c[:, i:i + 1], None, ALU.mult)\
                        .then_inc(setup_w, 1)
                nc.vector.tensor_tensor(bm_c, bank[4][:, 0:4], bm1_c, ALU.add).then_inc(setup_w, 1)
                dve.wait_ge(setup_mm, 3)
                nc.vector.tensor_tensor(bm2_r[0:1, :], bank[5][0:1, 0:D], bm2_r[0:1, :], ALU.add)
                for j in range(4):
                    nc.vector.tensor_scalar(wm2[:, j, :], wm2[:, j, :], g2_c[:, j:j + 1], None, ALU.mult)
                dve.wait_ge(setup_mm, 4)
                nc.vector.tensor_scalar(wlin[:, :, :], bank[7][:, 0:4].rearrange("p (a b) -> p a b", a=2), 0.2, None,
                                        ALU.mult)
                nc.vector.tensor_scalar(wa_b[:, 0:D], wa_b[:, 0:D], 0.8, None, ALU.mult)
                nc.vector.memset(wa_b[:, D:D + 1], 1.0)
                dve.wait_ge(setup_mm, 5)
                nc.vector.tensor_copy(b11_r[0:1, :], bank[6][0:1, :])

        def slots_by(nodes_i, name, local, address, tile_of_chunk, tile_i):
            step = sem(f"{name}_step")
            counted, summed, passed = sem(f"{name}_counted"), sem(f"{name}_summed"), sem(f"{name}_passed")

            with nc.Block() as block:
                @block.vector
                def _(dve):
                    done = [0]

                    def link(ins):
                        done[0] += 1
                        ins.then_inc(step, 1)
                        dve.wait_ge(step, done[0])

                    link(nc.vector.tensor_copy(node_f, nodes_i))
                    link(nc.vector.tensor_scalar(tmp, node_f, 1.0 / P, 0.5 / P - 0.5, ALU.mult, ALU.add))
                    link(nc.vector.tensor_scalar(tmp, tmp, ROUND, None, ALU.add))
                    link(nc.vector.tensor_scalar(hi, tmp, ROUND, None, ALU.subtract))
                    nc.vector.scalar_tensor_tensor(local, hi, -float(P), node_f, ALU.mult, ALU.add)
                    with dve.Fori(0, TILES) as b:
                        nc.vector.tensor_scalar(mask, hi, col(iota_n, b), None, ALU.is_equal).then_inc(step, 1)
                        dve.wait_ge(step, b * 2 + (done[0] + 1))
                        nc.vector.tensor_reduce(col(count, b), mask, AX.X, ALU.add).then_inc(step, 1)
                        dve.wait_ge(step, b * 2 + (done[0] + 2))
                    done[0] += 2 * TILES
                    nc.vector.tensor_scalar(tmp[:, 0:1], tmp[:, 0:1], 0.0, None, ALU.mult).then_inc(counted, 1)
                    dve.wait_ge(summed, 1)
                    link(nc.vector.tensor_scalar(bucket_c, bank[0][0:TILES, 0:1], 1.0 / SLOTS,
                                                 (SLOTS - 1.0) / SLOTS - 0.5 + 0.5 / SLOTS, ALU.mult, ALU.add))
                    link(nc.vector.tensor_scalar(bucket_c, bucket_c, ROUND, None, ALU.add))
                    nc.vector.tensor_scalar(bucket_c, bucket_c, ROUND, None, ALU.subtract).then_inc(counted, 1)
                    dve.wait_ge(summed, 2)
                    link(nc.vector.tensor_copy(first_c, bank[1][0:TILES, 0:1]))
                    nc.vector.tensor_scalar(diag, ident[0:TILES, 0:TILES], first_c, float(SLOTS), ALU.mult, ALU.mult)\
                        .then_inc(counted, 1)
                    nc.vector.tensor_scalar(atleast, iota_n[0:TILES, :], first_c, None, ALU.is_ge)\
                        .then_inc(counted, 1)
                    dve.wait_ge(summed, 3)
                    link(nc.vector.tensor_scalar(start, bank[2][0:P, 0:TILES], -1.0, None, ALU.add))
                    dve.wait_ge(summed, 4)
                    link(nc.vector.tensor_scalar(tile_of_chunk[:, :], bank[3][:, 0:CHUNKS], -1.0, None, ALU.add))
                    nc.vector.tensor_copy(tile_i[0:1, :], tile_of_chunk[0:1, :])
                    with dve.Fori(0, TILES) as b:
                        nc.vector.tensor_copy(cell[0:P, 0:1], col(start, b))
                        nc.vector.tensor_scalar(mask, hi, col(iota_n, b), None, ALU.is_equal).then_inc(step, 1)
                        dve.wait_ge(step, b * 3 + (done[0] + 1))
                        nc.vector.tensor_tensor_scan(rank, ones_e, mask, cell[0:P, 0:1], ALU.mult, ALU.add)\
                            .then_inc(step, 1)
                        dve.wait_ge(step, b * 3 + (done[0] + 2))
                        dve.sem_inc(passed, 1)
                        nc.vector.copy_predicated(slot, mask.bitcast(I32), rank).then_inc(step, 1)
                        dve.wait_ge(step, b * 3 + (done[0] + 3))
                    done[0] += 3 * TILES
                    link(nc.vector.tensor_scalar(tmp, slot, 1.0 / SLOTS, 0.5 / SLOTS - 0.5, ALU.mult, ALU.add))
                    link(nc.vector.tensor_scalar(tmp, tmp, ROUND, None, ALU.add))
                    link(nc.vector.tensor_scalar(tmp, tmp, ROUND, None, ALU.subtract))
                    link(nc.vector.scalar_tensor_tensor(slot, tmp, -float(SLOTS), slot, ALU.mult, ALU.add))
                    for a in address:
                        link(nc.vector.scalar_tensor_tensor(a, slot, float(CHUNKS), tmp, ALU.mult, ALU.add))

                @block.tensor
                def _(pe):
                    pe.wait_ge(counted, 1)
                    nc.tensor.matmul(bank[0][0:TILES, 0:1], count, ones[0:P, 0:1], start=True, stop=True)\
                        .then_inc(summed, 1)
                    pe.wait_ge(counted, 2)
                    nc.tensor.matmul(bank[1][0:TILES, 0:1], upper[0:TILES, 0:TILES], bucket_c, start=True, stop=True)\
                        .then_inc(summed, 1)
                    pe.wait_ge(counted, 4)
                    nc.tensor.matmul(bank[2][0:P, 0:TILES], upper[0:P, 0:P], count, start=True, stop=False)
                    nc.tensor.matmul(bank[2][0:P, 0:TILES], ones[0:TILES, 0:P], diag, start=False, stop=True)\
                        .then_inc(summed, 1)
                    nc.tensor.matmul(bank[3][:, 0:CHUNKS], ones[0:TILES, :], atleast, start=True, stop=True)\
                        .then_inc(summed, 1)

        slots_by(src_i, "by_src", rec_in_s[:, :, 1], (adr_s, rec_in[:, :, 3]), src_tile, src_tile_i)
        slots_by(dst_i, "by_dst", rec_in[:, :, 1], (adr_d,), dst_tile, dst_tile_i)

        def norm_vector(dve, src, width, seen, rooted, scale, own):
            with dve.Fori(0, TILES) as t:
                nc.vector.bn_stats(at(stats, t, 0, 6), at(src, t, 0, width)).then_inc(own, 1)
            dve.wait_ge(own, TILES)
            a_, b_ = stats[0:P, :, 1], stats[0:P, :, 4]
            sq_a, sq_b = stats[0:P, :, 2], stats[0:P, :, 5]
            nc.vector.tensor_tensor(nmr, a_, b_, ALU.subtract).then_inc(own, 1)
            nc.vector.tensor_tensor(rstd, sq_a, sq_b, ALU.add).then_inc(own, 1)
            nc.vector.tensor_tensor(mean, a_, b_, ALU.add).then_inc(own, 1)
            dve.wait_ge(own, TILES + 3)
            nc.vector.scalar_tensor_tensor(nmr, nmr, 0.25, nmr, ALU.mult, ALU.mult).then_inc(own, 1)
            nc.vector.tensor_scalar(rstd, rstd, 1.0 / width, EPS, ALU.mult, ALU.add).then_inc(own, 1)
            dve.wait_ge(own, TILES + 5)
            nc.vector.tensor_tensor(rstd, rstd, nmr, ALU.add).then_inc(seen, 1)
            dve.wait_ge(rooted, 1)
            nc.vector.reciprocal(rstd, rstd).then_inc(own, 1)
            dve.wait_ge(own, TILES + 6)
            if scale is not None:
                nc.vector.tensor_tensor(rstd, rstd, scale, ALU.mult).then_inc(own, 1)
                dve.wait_ge(own, TILES + 7)
            nc.vector.scalar_tensor_tensor(nmr, mean, -0.5, rstd, ALU.mult, ALU.mult).then_inc(seen, 1)

        def norm_scalar(act, src, dest, width, func, seen, rooted, applied):
            act.wait_ge(seen, 1)
            nc.scalar.activation(rstd, rstd, ACT.Sqrt).then_inc(rooted, 1)
            act.wait_ge(seen, 2)
            with act.Fori(0, TILES) as t:
                nc.scalar.activation(at(dest, t, 0, width), at(src, t, 0, width), func,
                                     bias=col(nmr, t), scale=col(rstd, t)).then_inc(applied, 1)

        def layer_norm(name, src, dest, width, func, scale=None, store=None):
            own, seen, rooted, applied, stored = (sem(f"{name}_{s}") for s in ("own", "seen", "rooted", "applied", "stored"))
            with nc.Block() as block:
                @block.vector
                def _(dve):
                    norm_vector(dve, src, width, seen, rooted, scale, own)

                @block.scalar
                def _(act):
                    norm_scalar(act, src, dest, width, func, seen, rooted, applied)

                if store is not None:
                    @block.sync
                    def _(sp):
                        table, buf, w = store
                        with sp.Fori(0, TILES) as t:
                            sp.wait_ge(applied, t + 1)
                            sp.dma_start(node_rows(table, t, 0, w), at(buf, t, 0, w)).then_inc(stored, 16)
                        sp.wait_ge(stored, 16 * TILES)

        rec_staged, scatter_go = sem("scatter_staged"), sem("scatter_go")
        sent = [sem("scatter_sent0"), sem("scatter_sent1")]
        rec_built, rec_loaded, unpacked = sem("rec_built"), sem("rec_loaded"), sem("unpacked")
        own, seen, rooted, applied, stored = (sem(f"ln0_{s}") for s in ("own", "seen", "rooted", "applied", "stored"))
        hot, counted_in = sem("hot"), sem("counted_in")
        deg_own, deg_root = sem("deg_own"), sem("deg_root")
        low_deg = small[0:P, 10, :]
        n_groups = COLS // HALF
        with nc.Block() as block:
            @block.gpsimd
            def _(pool):
                def scatter(records, address, rec_flat, before):
                    def step(it):
                        for h in range(2):
                            wait_if(pool, sent[h], it * (16 * HALF) + before * (16 * HALF))
                            g = it * 2 + h
                            nc.gpsimd.tensor_copy(stage[0:P, h, :], col(address, g * HALF, HALF)).then_inc(rec_staged, 1)
                            nc.gpsimd.tensor_copy(stage_rec[0:P, h, :], col(rec_flat, g * (HALF * REC), HALF * REC))\
                                .then_inc(rec_staged, 1)
                            pool.wait_ge(rec_staged, g * 2 + (4 * before + 2))
                            pool.sem_inc(scatter_go, 1)
                            for r in range(HALF):
                                pool.indirect_dma_start(
                                    records, bass.IndirectOffsetOnAxis(ap=stage[0:P, h, r:r + 1], axis=0),
                                    stage_rec[0:P, h, r * REC:(r + 1) * REC], None).then_inc(sent[h], 16)
                    peeled(pool, n_groups // 2, step)
                pool.wait_ge(rec_built, 5)
                scatter(records_s, adr_s, aflat[:, 6000:7600], 0)
                scatter(records_d, adr_d, flat[:, 4000:5600], n_groups // 2)
                for h in range(2):
                    pool.wait_ge(sent[h], 2 * 16 * COLS // 2)

            @block.vector
            def _(dve):
                nc.vector.tensor_copy(rec_in[:, :, 0], src_i).then_inc(rec_built, 1)
                nc.vector.tensor_copy(rec_in[:, :, 2], wgt).then_inc(rec_built, 1)
                nc.vector.tensor_copy(rec_in_s[:, :, 0], dst_i).then_inc(rec_built, 1)
                nc.vector.tensor_copy(rec_in_s[:, :, 2], wgt).then_inc(rec_built, 1)
                nc.vector.memset(rec_in_s[:, :, 3], 0.0).then_inc(rec_built, 1)
                norm_vector(dve, x, D, seen, rooted, None, own)

                def hots(c, q):
                    wait_if(dve, counted_in, c - (NPS - 1))
                    nc.vector.tensor_scalar(hot_node[:, q, :], iota_n[0:P, 0:P], at(rec_in, c, 1, 2), None, ALU.is_equal)
                    nc.vector.tensor_scalar(hot_tile[:, q, 0:TILES], iota_n[0:P, 0:TILES], col(hi, c), col(wgt, c),
                                            ALU.is_equal, ALU.mult)
                    nc.vector.tensor_scalar(hot_tile[:, q, TILES:2 * TILES], iota_n[0:P, 0:TILES], col(hi, c), None,
                                            ALU.is_equal).then_inc(hot, 1)

                def four(i):
                    for q in range(NPS):
                        hots(i * NPS + q, q)
                peeled(dve, COLS // NPS, four)

                dve.wait_ge(counted_in, COLS)
                done = 0
                for n, dis in enumerate((dis2, dis1)):
                    nc.vector.tensor_scalar(dis, bank[5][0:P, n * TILES:(n + 1) * TILES], 1.0, None, ALU.add)\
                        .then_inc(deg_own, 1)
                    dve.wait_ge(deg_own, done + 1)
                    nc.vector.tensor_scalar(low_deg, dis, 0.0, None, ALU.is_gt).then_inc(deg_own, 1)
                    nc.vector.tensor_scalar(deg, dis, 1e-30, None, ALU.max).then_inc(deg_own, 1)
                    dve.wait_ge(deg_root, n + 1)
                    nc.vector.reciprocal(deg, deg).then_inc(deg_own, 1)
                    dve.wait_ge(deg_own, done + 4)
                    nc.vector.tensor_tensor(dis, deg, low_deg, ALU.mult).then_inc(deg_own, 1)
                    dve.wait_ge(deg_own, done + 5)
                    done += 5

            @block.tensor
            def _(pe):
                def add_column(c, q, start, stop):
                    pe.wait_ge(hot, c + 1)
                    nc.tensor.matmul(bank[5][0:P, 0:2 * TILES], hot_node[:, q, :], hot_tile[:, q, :],
                                     start=start, stop=stop).then_inc(counted_in, 1)

                def four(i):
                    for q in range(NPS):
                        add_column(i * NPS + q, q, isinstance(i, int) and i * NPS + q == 0,
                                   isinstance(i, int) and i * NPS + q == COLS - 1)
                peeled(pe, COLS // NPS, four)

            @block.scalar
            def _(act):
                norm_scalar(act, x, hbuf, D, ACT.Relu, seen, rooted, applied)
                for n in range(2):
                    act.wait_ge(deg_own, 5 * n + 3)
                    nc.scalar.activation(deg, deg, ACT.Sqrt).then_inc(deg_root, 1)

            @block.sync
            def _(sp):
                with sp.Fori(0, TILES) as t:
                    sp.wait_ge(applied, t + 1)
                    sp.dma_start(node_rows(table0, t, 0, D), at(hbuf, t, 0, D)).then_inc(stored, 16)
                sp.wait_ge(stored, 16 * TILES)

        def unpack(name, records, fields):
            loaded = sem(f"{name}_loaded")
            with nc.Block() as block:
                @block.sync
                def _(sp):
                    sp.dma_start(rec[:, :, :], records.rearrange("(p c) k -> p c k", p=SLOTS)).then_inc(loaded, 16)

                @block.vector
                def _(dve):
                    nc.vector.memset(acc[:, :, 0:D], 0.0)
                    dve.wait_ge(loaded, 16)
                    for k, field in enumerate(fields):
                        nc.vector.tensor_copy(field, rec[:, :, k])
        unpack("rec_s", records_s, (dst_idx, src_loc[:, :], ew_s))
        unpack("rec_d", records_d, (src_idx[:, :], dst_loc[:, :], ew[:, :], src_adr[:, :]))

        staged, go = sem("gather_staged"), sem("gather_go")

        def gathers(pool, table, width, index, uses, released, before):
            def step(it):
                for h in range(2):
                    wait_if(pool, released, it * GROUP + (before + h * HALF - HALF))
                    nc.gpsimd.tensor_copy(stage[:, h, :], col(index, it * GROUP + h * HALF, HALF, 128))\
                        .then_inc(staged, 1)
                    pool.wait_ge(staged, it * 2 + (2 * uses + h + 1))
                    pool.sem_inc(go, 1)
                    for r in range(h * HALF, (h + 1) * HALF):
                        pool.indirect_dma_start(
                            G[:, r, 0:width], None, table,
                            bass.IndirectOffsetOnAxis(ap=stage[:, h, r - h * HALF:r - h * HALF + 1], axis=0))\
                            .then_inc(arrived[r], 16)
            peeled(pool, STEPS, step)

        built, summed, added = sem("built"), sem("summed"), sem("added")
        weighed, exped = sem("weighed"), sem("exped")
        sums = [0]

        def sum_over_edges(table, width, weight=None, attend=False, by_source=False):
            index, local, tile_i = (dst_idx, src_loc, src_tile_i) if by_source else (src_idx, dst_loc, dst_tile_i)
            uses, before = passes[0], sums[0]
            sums[0] += CHUNKS
            passes[0] += STEPS
            used = D if attend else width

            with nc.Block() as block:
                @block.gpsimd
                def _(pool):
                    gathers(pool, table, width, index, uses, summed, before)

                if attend:
                    @block.scalar
                    def _(act):
                        def step(it):
                            for r in range(GROUP):
                                act.wait_ge(arrived[r], it * 16 + 16 * (uses + 1))
                                wait_if(act, built, it * GROUP + (before + r - NPS + 1))
                                nc.scalar.activation(alpha[:, 0, r % NPS:r % NPS + 1], G[:, r, D:D + 1], ACT.Exp,
                                                     bias=col(escore, it * GROUP + r, 1, 128), scale=-1.0)\
                                    .then_inc(exped, 1)
                                act.wait_ge(exped, it * GROUP + (r + 1))
                                nc.scalar.activation(alpha[:, 1, r % NPS:r % NPS + 1], alpha[:, 0, r % NPS:r % NPS + 1],
                                                     ACT.Copy, scale=G[:, r, D + 1:D + 2]).then_inc(weighed, 1)
                        peeled(act, STEPS, step)

                @block.tensor
                def _(pe):
                    def step(it):
                        for r in range(GROUP):
                            q = r % NPS
                            pe.wait_ge(built, it * GROUP + (before + r + 1))
                            wait_if(pe, added, it * GROUP + (before + r + 1 - NPS))
                            pe.wait_ge(arrived[r], it * 16 + 16 * (uses + 1))
                            nc.tensor.matmul(bank[q][0:P, 0:used], sel[:, q, :], G[:, r, 0:used],
                                             start=True, stop=True).then_inc(summed, 1)
                    peeled(pe, STEPS, step)

                @block.vector
                def _(dve):
                    def build(it, r):
                        c = it * GROUP + r
                        q = r % NPS
                        wait_if(dve, summed, it * GROUP + (before + r + 1 - NPS))
                        if attend:
                            dve.wait_ge(weighed, it * GROUP + (r + 1))
                            w = alpha[:, 1, q:q + 1]
                        else:
                            w = None if weight is None else col(weight, c, 1, 128)
                        if w is None:
                            last = nc.vector.tensor_scalar(sel[:, q, :], iota_n[:, 0:P], col(local, c, 1, 128), None,
                                                           ALU.is_equal)
                        else:
                            last = nc.vector.tensor_scalar(sel[:, q, :], iota_n[:, 0:P], col(local, c, 1, 128), w,
                                                           ALU.is_equal, ALU.mult)
                        last.then_inc(built, 1)

                    def step(it):
                        for r in range(GROUP):
                            if r % 4 == 0:
                                tile = [dve.value_load(col(tile_i, it * GROUP + (r + k), 1, 1),
                                                       min_val=0, max_val=TILES - 1) for k in range(4)]
                            if not (it is LAST and r + 2 >= GROUP):
                                build(it, r + 2)
                            dve.wait_ge(summed, it * GROUP + (before + r + 1))
                            wait_if(dve, added, it * GROUP + (before + r))
                            row = at(acc, tile[r % 4], 0, used)
                            nc.vector.tensor_tensor(row, bank[r % NPS][0:P, 0:used], row, ALU.add)\
                                .then_inc(added, 1)
                    LAST = STEPS - 1
                    build(0, 0)
                    build(0, 1)
                    peeled(dve, STEPS, step)

        xt = G[:, 0:2, :]
        tile_in = sb("tile_in", [128, 2, H + 2])

        turned, copied, multiplied, finished, ready = (sem(f"tiles_{s}") for s in (
            "turned", "copied", "multiplied", "finished", "ready"))
        projected = [0]

        def project(name, src, kt, w, n, bias, finish, on_scalar, aug=None, scale=None, store=None,
                    narrow=None):
            width = 128 * kt + (1 if aug is not None else 0)
            base = projected[0]
            projected[0] += TILES
            if store is not None:
                stored = sem(f"{name}_stored")
            copy = nc.vector if on_scalar else nc.scalar
            with nc.Block() as block:
                @block.tensor
                def _(pe):
                    def turn(t, q):
                        pe.wait_ge(ready, t + (base + 1))
                        wait_if(pe, copied, t + (base - 1))
                        for k in range(kt):
                            last = nc.tensor.transpose(bank[q][:, k * P:(k + 1) * P], tile_in[0:P, q, 128 * k:128 * (k + 1)],
                                                       ident[0:P, 0:P])
                        if aug is not None:
                            last = nc.tensor.transpose(bank[q][0:2, kt * P:(kt + 1) * P], tile_in[0:P, q, 128 * kt:128 * kt + 2],
                                                       ident[0:P, 0:P])
                        last.then_inc(turned, 1)

                    def multiply(t, q):
                        pe.wait_ge(copied, t + (base + 1))
                        wait_if(pe, finished, t + (base - 1))
                        o = bank[2 + q][0:P, 0:n]
                        for k in range(kt):
                            last = nc.tensor.matmul(o, xt[:, q, k * P:(k + 1) * P], w[:, k, 0:n], start=(k == 0),
                                                    stop=(k == kt - 1 and bias is None and aug is None))
                        if bias is not None:
                            last = nc.tensor.matmul(o, ones[0:1, 0:P], bias[0:1, 0:n], start=False, stop=True)
                        if aug is not None:
                            last = nc.tensor.matmul(o, xt[0:2, q, kt * P:(kt + 1) * P], aug[0:2, 0:n],
                                                    start=False, stop=True)
                        if narrow is not None:
                            for k in range(kt):
                                last = nc.tensor.matmul(bank[4 + q][0:P, 0:2], xt[:, q, k * P:(k + 1) * P],
                                                        narrow[0][:, k, :], start=(k == 0), stop=(k == kt - 1))
                        last.then_inc(multiplied, 1)

                    turn(0, 0)
                    turn(1, 1)
                    multiply(0, 0)
                    with pe.Fori(1, TILES // 2) as i:
                        turn(i * 2, 0)
                        multiply(i * 2 - 1, 1)
                        turn(i * 2 + 1, 1)
                        multiply(i * 2, 0)
                    turn(TILES - 1, 0)
                    multiply(TILES - 2, 1)
                    multiply(TILES - 1, 0)

                def copy_tile(eng, t, q):
                    eng.wait_ge(turned, t + (base + 1))
                    wait_if(eng, multiplied, t + (base - 1))
                    parts = ([(128, 0, kt * P)] if kt else []) + ([(2, kt * P, (kt + 1) * P)] if aug is not None else [])
                    for n_part, lo, hi_ in parts:
                        if on_scalar:
                            last = nc.vector.tensor_copy(xt[0:n_part, q, lo:hi_], bank[q][0:n_part, lo:hi_])
                        else:
                            last = nc.scalar.activation(xt[0:n_part, q, lo:hi_], bank[q][0:n_part, lo:hi_], ACT.Copy)
                    last.then_inc(copied, 1)

                def finish_tile(eng, t, q):
                    eng.wait_ge(multiplied, t + (base + 1))
                    if narrow is not None:
                        narrow[1](t, bank[4 + q][0:P, 0:2])
                    finish(t, bank[2 + q][0:P, 0:n]).then_inc(finished, 1)

                def scale_tile(dve, t, q):
                    wait_if(dve, turned, t + (base - 1))
                    nc.vector.tensor_scalar(tile_in[0:P, q, 0:width], at(src, t, 0, width), col(scale, t), None,
                                            ALU.mult).then_inc(ready, 1)

                @block.vector
                def _(dve):
                    handle = copy_tile if on_scalar else finish_tile
                    if scale is None:
                        over_tiles(dve, lambda t, q: handle(dve, t, q))
                        return

                    def pair(i):
                        for q in range(2):
                            handle(dve, i * 2 + q, q)
                            scale_tile(dve, i * 2 + (q + 2), q)
                    scale_tile(dve, 0, 0)
                    scale_tile(dve, 1, 1)
                    pair(0)
                    with dve.Fori(1, TILES // 2 - 1) as i:
                        pair(i)
                    handle(dve, TILES - 3, 0)
                    scale_tile(dve, TILES - 1, 0)
                    handle(dve, TILES - 2, 1)
                    handle(dve, TILES - 1, 0)

                if scale is None:
                    @block.gpsimd
                    def _(pool):
                        def copy_in(t, q):
                            wait_if(pool, turned, t + (base - 1))
                            nc.gpsimd.tensor_copy(tile_in[0:P, q, 0:width], at(src, t, 0, width)).then_inc(ready, 1)
                        over_tiles(pool, copy_in)

                @block.scalar
                def _(act):
                    over_tiles(act, lambda t, q: (finish_tile if on_scalar else copy_tile)(act, t, q))

                if store is not None:
                    @block.sync
                    def _(sp):
                        with sp.Fori(0, TILES) as t:
                            sp.wait_ge(finished, t + (base + 1))
                            table, buf, w_ = store
                            dest = node_rows(table, t, 0, w_)
                            sp.dma_start(dest, at(buf, t, 0, w_)).then_inc(stored, 16)
                        sp.wait_ge(stored, 16 * TILES)

        def add_to_x(t, o):
            return nc.vector.tensor_tensor(at(x, t, 0, D), o, at(x, t, 0, D), ALU.add)

        sum_over_edges(table0, D, weight=ew_s, by_source=True)
        project("l0p", acc, 2, w0, D, b0_r, add_to_x, on_scalar=False)

        layer_norm("ln1", x, hbuf, D, ACT.Relu)
        project("l1s", hbuf, 2, wsk, D, bs_r, add_to_x, on_scalar=False)
        with nc.Block() as block:
            @block.vector
            def _(dve):
                nc.vector.tensor_copy(acc[0:P, :, D], dis1)
                nc.vector.memset(tile_in[:, :, D + 1:D + 2], 1.0)
        layer_norm("ln1b", hbuf, acc, D, ACT.Identity, scale=dis1, store=(table1, acc, D + 1))
        sum_over_edges(table1, D + 1)
        project("l1p", acc, 2, w11, H, None,
                lambda t, o: nc.scalar.activation(at(acc, t, 0, H), o, ACT.Gelu), on_scalar=True,
                aug=b11_r, scale=dis1)

        def last_touch(name, table, width, touch):
            touched, stored = sem(f"{name}_touched"), sem(f"{name}_stored")
            with nc.Block() as block:
                @block.vector
                def _(dve):
                    with dve.Fori(0, TILES) as t:
                        touch(t).then_inc(touched, 1)

                @block.sync
                def _(sp):
                    with sp.Fori(0, TILES) as t:
                        sp.wait_ge(touched, t + 1)
                        sp.dma_start(node_rows(table, t, 0, width), at(acc, t, 0, width)).then_inc(stored, 16)
                    sp.wait_ge(stored, 16 * TILES)

        last_touch("t2", table2, H, lambda t: nc.vector.tensor_scalar(
            at(acc, t, 0, H), at(acc, t, 0, H), col(dis1, t), None, ALU.mult))
        sum_over_edges(table2, H)
        project("l1q", acc, 4, w2, H, b2_r,
                lambda t, o: nc.scalar.activation(at(acc, t, 0, H), o, ACT.Gelu), on_scalar=True,
                scale=dis1)
        layer_norm("ln2", acc, acc, H, ACT.Identity)
        project("l1o", acc, 4, wm2, D, bm2_r, add_to_x, on_scalar=False)

        layer_norm("ln3", x, acc, D, ACT.Relu, scale=dis2, store=(table3, acc, D))
        sum_over_edges(table3, D, weight=ew)
        project("l2p", acc, 2, l2w1, D, l2b1_r,
                lambda t, o: nc.scalar.activation(at(acc, t, 0, D), o, ACT.Copy, scale=col(dis2, t)),
                on_scalar=True, scale=dis2)
        last_touch("t4", table4, D, lambda t: nc.vector.scalar_tensor_tensor(
            at(acc, t, 0, D), at(acc, t, 0, D), 0.01, at(acc, t, 0, D), ALU.mult, ALU.max))
        sum_over_edges(table4, D, weight=ew)
        project("l2q", acc, 2, l2w2, D, l2b2_r, add_to_x, on_scalar=False, scale=dis2)

        layer_norm("ln4", x, hbuf, D, ACT.Relu, store=(table_h3[:, :], hbuf, D))
        project("l3p", hbuf, 2, wst, 2 * D, None,
                lambda t, o: nc.scalar.activation(at(acc, t, 0, 2 * D), o, ACT.Copy), on_scalar=True,
                narrow=(wlin, lambda t, o: nc.scalar.activation(at(lin, t, 0, 2), o, ACT.Copy)))
        ps_stored, col_stored = sem("ps_stored"), sem("col_stored")
        with nc.Block() as block:
            @block.sync
            def _(sp):
                ps_rows = table_ps.rearrange("(t p) f -> p t f", p=P)
                sp.dma_start(ps_rows[:, :, 0:D], acc[0:P, :, D:2 * D]).then_inc(ps_stored, 16)
                sp.dma_start(ps_rows[:, :, D:D + 1], lin[0:P, :, 1:2], allow_slow_non_contiguous=True)\
                    .then_inc(col_stored, 16)
                sp.wait_ge(col_stored, 16)

            @block.vector
            def _(dve):
                dve.wait_ge(ps_stored, 16)
                nc.vector.tensor_copy(acc[0:P, :, D], lin[0:P, :, 0])

        zbuf = hflat[:, 0:4 * (D + 1)].rearrange("p (a b) -> p a b", a=4)
        st = hflat[:, 8 * D:8 * D + 512].rearrange("p (a b) -> p a b", a=4)
        s_built, s_turned, s_copied, expanded, zed, relued, scored, kept = (sem(f"score_{s}") for s in (
            "built", "turned", "copied", "expanded", "zed", "relued", "scored", "kept"))
        uses = passes[0]
        passes[0] += STEPS
        with nc.Block() as block:
            @block.gpsimd
            def _(pool):
                gathers(pool, table_ps, D + 1, src_idx, uses, zed, 0)

            @block.tensor
            def _(pe):
                def turn(it, r):
                    pe.wait_ge(s_built, it * GROUP + (r + 1))
                    wait_if(pe, s_copied, it * GROUP + (r - 1))
                    nc.tensor.transpose(bank[4 + r % 2][0:P, 0:SLOTS], sel[:, r % NPS, :], ident[:, :])\
                        .then_inc(s_turned, 1)

                def expand(it, r, tile):
                    pe.wait_ge(s_copied, it * GROUP + (r + 1))
                    wait_if(pe, zed, it * GROUP + (r + 1 - NPS))
                    nc.tensor.matmul(bank[r % NPS][:, 0:D + 1], st[0:P, r % NPS, :], at(acc, tile, 0, D + 1),
                                     start=True, stop=True).then_inc(expanded, 1)

                def step(it):
                    for r in range(GROUP):
                        turn(it, r)
                        if isinstance(it, int) and it == 0 and r == 0:
                            continue
                        tile = pe.value_load(col(dst_tile_i, it * GROUP + (r - 1), 1, 1), min_val=0, max_val=TILES - 1)
                        expand(it, r - 1, tile)
                peeled(pe, STEPS, step)
                tile = pe.value_load(col(dst_tile_i, CHUNKS - 1, 1, 1), min_val=0, max_val=TILES - 1)
                expand(STEPS - 1, GROUP - 1, tile)

            @block.scalar
            def _(act):
                def copy(it, r):
                    act.wait_ge(s_turned, it * GROUP + (r + 1))
                    wait_if(act, expanded, it * GROUP + (r + 1 - NPS))
                    nc.scalar.activation(st[0:P, r % NPS, :], bank[4 + r % 2][0:P, 0:SLOTS], ACT.Copy)\
                        .then_inc(s_copied, 1)

                def relu(it, r):
                    act.wait_ge(zed, it * GROUP + (r + 1))
                    nc.scalar.activation(zbuf[:, r % NPS, 0:D], zbuf[:, r % NPS, 0:D], ACT.Relu)\
                        .then_inc(relued, 1)

                def step(it):
                    for r in range(GROUP):
                        copy(it, r)
                        if not (isinstance(it, int) and it == 0 and r == 0):
                            relu(it, r - 1)
                peeled(act, STEPS, step)
                relu(STEPS - 1, GROUP - 1)

            @block.vector
            def _(dve):
                def build(it, r):
                    wait_if(dve, s_turned, it * GROUP + (r + 1 - NPS))
                    nc.vector.tensor_scalar(sel[:, r % NPS, :], iota_n[:, 0:P], col(dst_loc, it * GROUP + r, 1, 128),
                                            None, ALU.is_equal).then_inc(s_built, 1)

                def add(it, r):
                    dve.wait_ge(expanded, it * GROUP + (r + 1))
                    wait_if(dve, scored, it * GROUP + (r + 1 - NPS))
                    dve.wait_ge(arrived[r], it * 16 + 16 * (uses + 1))
                    nc.vector.tensor_tensor(zbuf[:, r % NPS, :], bank[r % NPS][:, 0:D + 1], G[:, r, 0:D + 1], ALU.add)\
                        .then_inc(zed, 1)

                def score(it, r):
                    dve.wait_ge(relued, it * GROUP + (r + 1))
                    if r == 0:
                        wait_if(dve, kept, it)
                    nc.vector.tensor_tensor_reduce(out=zbuf[:, r % NPS, :], in0=zbuf[:, r % NPS, :], in1=wa_b[:, :], scale=1.0,
                                                   scalar=0.0, op0=ALU.mult, op1=ALU.add,
                                                   accum_out=cell[:, r % GROUP:r % GROUP + 1]).then_inc(scored, 1)

                def keep(it):
                    dve.wait_ge(scored, it * GROUP + GROUP)
                    nc.vector.tensor_copy(col(escore, it * GROUP, GROUP, 128), cell[:, :]).then_inc(kept, 1)

                def step(it):
                    for r in range(GROUP):
                        if not (it is LAST and r + 2 >= GROUP):
                            build(it, r + 2)
                        add(it, r)
                        if not (isinstance(it, int) and it == 0 and r < 2):
                            score(it, r - 2)
                        if r == 1 and not (isinstance(it, int) and it == 0):
                            keep(it - 1)
                LAST = STEPS - 1
                build(0, 0)
                build(0, 1)
                peeled(dve, STEPS, step)
                score(LAST, GROUP - 2)
                score(LAST, GROUP - 1)
                keep(LAST)

        by_src = flat[:, 1024:1024 + CHUNKS]
        lows = flat[:, 2048:2048 + CHUNKS]
        masked = flat[:, 3072:3072 + CHUNKS]
        pair_staged, pair_go, paired, low_set, low_stored = sem("pair_staged"), sem("pair_go"), sem("paired"), sem("low_set"), sem("low_stored")
        sent = [sem("pair_sent0"), sem("pair_sent1")]
        with nc.Block() as block:
            @block.vector
            def _(dve):
                nc.vector.memset(lows, LOW).then_inc(low_set, 1)
                nc.vector.tensor_scalar(masked, dst_loc[:, :], 0.0, LOW, ALU.is_lt, ALU.mult).then_inc(paired, 1)
                dve.wait_ge(paired, 1)
                nc.vector.tensor_tensor(escore[:, :], escore[:, :], masked, ALU.add).then_inc(paired, 1)

            @block.sync
            def _(sp):
                sp.wait_ge(low_set, 1)
                sp.dma_start(scores.rearrange("(p c) k -> p (c k)", p=SLOTS), lows).then_inc(low_stored, 16)

            @block.gpsimd
            def _(pool):
                pool.wait_ge(low_stored, 16)
                pool.wait_ge(paired, 2)

                def step(it):
                    for h in range(2):
                        wait_if(pool, sent[h], it * (16 * HALF))
                        g = it * 2 + h
                        nc.gpsimd.tensor_copy(stage[:, h, :], col(src_adr, g * HALF, HALF, 128)).then_inc(pair_staged, 1)
                        nc.gpsimd.tensor_copy(stage_rec[:, h, 0:HALF], col(escore, g * HALF, HALF, 128))\
                            .then_inc(pair_staged, 1)
                        pool.wait_ge(pair_staged, g * 2 + 2)
                        pool.sem_inc(pair_go, 1)
                        for r in range(HALF):
                            pool.indirect_dma_start(
                                scores, bass.IndirectOffsetOnAxis(ap=stage[:, h, r:r + 1], axis=0),
                                stage_rec[:, h, r:r + 1], None, bounds_check=SLOTS * CHUNKS - 1,
                                oob_is_err=False).then_inc(sent[h], 16)
                peeled(pool, STEPS, step)
                for h in range(2):
                    pool.wait_ge(sent[h], 16 * CHUNKS // 2)

        QUAD = 4
        quads = CHUNKS // QUAD
        seld = hflat[:, 0:8 * P].rearrange("p (a b) -> p a b", a=8)
        dia = hflat[:, 8 * P:8 * P + 8 * SLOTS].rearrange("p (a b) -> p a b", a=8)
        o = 8 * P + 8 * SLOTS
        high_id = hflat[:, o:o + SLOTS]
        low_row = hflat[0:1, o + SLOTS:o + 2 * SLOTS]
        o += 2 * SLOTS
        cmax = hflat[0:P, o:o + CHUNKS]
        cneg = hflat[0:P, o + CHUNKS:o + 2 * CHUNKS]
        csum = hflat[0:P, o + 2 * CHUNKS:o + 3 * CHUNKS]
        loaded, set_up, q_built, grid, maxed, negged, q_summed = (sem(f"soft_{s}") for s in (
            "loaded", "set_up", "built", "grid", "maxed", "negged", "summed"))
        with nc.Block() as block:
            @block.sync
            def _(sp):
                sp.dma_start(by_src, scores.rearrange("(p c) k -> p (c k)", p=SLOTS)).then_inc(loaded, 16)

            @block.tensor
            def _(pe):
                pe.wait_ge(set_up, 2)

                def quad(i, q):
                    pe.wait_ge(q_built, (i + 1) * QUAD)
                    wait_if(pe, q_summed, (i - 1) * QUAD)
                    for k in range(QUAD):
                        g = bank[q][0:P, k * SLOTS:(k + 1) * SLOTS]
                        s = seld[:, QUAD * q + k, :]
                        nc.tensor.matmul(g, ones[0:1, 0:P], low_row, start=True, stop=False)
                        nc.tensor.matmul(g, s, high_id, start=False, stop=False)
                        last = nc.tensor.matmul(g, s, dia[:, QUAD * q + k, :], start=False, stop=True)
                    last.then_inc(grid, 1)
                quad(0, 0)
                quad(1, 1)
                with pe.Fori(1, quads // 2) as i:
                    quad(i * 2, 0)
                    quad(i * 2 + 1, 1)

            @block.vector
            def _(dve):
                nc.vector.memset(low_row, LOW).then_inc(set_up, 1)
                nc.vector.tensor_scalar(high_id, ident[:, :], -LOW, None, ALU.mult).then_inc(set_up, 1)
                dve.wait_ge(loaded, 16)

                def build(i, q):
                    wait_if(dve, grid, i - 1)
                    for k in range(QUAD):
                        c = i * QUAD + k
                        nc.vector.tensor_scalar(seld[:, QUAD * q + k, :], iota_n[:, 0:P], col(src_loc, c, 1, 128), None,
                                                ALU.is_equal)
                        nc.vector.tensor_scalar(dia[:, QUAD * q + k, :], ident[:, :], col(by_src, c, 1, 128), None,
                                                ALU.mult).then_inc(q_built, 1)

                def largest(i, q):
                    dve.wait_ge(grid, i + 1)
                    nc.vector.tensor_reduce(col(cmax, i * QUAD, QUAD), bank[q][0:P, :].rearrange("p (a b) -> p a b", a=QUAD),
                                            AX.X, ALU.max).then_inc(maxed, 1)
                    dve.wait_ge(maxed, i + 1)
                    nc.vector.tensor_scalar(col(cneg, i * QUAD, QUAD), col(cmax, i * QUAD, QUAD), -1.0, None, ALU.mult)\
                        .then_inc(negged, 1)

                build(0, 0)
                build(1, 1)
                largest(0, 0)
                with dve.Fori(1, quads // 2) as i:
                    build(i * 2, 0)
                    largest(i * 2 - 1, 1)
                    build(i * 2 + 1, 1)
                    largest(i * 2, 0)
                largest(quads - 1, 1)

            @block.scalar
            def _(act):
                def exps(i, q):
                    act.wait_ge(negged, i + 1)
                    for k in range(QUAD):
                        c = i * QUAD + k
                        g = bank[q][0:P, k * SLOTS:(k + 1) * SLOTS]
                        nc.scalar.activation(g, g, ACT.Exp, bias=col(cneg, c), scale=1.0, accum_out=col(csum, c)).then_inc(q_summed, 1)
                with act.Fori(0, quads // 2) as i:
                    exps(i * 2, 0)
                    exps(i * 2 + 1, 1)

        member = flat[0:P, 0:CHUNKS]
        work = flat[0:P, 512:512 + CHUNKS]
        own, maxes, max_exped, used = sem("comb_own"), sem("comb_maxes"), sem("comb_exped"), sem("comb_used")
        mr_stored = sem("mr_stored")
        with nc.Block() as block:
            @block.vector
            def _(dve):
                with dve.Fori(0, TILES) as t:
                    nc.vector.tensor_scalar(member, src_tile[0:P, :], col(iota_n, t), None, ALU.is_equal).then_inc(own, 1)
                    dve.wait_ge(own, t * 7 + 1)
                    nc.vector.tensor_scalar(work, member, -LOW, LOW, ALU.mult, ALU.add).then_inc(own, 1)
                    dve.wait_ge(own, t * 7 + 2)
                    nc.vector.tensor_tensor(work, work, cmax, ALU.add).then_inc(own, 1)
                    dve.wait_ge(own, t * 7 + 3)
                    nc.vector.tensor_reduce(at(m_rden, t, 0, 1), work, AX.X, ALU.max).then_inc(own, 1)
                    dve.wait_ge(own, t * 7 + 4)
                    nc.vector.tensor_scalar(work, work, at(m_rden, t, 0, 1), None, ALU.subtract).then_inc(maxes, 1)
                    dve.wait_ge(max_exped, t + 1)
                    nc.vector.tensor_tensor(work, work, csum, ALU.mult).then_inc(own, 1)
                    dve.wait_ge(own, t * 7 + 5)
                    nc.vector.tensor_tensor(work, work, member, ALU.mult).then_inc(own, 1)
                    dve.wait_ge(own, t * 7 + 6)
                    nc.vector.tensor_reduce(at(m_rden, t, 1, 2), work, AX.X, ALU.add).then_inc(own, 1)
                    dve.wait_ge(own, t * 7 + 7)
                nc.vector.tensor_scalar(m_rden[0:P, :, 1], m_rden[0:P, :, 1], 1e-30, None, ALU.max).then_inc(used, 1)
                dve.wait_ge(used, 1)
                nc.vector.reciprocal(m_rden[0:P, :, 1], m_rden[0:P, :, 1]).then_inc(used, 1)
                nc.vector.memset(acc[0:P, :, 0:D], 0.0)

            @block.scalar
            def _(act):
                with act.Fori(0, TILES) as t:
                    act.wait_ge(maxes, t + 1)
                    nc.scalar.activation(work, work, ACT.Exp).then_inc(max_exped, 1)

            @block.sync
            def _(sp):
                sp.wait_ge(used, 2)
                sp.dma_start(table_h3.rearrange("(t p) f -> p t f", p=P)[:, :, D:D + 2], m_rden[0:P, :, :])\
                    .then_inc(mr_stored, 16)
                sp.wait_ge(mr_stored, 16)

        sum_over_edges(table_h3, D + 2, attend=True)
        project("l3q", acc, 2, wfc, D, bfc_r, add_to_x, on_scalar=False, store=(out, x, D))


_INS = ["x", "src", "dst", "edge_weight", "L0_gnn_weight", "L0_gnn_bias", "L1_gnn_gamma1", "L1_gnn_beta1",
        "L1_gnn_gamma2", "L1_gnn_beta2", "L1_gnn_Wm1", "L1_gnn_bm1", "L1_gnn_W1", "L1_gnn_b1", "L1_gnn_W2",
        "L1_gnn_b2", "L1_gnn_Wm2", "L1_gnn_bm2", "L1_gnn_Ws", "L1_gnn_bs", "L2_gnn_W1", "L2_gnn_b1",
        "L2_gnn_W2", "L2_gnn_b2", "L3_gnn_W_s", "L3_gnn_W_t", "L3_gnn_W_attn", "L3_gnn_W_fc", "L3_gnn_b_fc"]


def kernel(**inputs):
    import numpy as _np
    import concourse.bacc as _bacc
    from concourse import mybir as _mybir
    from concourse.bass_utils import run_bass_kernel_spmd as _run

    nc = _bacc.Bacc("TRN2", target_bir_lowering=False, num_devices=1)
    arrays, args = {}, []
    for name in _INS:
        a = _np.ascontiguousarray(inputs[name])
        arrays[f"in_{name}"] = a
        args.append(nc.dram_tensor(f"in_{name}", a.shape, _mybir.dt.from_np(a.dtype), kind="ExternalInput").ap())
    args.append(nc.dram_tensor("out_x", (NODES, D), _mybir.dt.float32, kind="ExternalOutput").ap())
    gnn(nc, *args)
    r = _run(nc, [arrays], core_ids=[0])
    return r.results[0]["out_x"]
```

```python
import concourse.bass as bass
from concourse import mybir
from contextlib import ExitStack

F32 = mybir.dt.float32
I32 = mybir.dt.int32
ALU = mybir.AluOpType
ACT = mybir.ActivationFunctionType
AX = mybir.AxisListType

NODES = 3125
EDGES = 50000
D = 256
H = 512
P = 125
TILES = NODES // P
COLS = EDGES // P
SLOTS = 128
GROUP = 16
HALF = GROUP // 2
PAIR = 2 * SLOTS
CHUNKS = -(-2 * (EDGES // PAIR + TILES) // GROUP) * GROUP
PAIRS = CHUNKS // 2
STEPS = CHUNKS // GROUP
NPS = 4
NSEL = 8
REC = 4
EPS = 1e-5
ROUND = 12582912.0
LOW = -float(2 ** 100)


def wait_if(eng, sem, value):
    if not isinstance(value, int) or value > 0:
        eng.wait_ge(sem, value)


def peeled(eng, n, body):
    body(0)
    with eng.Fori(1, n - 1) as i:
        body(i)
    body(n - 1)


def valid(it, r):
    return not isinstance(it, int) or 0 <= it * GROUP + r < CHUNKS


def run_steps(eng, ahead, behind, step):
    for r in range(GROUP - ahead, GROUP):
        step(-1, r)
    for r in range(GROUP):
        step(0, r)
    with eng.Fori(1, STEPS - 1) as it:
        for r in range(GROUP):
            step(it, r)
    for r in range(GROUP):
        step(STEPS - 1, r)
    for r in range(behind):
        step(STEPS, r)


def over_tiles(eng, body):
    body(0, 0)
    body(1, 1)
    with eng.Fori(1, TILES // 2) as i:
        body(i * 2, 0)
        body(i * 2 + 1, 1)
    body(TILES - 1, 0)


def at(buf, i, lo, hi, parts=P):
    if isinstance(i, int):
        return buf[0:parts, i, lo:hi]
    return buf[0:parts, bass.ds(i, 1), lo:hi].rearrange("p a f -> p (a f)")


def col(buf, i, n=1, parts=P):
    if isinstance(i, int):
        return buf[0:parts, i:i + n]
    return buf[0:parts, bass.ds(i, n)]


def gnn(nc, x_in, src_in, dst_in, ew_in, L0_W, L0_b, g1, be1, g2, be2, Wm1, bm1, W1, b1, W2, b2, Wm2, bm2,
        Ws, bs, L2_W1, L2_b1, L2_W2, L2_b2, L3_Ws, L3_Wt, L3_wa, L3_Wfc, L3_bfc, out):
    ctx = ExitStack()
    with ctx:
        def sb(name, shape, dt=F32):
            return ctx.enter_context(nc.sbuf_tensor(name, shape, dt))

        def sem(name):
            return ctx.enter_context(nc.semaphore(name))

        def dram(name, shape):
            return nc.dram_tensor(name, shape, F32, kind="Internal").ap()

        bank = [ctx.enter_context(nc.psum_tensor(f"bank{i}", [128, 512], F32)) for i in range(8)]

        table0 = dram("table0", (NODES, D))
        table1 = dram("table1", (NODES, D + 1))
        table2 = dram("table2", (NODES, H))
        table3 = dram("table3", (NODES, D))
        table4 = dram("table4", (NODES, D))
        table_pt = dram("table_pt", (NODES, D + 1))
        table_src = dram("table_src", (NODES, 2 * D + 2))
        records_d = dram("records_d", (SLOTS * CHUNKS, REC))
        records_s = dram("records_s", (SLOTS * CHUNKS, REC))

        x = sb("x", [128, TILES, D])
        acc = sb("acc", [128, TILES, H])
        hbuf = sb("hbuf", [128, TILES, D + 1])
        flat = sb("G", [128, GROUP * (2 * D + 2)])[:, :]
        hflat = hbuf[:, :, :].rearrange("p a b -> p (a b)")
        aflat = acc[:, :, :].rearrange("p a b -> p (a b)")
        sel = sb("sel", [128, NSEL, P])
        rec = flat[:, 0:CHUNKS * REC].rearrange("p (c k) -> p c k", k=REC)
        src_idx = sb("src_idx", [128, CHUNKS], I32)
        dst_loc = sb("dst_loc", [128, CHUNKS])
        ew = sb("ew", [128, CHUNKS])
        dst_idx = sb("dst_idx", [128, CHUNKS], I32)
        src_loc = sb("src_loc", [128, CHUNKS])
        ew_s = sb("ew_s", [128, CHUNKS])
        dst_tile = flat[:, 7792:7792 + PAIRS]
        dst_tile_i = sb("dst_tile_i", [1, PAIRS], I32)
        src_tile_i = sb("src_tile_i", [1, PAIRS], I32)
        src_tile = sb("src_tile", [128, PAIRS])
        stage = sb("stage", [128, 2, HALF], I32)
        stage_rec = sb("stage_rec", [128, 2, HALF * REC])
        iota_n = sb("iota_n", [128, CHUNKS])
        ident = sb("ident", [128, 128])
        ones = sb("ones", [128, 128])
        upper = sb("upper", [128, 128])
        stats = sb("stats", [128, TILES, 6])
        cell = sb("cell", [128, GROUP])
        small = sb("small", [128, 12, TILES])
        rstd, nmr, dis1, dis2, deg, mean = (small[0:P, k, :] for k in (0, 1, 2, 3, 4, 11))
        top = sb("top", [128, TILES])
        escore = sb("escore", [128, GROUP])
        w0 = sb("w0", [128, 2, D])
        wsk = sb("wsk", [128, 2, D])
        w11 = sb("w11", [128, 2, H])
        w2 = sb("w2", [128, 4, H])
        wm2 = sb("wm2", [128, 4, D])
        l2w1 = sb("l2w1", [128, 2, D])
        l2w2 = sb("l2w2", [128, 2, D])
        wst = sb("wst", [128, 2, 2 * D])
        wfc = sb("wfc", [128, 2, D])
        wa_b = sb("wa_b", [128, D + 1])
        wlin = sb("wlin", [128, 2, 2])
        b0_r = sb("b0_r", [1, D])
        bs_r = sb("bs_r", [1, D])
        b11_r = sb("b11_r", [2, H])
        b2_r = sb("b2_r", [1, H])
        bm2_r = sb("bm2_r", [1, D])
        l2b1_r = sb("l2b1_r", [1, D])
        l2b2_r = sb("l2b2_r", [1, D])
        bfc_r = sb("bfc_r", [1, D])
        cols = sb("cols", [128, 24])

        arrived = [sem(f"arrived{r}") for r in range(GROUP)]
        passes = [0]

        def node_rows(table, t, lo, hi):
            if isinstance(t, int):
                return table[t * P:(t + 1) * P, lo:hi]
            return table[bass.ds(t * P, P), lo:hi]

        wm1_raw = aflat[:, 0:1024].rearrange("p (k n) -> p k n", k=2)
        w1_raw = aflat[:, 1024:3072].rearrange("p (k n) -> p k n", k=4)
        wm1_t = aflat[:, 3072:4096].rearrange("p (k n) -> p k n", k=4)
        w3_raw = aflat[:, 4096:5632].rearrange("p (m k n) -> p m k n", m=3, k=2)
        g1_c, be1_c, g2_c, be2_c, bm1_c = cols[:, 0:2], cols[:, 2:4], cols[:, 4:8], cols[:, 8:12], cols[:, 12:16]
        wa_c = cols[:, 20:22]
        dst_i = flat[0:P, 0:400].bitcast(I32)
        src_i = flat[0:P, 400:800].bitcast(I32)
        wgt = flat[0:P, 800:1200]
        node_f = flat[0:P, 1200:1600]
        hi = flat[0:P, 1600:2000]
        tmp = flat[0:P, 2000:2400]
        mask = flat[0:P, 2400:2800]
        rank = flat[0:P, 2800:3200]
        slot = flat[0:P, 3200:3600]
        rec_in_s = aflat[0:P, 6000:7600].rearrange("p (c k) -> p c k", k=REC)
        adr_s = aflat[0:P, 7600:8000].bitcast(I32)
        hot_node = aflat[0:P, 8000:8000 + NPS * P].rearrange("p (a b) -> p a b", a=NPS)
        hot_tile = aflat[0:P, 8600:8600 + NPS * 2 * TILES].rearrange("p (a b) -> p a b", a=NPS)
        adr_d = flat[0:P, 3600:4000].bitcast(I32)
        rec_in = flat[0:P, 4000:5600].rearrange("p (c k) -> p c k", k=REC)
        ones_e = flat[0:P, 5600:6000]
        rec_pad = flat[:, 6000:6000 + CHUNKS * REC].rearrange("p (c k) -> p c k", k=REC)
        count = small[0:P, 5, :]
        start = small[0:P, 6, :]
        bucket_c = small[0:TILES, 7, 0:1]
        first_c = small[0:TILES, 8, 0:1]
        diag = small[0:TILES, 9, 0:TILES]
        atleast = aflat[0:TILES, 8800:8800 + PAIRS]

        loaded_x, loaded_e, loaded_w = sem("loaded_x"), sem("loaded_e"), sem("loaded_w")
        const_ready, pad_ready, pad_stored = sem("const_ready"), sem("pad_ready"), sem("pad_stored")
        setup_tr, setup_tc, setup_mm, setup_w = sem("setup_tr"), sem("setup_tc"), sem("setup_mm"), sem("setup_w")

        weights = [(w0, L0_W, 2), (wsk, Ws, 2), (w2, W2, 4), (wm2, Wm2, 4), (l2w1, L2_W1, 2), (l2w2, L2_W2, 2),
                   (wm1_raw, Wm1, 2), (w1_raw, W1, 4), (w3_raw[:, 0, :, :], L3_Ws, 2), (w3_raw[:, 1, :, :], L3_Wt, 2),
                   (w3_raw[:, 2, :, :], L3_Wfc, 2)]
        rows = [(b0_r[0:1, :], L0_b), (bs_r[0:1, :], bs), (b11_r[1:2, :], b1), (b2_r[0:1, :], b2), (bm2_r[0:1, :], bm2),
                (l2b1_r[0:1, :], L2_b1), (l2b2_r[0:1, :], L2_b2), (bfc_r[0:1, :], L3_bfc)]
        columns = [(g1_c, g1), (be1_c, be1), (g2_c, g2), (be2_c, be2), (bm1_c, bm1), (wa_c, L3_wa.rearrange("a n -> (a n)"))]
        n_loads = len(weights) + len(rows) + len(columns) + 1

        with nc.Block() as block:
            @block.sync
            def _(sp):
                sp.dma_start(dst_i, dst_in.rearrange("(p c) -> p c", p=P)).then_inc(loaded_e, 16)
                sp.dma_start(src_i, src_in.rearrange("(p c) -> p c", p=P)).then_inc(loaded_e, 16)
                sp.dma_start(wgt, ew_in.rearrange("(p c) -> p c", p=P)).then_inc(loaded_e, 16)
                sp.dma_start(x[0:P, :, :], x_in.rearrange("(t p) f -> p t f", p=P)).then_inc(loaded_x, 16)
                for tile, w, k in weights:
                    sp.dma_start(tile[:, :, :], w.rearrange("(k p) n -> p k n", k=k)).then_inc(loaded_w, 16)
                sp.wait_ge(pad_ready, REC)
                for records in (records_s, records_d):
                    sp.dma_start(records.rearrange("(p c) k -> p c k", p=SLOTS), rec_pad).then_inc(pad_stored, 16)
                sp.wait_ge(pad_stored, 32)
                sp.wait_ge(loaded_x, 16)
                sp.wait_ge(loaded_e, 48)
                sp.wait_ge(loaded_w, 16 * n_loads)

            @block.scalar
            def _(act):
                for tile, b in rows:
                    act.dma_start(tile, b.rearrange("(a n) -> a n", a=1)).then_inc(loaded_w, 16)
                for tile, b in columns:
                    act.dma_start(tile, b.rearrange("(k p) -> p k", p=128),
                                  allow_slow_non_contiguous=True).then_inc(loaded_w, 16)
                act.dma_start(wa_b[:, 0:D], L3_wa.broadcast_to([128, D])).then_inc(loaded_w, 16)

            @block.gpsimd
            def _(pool):
                nc.gpsimd.iota(iota_n[:, :], [[1, CHUNKS]], base=0, channel_multiplier=0,
                               allow_small_or_imprecise_dtypes=True).then_inc(const_ready, 1)
                nc.gpsimd.memset(ones[:, :], 1.0).then_inc(const_ready, 1)
                nc.gpsimd.memset(ones_e, 1.0).then_inc(const_ready, 1)
                pool.wait_ge(const_ready, 3)
                nc.gpsimd.affine_select(out=ident[:, :], in_=ones[:, :], compare_op=ALU.is_equal, fill=0.0,
                                        base=0, pattern=[[-1, 128]], channel_multiplier=1).then_inc(const_ready, 1)
                nc.gpsimd.affine_select(out=upper[:, :], in_=ones[:, :], compare_op=ALU.is_gt, fill=0.0,
                                        base=0, pattern=[[1, 128]], channel_multiplier=-1).then_inc(const_ready, 1)

            @block.vector
            def _(dve):
                for k, value in enumerate((0.0, -1.0, 0.0, 0.0)):
                    nc.vector.memset(rec_pad[:, :, k], value).then_inc(pad_ready, 1)

        bm_c = cols[:, 16:20]
        lhs_b = flat[:, 0:8]
        with nc.Block() as block:
            blocks = [(wm1_raw[:, i, 128 * j:128 * (j + 1)], wm1_t[:, j, 128 * i:128 * (i + 1)])
                      for j in range(4) for i in range(2)]
            for m, (dest, off) in enumerate(((wst, 0), (wst, D), (wfc, 0))):
                blocks += [(w3_raw[:, m, i, 128 * j:128 * (j + 1)], dest[:, j, off + 128 * i:off + 128 * (i + 1)])
                           for i in range(2) for j in range(2)]
            nb = len(blocks)

            @block.tensor
            def _(pe):
                for n, (a, _o) in enumerate(blocks):
                    wait_if(pe, setup_tc, n - 1)
                    nc.tensor.transpose(bank[n % 2][:, 0:128], a, ident[:, :]).then_inc(setup_tr, 1)
                pe.wait_ge(setup_tc, nb)
                for i in range(2):
                    for j in range(4):
                        last = nc.tensor.matmul(bank[2 + i][:, :], wm1_t[:, j, 128 * i:128 * (i + 1)], w1_raw[:, j, :],
                                                start=(j == 0), stop=(j == 3))
                last.then_inc(setup_mm, 1)
                for j in range(4):
                    for i in range(2):
                        last = nc.tensor.matmul(bank[4][:, j:j + 1], wm1_raw[:, i, 128 * j:128 * (j + 1)],
                                                be1_c[:, i:i + 1], start=(i == 0), stop=(i == 1))
                last.then_inc(setup_mm, 1)
                for j in range(4):
                    last = nc.tensor.matmul(bank[5][0:1, 0:D], be2_c[:, j:j + 1], wm2[:, j, :],
                                            start=(j == 0), stop=(j == 3))
                last.then_inc(setup_mm, 1)
                for m in range(2):
                    for i in range(2):
                        for j in range(2):
                            last = nc.tensor.matmul(bank[7][:, 2 * i + m:2 * i + m + 1],
                                                    w3_raw[:, m, j, 128 * i:128 * (i + 1)],
                                                    wa_c[:, j:j + 1], start=(j == 0), stop=(j == 1))
                last.then_inc(setup_mm, 1)
                pe.wait_ge(setup_w, 3)
                for j in range(4):
                    last = nc.tensor.matmul(bank[6][0:1, :], bm_c[:, j:j + 1], w1_raw[:, j, :],
                                            start=(j == 0), stop=(j == 3))
                last.then_inc(setup_mm, 1)

            @block.vector
            def _(dve):
                for n, (_a, o) in enumerate(blocks):
                    dve.wait_ge(setup_tr, n + 1)
                    nc.vector.tensor_copy(o, bank[n % 2][:, 0:128]).then_inc(setup_tc, 1)
                dve.wait_ge(setup_mm, 2)
                for i in range(2):
                    nc.vector.tensor_scalar(w11[:, i, :], bank[2 + i][:, :], g1_c[:, i:i + 1], None, ALU.mult)\
                        .then_inc(setup_w, 1)
                nc.vector.tensor_tensor(bm_c, bank[4][:, 0:4], bm1_c, ALU.add).then_inc(setup_w, 1)
                dve.wait_ge(setup_mm, 3)
                nc.vector.tensor_tensor(bm2_r[0:1, :], bank[5][0:1, 0:D], bm2_r[0:1, :], ALU.add)
                for j in range(4):
                    nc.vector.tensor_scalar(wm2[:, j, :], wm2[:, j, :], g2_c[:, j:j + 1], None, ALU.mult)
                dve.wait_ge(setup_mm, 4)
                nc.vector.tensor_scalar(wlin[:, :, :], bank[7][:, 0:4].rearrange("p (a b) -> p a b", a=2), 0.2, None,
                                        ALU.mult)
                nc.vector.tensor_scalar(wa_b[:, 0:D], wa_b[:, 0:D], 0.8, None, ALU.mult)
                nc.vector.memset(wa_b[:, D:D + 1], 1.0)
                dve.wait_ge(setup_mm, 5)
                nc.vector.tensor_copy(b11_r[0:1, :], bank[6][0:1, :])

        def slots_by(nodes_i, name, local, address, tile_of_pair, tile_i):
            step = sem(f"{name}_step")
            counted, summed, passed = sem(f"{name}_counted"), sem(f"{name}_summed"), sem(f"{name}_passed")

            with nc.Block() as block:
                @block.vector
                def _(dve):
                    done = [0]

                    def link(ins):
                        done[0] += 1
                        ins.then_inc(step, 1)
                        dve.wait_ge(step, done[0])

                    link(nc.vector.tensor_copy(node_f, nodes_i))
                    link(nc.vector.tensor_scalar(tmp, node_f, 1.0 / P, 0.5 / P - 0.5, ALU.mult, ALU.add))
                    link(nc.vector.tensor_scalar(tmp, tmp, ROUND, None, ALU.add))
                    link(nc.vector.tensor_scalar(hi, tmp, ROUND, None, ALU.subtract))
                    nc.vector.scalar_tensor_tensor(local, hi, -float(P), node_f, ALU.mult, ALU.add)
                    with dve.Fori(0, TILES) as b:
                        nc.vector.tensor_scalar(mask, hi, col(iota_n, b), None, ALU.is_equal).then_inc(step, 1)
                        dve.wait_ge(step, b * 2 + (done[0] + 1))
                        nc.vector.tensor_reduce(col(count, b), mask, AX.X, ALU.add).then_inc(step, 1)
                        dve.wait_ge(step, b * 2 + (done[0] + 2))
                    done[0] += 2 * TILES
                    nc.vector.tensor_scalar(tmp[:, 0:1], tmp[:, 0:1], 0.0, None, ALU.mult).then_inc(counted, 1)
                    dve.wait_ge(summed, 1)
                    link(nc.vector.tensor_scalar(bucket_c, bank[0][0:TILES, 0:1], 1.0 / PAIR,
                                                 (PAIR - 1.0) / PAIR - 0.5 + 0.5 / PAIR, ALU.mult, ALU.add))
                    link(nc.vector.tensor_scalar(bucket_c, bucket_c, ROUND, None, ALU.add))
                    nc.vector.tensor_scalar(bucket_c, bucket_c, ROUND, None, ALU.subtract).then_inc(counted, 1)
                    dve.wait_ge(summed, 2)
                    link(nc.vector.tensor_copy(first_c, bank[1][0:TILES, 0:1]))
                    nc.vector.tensor_scalar(diag, ident[0:TILES, 0:TILES], first_c, float(PAIR), ALU.mult, ALU.mult)\
                        .then_inc(counted, 1)
                    nc.vector.tensor_scalar(atleast, iota_n[0:TILES, 0:PAIRS], first_c, None, ALU.is_ge)\
                        .then_inc(counted, 1)
                    dve.wait_ge(summed, 3)
                    link(nc.vector.tensor_scalar(start, bank[2][0:P, 0:TILES], -1.0, None, ALU.add))
                    dve.wait_ge(summed, 4)
                    link(nc.vector.tensor_scalar(tile_of_pair, bank[3][:, 0:PAIRS], -1.0, None, ALU.add))
                    nc.vector.tensor_copy(tile_i[0:1, :], tile_of_pair[0:1, :])
                    with dve.Fori(0, TILES) as b:
                        nc.vector.tensor_copy(cell[0:P, 0:1], col(start, b))
                        nc.vector.tensor_scalar(mask, hi, col(iota_n, b), None, ALU.is_equal).then_inc(step, 1)
                        dve.wait_ge(step, b * 3 + (done[0] + 1))
                        nc.vector.tensor_tensor_scan(rank, ones_e, mask, cell[0:P, 0:1], ALU.mult, ALU.add)\
                            .then_inc(step, 1)
                        dve.wait_ge(step, b * 3 + (done[0] + 2))
                        dve.sem_inc(passed, 1)
                        nc.vector.copy_predicated(slot, mask.bitcast(I32), rank).then_inc(step, 1)
                        dve.wait_ge(step, b * 3 + (done[0] + 3))
                    done[0] += 3 * TILES
                    link(nc.vector.tensor_scalar(tmp, slot, 1.0 / SLOTS, 0.5 / SLOTS - 0.5, ALU.mult, ALU.add))
                    link(nc.vector.tensor_scalar(tmp, tmp, ROUND, None, ALU.add))
                    link(nc.vector.tensor_scalar(tmp, tmp, ROUND, None, ALU.subtract))
                    link(nc.vector.scalar_tensor_tensor(slot, tmp, -float(SLOTS), slot, ALU.mult, ALU.add))
                    for a in address:
                        link(nc.vector.scalar_tensor_tensor(a, slot, float(CHUNKS), tmp, ALU.mult, ALU.add))

                @block.tensor
                def _(pe):
                    pe.wait_ge(counted, 1)
                    nc.tensor.matmul(bank[0][0:TILES, 0:1], count, ones[0:P, 0:1], start=True, stop=True)\
                        .then_inc(summed, 1)
                    pe.wait_ge(counted, 2)
                    nc.tensor.matmul(bank[1][0:TILES, 0:1], upper[0:TILES, 0:TILES], bucket_c, start=True, stop=True)\
                        .then_inc(summed, 1)
                    pe.wait_ge(counted, 4)
                    nc.tensor.matmul(bank[2][0:P, 0:TILES], upper[0:P, 0:P], count, start=True, stop=False)
                    nc.tensor.matmul(bank[2][0:P, 0:TILES], ones[0:TILES, 0:P], diag, start=False, stop=True)\
                        .then_inc(summed, 1)
                    nc.tensor.matmul(bank[3][:, 0:PAIRS], ones[0:TILES, :], atleast, start=True, stop=True)\
                        .then_inc(summed, 1)

        slots_by(src_i, "by_src", rec_in_s[:, :, 1], (adr_s,), src_tile[:, :], src_tile_i)
        slots_by(dst_i, "by_dst", rec_in[:, :, 1], (adr_d,), dst_tile, dst_tile_i)

        def norm_vector(dve, src, width, seen, rooted, scale, own):
            with dve.Fori(0, TILES) as t:
                nc.vector.bn_stats(at(stats, t, 0, 6), at(src, t, 0, width)).then_inc(own, 1)
            dve.wait_ge(own, TILES)
            a_, b_ = stats[0:P, :, 1], stats[0:P, :, 4]
            sq_a, sq_b = stats[0:P, :, 2], stats[0:P, :, 5]
            nc.vector.tensor_tensor(nmr, a_, b_, ALU.subtract).then_inc(own, 1)
            nc.vector.tensor_tensor(rstd, sq_a, sq_b, ALU.add).then_inc(own, 1)
            nc.vector.tensor_tensor(mean, a_, b_, ALU.add).then_inc(own, 1)
            dve.wait_ge(own, TILES + 3)
            nc.vector.scalar_tensor_tensor(nmr, nmr, 0.25, nmr, ALU.mult, ALU.mult).then_inc(own, 1)
            nc.vector.tensor_scalar(rstd, rstd, 1.0 / width, EPS, ALU.mult, ALU.add).then_inc(own, 1)
            dve.wait_ge(own, TILES + 5)
            nc.vector.tensor_tensor(rstd, rstd, nmr, ALU.add).then_inc(seen, 1)
            dve.wait_ge(rooted, 1)
            nc.vector.reciprocal(rstd, rstd).then_inc(own, 1)
            dve.wait_ge(own, TILES + 6)
            if scale is not None:
                nc.vector.tensor_tensor(rstd, rstd, scale, ALU.mult).then_inc(own, 1)
                dve.wait_ge(own, TILES + 7)
            nc.vector.scalar_tensor_tensor(nmr, mean, -0.5, rstd, ALU.mult, ALU.mult).then_inc(seen, 1)

        def norm_scalar(act, src, dest, width, func, seen, rooted, applied):
            act.wait_ge(seen, 1)
            nc.scalar.activation(rstd, rstd, ACT.Sqrt).then_inc(rooted, 1)
            act.wait_ge(seen, 2)
            with act.Fori(0, TILES) as t:
                nc.scalar.activation(at(dest, t, 0, width), at(src, t, 0, width), func,
                                     bias=col(nmr, t), scale=col(rstd, t)).then_inc(applied, 1)

        def layer_norm(name, src, dest, width, func, scale=None, store=None):
            own, seen, rooted, applied, stored = (sem(f"{name}_{s}") for s in ("own", "seen", "rooted", "applied", "stored"))
            with nc.Block() as block:
                @block.vector
                def _(dve):
                    norm_vector(dve, src, width, seen, rooted, scale, own)

                @block.scalar
                def _(act):
                    norm_scalar(act, src, dest, width, func, seen, rooted, applied)

                if store is not None:
                    @block.sync
                    def _(sp):
                        table, buf, w = store
                        with sp.Fori(0, TILES) as t:
                            sp.wait_ge(applied, t + 1)
                            sp.dma_start(node_rows(table, t, 0, w), at(buf, t, 0, w)).then_inc(stored, 16)
                        sp.wait_ge(stored, 16 * TILES)

        rec_staged, scatter_go = sem("scatter_staged"), sem("scatter_go")
        sent = [sem("scatter_sent0"), sem("scatter_sent1")]
        rec_built, rec_loaded, unpacked = sem("rec_built"), sem("rec_loaded"), sem("unpacked")
        own, seen, rooted, applied, stored = (sem(f"ln0_{s}") for s in ("own", "seen", "rooted", "applied", "stored"))
        hot, counted_in = sem("hot"), sem("counted_in")
        deg_own, deg_root = sem("deg_own"), sem("deg_root")
        low_deg = small[0:P, 10, :]
        n_groups = COLS // HALF
        with nc.Block() as block:
            @block.gpsimd
            def _(pool):
                def scatter(records, address, rec_flat, before):
                    def step(it):
                        for h in range(2):
                            wait_if(pool, sent[h], it * (16 * HALF) + before * (16 * HALF))
                            g = it * 2 + h
                            nc.gpsimd.tensor_copy(stage[0:P, h, :], col(address, g * HALF, HALF)).then_inc(rec_staged, 1)
                            nc.gpsimd.tensor_copy(stage_rec[0:P, h, :], col(rec_flat, g * (HALF * REC), HALF * REC))\
                                .then_inc(rec_staged, 1)
                            pool.wait_ge(rec_staged, g * 2 + (4 * before + 2))
                            pool.sem_inc(scatter_go, 1)
                            for r in range(HALF):
                                pool.indirect_dma_start(
                                    records, bass.IndirectOffsetOnAxis(ap=stage[0:P, h, r:r + 1], axis=0),
                                    stage_rec[0:P, h, r * REC:(r + 1) * REC], None).then_inc(sent[h], 16)
                    peeled(pool, n_groups // 2, step)
                pool.wait_ge(rec_built, 6)
                scatter(records_s, adr_s, aflat[:, 6000:7600], 0)
                scatter(records_d, adr_d, flat[:, 4000:5600], n_groups // 2)
                for h in range(2):
                    pool.wait_ge(sent[h], 2 * 16 * COLS // 2)

            @block.vector
            def _(dve):
                nc.vector.tensor_copy(rec_in[:, :, 0], src_i).then_inc(rec_built, 1)
                nc.vector.tensor_copy(rec_in[:, :, 2], wgt).then_inc(rec_built, 1)
                nc.vector.tensor_copy(rec_in_s[:, :, 0], dst_i).then_inc(rec_built, 1)
                nc.vector.tensor_copy(rec_in_s[:, :, 2], wgt).then_inc(rec_built, 1)
                nc.vector.memset(rec_in_s[:, :, 3], 0.0).then_inc(rec_built, 1)
                nc.vector.memset(rec_in[:, :, 3], 0.0).then_inc(rec_built, 1)
                norm_vector(dve, x, D, seen, rooted, None, own)

                def hots(c, q):
                    wait_if(dve, counted_in, c - (NPS - 1))
                    nc.vector.tensor_scalar(hot_node[:, q, :], iota_n[0:P, 0:P], at(rec_in, c, 1, 2), None, ALU.is_equal)
                    nc.vector.tensor_scalar(hot_tile[:, q, 0:TILES], iota_n[0:P, 0:TILES], col(hi, c), col(wgt, c),
                                            ALU.is_equal, ALU.mult)
                    nc.vector.tensor_scalar(hot_tile[:, q, TILES:2 * TILES], iota_n[0:P, 0:TILES], col(hi, c), None,
                                            ALU.is_equal).then_inc(hot, 1)

                def four(i):
                    for q in range(NPS):
                        hots(i * NPS + q, q)
                peeled(dve, COLS // NPS, four)

                dve.wait_ge(counted_in, COLS)
                done = 0
                for n, dis in enumerate((dis2, dis1)):
                    nc.vector.tensor_scalar(dis, bank[5][0:P, n * TILES:(n + 1) * TILES], 1.0, None, ALU.add)\
                        .then_inc(deg_own, 1)
                    dve.wait_ge(deg_own, done + 1)
                    nc.vector.tensor_scalar(low_deg, dis, 0.0, None, ALU.is_gt).then_inc(deg_own, 1)
                    nc.vector.tensor_scalar(deg, dis, 1e-30, None, ALU.max).then_inc(deg_own, 1)
                    dve.wait_ge(deg_root, n + 1)
                    nc.vector.reciprocal(deg, deg).then_inc(deg_own, 1)
                    dve.wait_ge(deg_own, done + 4)
                    nc.vector.tensor_tensor(dis, deg, low_deg, ALU.mult).then_inc(deg_own, 1)
                    dve.wait_ge(deg_own, done + 5)
                    done += 5

            @block.tensor
            def _(pe):
                def add_column(c, q, start, stop):
                    pe.wait_ge(hot, c + 1)
                    nc.tensor.matmul(bank[5][0:P, 0:2 * TILES], hot_node[:, q, :], hot_tile[:, q, :],
                                     start=start, stop=stop).then_inc(counted_in, 1)

                def four(i):
                    for q in range(NPS):
                        add_column(i * NPS + q, q, isinstance(i, int) and i * NPS + q == 0,
                                   isinstance(i, int) and i * NPS + q == COLS - 1)
                peeled(pe, COLS // NPS, four)

            @block.scalar
            def _(act):
                norm_scalar(act, x, hbuf, D, ACT.Relu, seen, rooted, applied)
                for n in range(2):
                    act.wait_ge(deg_own, 5 * n + 3)
                    nc.scalar.activation(deg, deg, ACT.Sqrt).then_inc(deg_root, 1)

            @block.sync
            def _(sp):
                with sp.Fori(0, TILES) as t:
                    sp.wait_ge(applied, t + 1)
                    sp.dma_start(node_rows(table0, t, 0, D), at(hbuf, t, 0, D)).then_inc(stored, 16)
                sp.wait_ge(stored, 16 * TILES)

        def unpack(name, records, fields):
            loaded = sem(f"{name}_loaded")
            with nc.Block() as block:
                @block.sync
                def _(sp):
                    sp.dma_start(rec[:, :, :], records.rearrange("(p c) k -> p c k", p=SLOTS)).then_inc(loaded, 16)

                @block.vector
                def _(dve):
                    dve.wait_ge(loaded, 16)
                    for k, field in enumerate(fields):
                        nc.vector.tensor_copy(field, rec[:, :, k])
        unpack("rec_s", records_s, (dst_idx[:, :], src_loc[:, :], ew_s[:, :]))
        unpack("rec_d", records_d, (src_idx[:, :], dst_loc[:, :], ew[:, :]))
        with nc.Block() as block:
            @block.vector
            def _(dve):
                nc.vector.memset(acc[0:P, :, 0:D], 0.0)

        def gathered(width, r, lo=0, hi_=None):
            r = r % GROUP
            return flat[:, r * width + lo:r * width + (width if hi_ is None else hi_)]

        def arrival(it, r, uses):
            return it * 16 + 16 * (uses + 1 + r // GROUP)

        staged, go = sem("gather_staged"), sem("gather_go")

        def gathers(pool, table, width, index, uses, released, before):
            def step(it):
                for h in range(2):
                    wait_if(pool, released, it * GROUP + (before + h * HALF - HALF))
                    nc.gpsimd.tensor_copy(stage[:, h, :], col(index, it * GROUP + h * HALF, HALF, 128))\
                        .then_inc(staged, 1)
                    pool.wait_ge(staged, it * 2 + (2 * uses + h + 1))
                    pool.sem_inc(go, 1)
                    for r in range(h * HALF, (h + 1) * HALF):
                        pool.indirect_dma_start(
                            gathered(width, r), None, table,
                            bass.IndirectOffsetOnAxis(ap=stage[:, h, r - h * HALF:r - h * HALF + 1], axis=0))\
                            .then_inc(arrived[r], 16)
            peeled(pool, STEPS, step)

        built, summed, added = sem("built"), sem("summed"), sem("added")
        sums = [0]

        def build_selector(dve, local, weight, it, r):
            c = it * GROUP + r
            if weight is None:
                return nc.vector.tensor_scalar(sel[:, r % NSEL, :], iota_n[:, 0:P], col(local, c, 1, 128), None,
                                               ALU.is_equal)
            return nc.vector.tensor_scalar(sel[:, r % NSEL, :], iota_n[:, 0:P], col(local, c, 1, 128),
                                           col(weight, c, 1, 128), ALU.is_equal, ALU.mult)

        def tile_of(eng, tile_i, it, r):
            return eng.value_load(col(tile_i, it * (GROUP // 2) + r // 2, 1, 1), min_val=0, max_val=TILES - 1)

        def sum_over_edges(table, width, weight=None, by_source=False):
            index, local, tile_i = (dst_idx, src_loc, src_tile_i) if by_source else (src_idx, dst_loc, dst_tile_i)
            uses, before = passes[0], sums[0]
            passes[0] += STEPS
            sums[0] += CHUNKS
            before2 = before // 2

            with nc.Block() as block:
                @block.gpsimd
                def _(pool):
                    gathers(pool, table, width, index, uses, summed, before)

                @block.tensor
                def _(pe):
                    def step(it, r):
                        q = r // 2 % NPS
                        pe.wait_ge(built, it * GROUP + (before + r + 1))
                        if r % 2 == 0:
                            wait_if(pe, added, it * (GROUP // 2) + (before2 + r // 2 + 1 - NPS))
                        pe.wait_ge(arrived[r], arrival(it, r, uses))
                        nc.tensor.matmul(bank[q][0:P, 0:width], sel[:, r % NSEL, :], gathered(width, r),
                                         start=(r % 2 == 0), stop=(r % 2 == 1)).then_inc(summed, 1)
                    run_steps(pe, 0, 0, step)

                @block.vector
                def _(dve):
                    def build(it, r):
                        wait_if(dve, summed, it * GROUP + (before + r + 1 - NSEL))
                        build_selector(dve, local, weight, it, r).then_inc(built, 1)

                    def add(it, r):
                        pair = it * (GROUP // 2) + (before2 + r // 2)
                        tile = tile_of(dve, tile_i, it, r)
                        dve.wait_ge(summed, it * GROUP + (before + r + 1))
                        wait_if(dve, added, pair)
                        row = at(acc, tile, 0, width)
                        nc.vector.tensor_tensor(row, bank[r // 2 % NPS][0:P, 0:width], row, ALU.add).then_inc(added, 1)

                    def step(it, r):
                        if valid(it, r + 4):
                            build(it, r + 4)
                        if valid(it, r) and r % 2 == 1:
                            add(it, r)
                    run_steps(dve, 4, 0, step)

        xt = flat[:, 0:2 * H].rearrange("p (a b) -> p a b", a=2)
        tile_in = sb("tile_in", [128, 2, H + 2])

        turned, copied, multiplied, finished, ready = (sem(f"tiles_{s}") for s in (
            "turned", "copied", "multiplied", "finished", "ready"))
        projected = [0]

        def project(name, src, kt, w, n, bias, finish, on_scalar, aug=None, scale=None, store=None,
                    narrow=None):
            width = 128 * kt + (1 if aug is not None else 0)
            base = projected[0]
            projected[0] += TILES
            if store is not None:
                stored = sem(f"{name}_stored")
            copy = nc.vector if on_scalar else nc.scalar
            with nc.Block() as block:
                @block.tensor
                def _(pe):
                    def turn(t, q):
                        pe.wait_ge(ready, t + (base + 1))
                        wait_if(pe, copied, t + (base - 1))
                        for k in range(kt):
                            last = nc.tensor.transpose(bank[q][:, k * P:(k + 1) * P], tile_in[0:P, q, 128 * k:128 * (k + 1)],
                                                       ident[0:P, 0:P])
                        if aug is not None:
                            last = nc.tensor.transpose(bank[q][0:2, kt * P:(kt + 1) * P], tile_in[0:P, q, 128 * kt:128 * kt + 2],
                                                       ident[0:P, 0:P])
                        last.then_inc(turned, 1)

                    def multiply(t, q):
                        pe.wait_ge(copied, t + (base + 1))
                        wait_if(pe, finished, t + (base - 1))
                        o = bank[2 + q][0:P, 0:n]
                        for k in range(kt):
                            last = nc.tensor.matmul(o, xt[:, q, k * P:(k + 1) * P], w[:, k, 0:n], start=(k == 0),
                                                    stop=(k == kt - 1 and bias is None and aug is None))
                        if bias is not None:
                            last = nc.tensor.matmul(o, ones[0:1, 0:P], bias[0:1, 0:n], start=False, stop=True)
                        if aug is not None:
                            last = nc.tensor.matmul(o, xt[0:2, q, kt * P:(kt + 1) * P], aug[0:2, 0:n],
                                                    start=False, stop=True)
                        if narrow is not None:
                            for k in range(kt):
                                last = nc.tensor.matmul(bank[4 + q][0:P, 0:2], xt[:, q, k * P:(k + 1) * P],
                                                        narrow[0][:, k, :], start=(k == 0), stop=(k == kt - 1))
                        last.then_inc(multiplied, 1)

                    turn(0, 0)
                    turn(1, 1)
                    multiply(0, 0)
                    with pe.Fori(1, TILES // 2) as i:
                        turn(i * 2, 0)
                        multiply(i * 2 - 1, 1)
                        turn(i * 2 + 1, 1)
                        multiply(i * 2, 0)
                    turn(TILES - 1, 0)
                    multiply(TILES - 2, 1)
                    multiply(TILES - 1, 0)

                def copy_tile(eng, t, q):
                    eng.wait_ge(turned, t + (base + 1))
                    wait_if(eng, multiplied, t + (base - 1))
                    parts = ([(128, 0, kt * P)] if kt else []) + ([(2, kt * P, (kt + 1) * P)] if aug is not None else [])
                    for n_part, lo, hi_ in parts:
                        if on_scalar:
                            last = nc.vector.tensor_copy(xt[0:n_part, q, lo:hi_], bank[q][0:n_part, lo:hi_])
                        else:
                            last = nc.scalar.activation(xt[0:n_part, q, lo:hi_], bank[q][0:n_part, lo:hi_], ACT.Copy)
                    last.then_inc(copied, 1)

                def finish_tile(eng, t, q):
                    eng.wait_ge(multiplied, t + (base + 1))
                    if narrow is not None:
                        narrow[1](t, bank[4 + q][0:P, 0:2])
                    finish(t, bank[2 + q][0:P, 0:n]).then_inc(finished, 1)

                def scale_tile(dve, t, q):
                    wait_if(dve, turned, t + (base - 1))
                    nc.vector.tensor_scalar(tile_in[0:P, q, 0:width], at(src, t, 0, width), col(scale, t), None,
                                            ALU.mult).then_inc(ready, 1)

                @block.vector
                def _(dve):
                    handle = copy_tile if on_scalar else finish_tile
                    if scale is None:
                        over_tiles(dve, lambda t, q: handle(dve, t, q))
                        return

                    def pair(i):
                        for q in range(2):
                            handle(dve, i * 2 + q, q)
                            scale_tile(dve, i * 2 + (q + 2), q)
                    scale_tile(dve, 0, 0)
                    scale_tile(dve, 1, 1)
                    pair(0)
                    with dve.Fori(1, TILES // 2 - 1) as i:
                        pair(i)
                    handle(dve, TILES - 3, 0)
                    scale_tile(dve, TILES - 1, 0)
                    handle(dve, TILES - 2, 1)
                    handle(dve, TILES - 1, 0)

                if scale is None:
                    @block.gpsimd
                    def _(pool):
                        def copy_in(t, q):
                            wait_if(pool, turned, t + (base - 1))
                            nc.gpsimd.tensor_copy(tile_in[0:P, q, 0:width], at(src, t, 0, width)).then_inc(ready, 1)
                        over_tiles(pool, copy_in)

                @block.scalar
                def _(act):
                    over_tiles(act, lambda t, q: (finish_tile if on_scalar else copy_tile)(act, t, q))

                if store is not None:
                    @block.sync
                    def _(sp):
                        with sp.Fori(0, TILES) as t:
                            sp.wait_ge(finished, t + (base + 1))
                            table, buf, w_ = store
                            dest = node_rows(table, t, 0, w_)
                            sp.dma_start(dest, at(buf, t, 0, w_)).then_inc(stored, 16)
                        sp.wait_ge(stored, 16 * TILES)

        def add_to_x(t, o):
            return nc.vector.tensor_tensor(at(x, t, 0, D), o, at(x, t, 0, D), ALU.add)

        sum_over_edges(table0, D, weight=ew_s, by_source=True)
        project("l0p", acc, 2, w0, D, b0_r, add_to_x, on_scalar=False)

        layer_norm("ln1", x, hbuf, D, ACT.Relu)
        project("l1s", hbuf, 2, wsk, D, bs_r, add_to_x, on_scalar=False)
        with nc.Block() as block:
            @block.vector
            def _(dve):
                nc.vector.tensor_copy(acc[0:P, :, D], dis1)
                nc.vector.memset(tile_in[:, :, D + 1:D + 2], 1.0)
        layer_norm("ln1b", hbuf, acc, D, ACT.Identity, scale=dis1, store=(table1, acc, D + 1))
        sum_over_edges(table1, D + 1)
        project("l1p", acc, 2, w11, H, None,
                lambda t, o: nc.scalar.activation(at(acc, t, 0, H), o, ACT.Gelu), on_scalar=True,
                aug=b11_r, scale=dis1)

        def last_touch(name, table, width, touch):
            touched, stored = sem(f"{name}_touched"), sem(f"{name}_stored")
            with nc.Block() as block:
                @block.vector
                def _(dve):
                    with dve.Fori(0, TILES) as t:
                        touch(t).then_inc(touched, 1)

                @block.sync
                def _(sp):
                    with sp.Fori(0, TILES) as t:
                        sp.wait_ge(touched, t + 1)
                        sp.dma_start(node_rows(table, t, 0, width), at(acc, t, 0, width)).then_inc(stored, 16)
                    sp.wait_ge(stored, 16 * TILES)

        last_touch("t2", table2, H, lambda t: nc.vector.tensor_scalar(
            at(acc, t, 0, H), at(acc, t, 0, H), col(dis1, t), None, ALU.mult))
        sum_over_edges(table2, H)
        project("l1q", acc, 4, w2, H, b2_r,
                lambda t, o: nc.scalar.activation(at(acc, t, 0, H), o, ACT.Gelu), on_scalar=True,
                scale=dis1)
        layer_norm("ln2", acc, acc, H, ACT.Identity)
        project("l1o", acc, 4, wm2, D, bm2_r, add_to_x, on_scalar=False)

        layer_norm("ln3", x, acc, D, ACT.Relu, scale=dis2, store=(table3, acc, D))
        sum_over_edges(table3, D, weight=ew)
        project("l2p", acc, 2, l2w1, D, l2b1_r,
                lambda t, o: nc.scalar.activation(at(acc, t, 0, D), o, ACT.Copy, scale=col(dis2, t)),
                on_scalar=True, scale=dis2)
        last_touch("t4", table4, D, lambda t: nc.vector.scalar_tensor_tensor(
            at(acc, t, 0, D), at(acc, t, 0, D), 0.01, at(acc, t, 0, D), ALU.mult, ALU.max))
        sum_over_edges(table4, D, weight=ew)
        project("l2q", acc, 2, l2w2, D, l2b2_r, add_to_x, on_scalar=False, scale=dis2)

        layer_norm("ln4", x, hbuf, D, ACT.Relu)

        def keep_projections(t, o):
            nc.scalar.activation(at(acc, t, 0, D), o[:, 0:D], ACT.Copy)
            return nc.scalar.activation(at(hbuf, t, 0, D), o[:, D:2 * D], ACT.Copy)

        def keep_narrow(t, o):
            nc.scalar.activation(at(acc, t, D, D + 1), o[:, 0:1], ACT.Copy)
            nc.scalar.activation(at(hbuf, t, D, D + 1), o[:, 1:2], ACT.Copy)
        project("l3p", hbuf, 2, wst, 2 * D, None, keep_projections, on_scalar=True,
                narrow=(wlin, keep_narrow), store=(table_pt, hbuf, D + 1))

        turned_sel = [acc[0:P, q, D + 1:D + 1 + SLOTS] for q in range(NPS)]
        a_built, a_turned, a_copied, expanded, zed, relued, scored = (sem(f"att_{s}") for s in (
            "built", "turned", "copied", "expanded", "zed", "relued", "scored"))

        def turn(pe, it, r, before):
            q = r % 2
            pe.wait_ge(a_built, it * GROUP + (before + r + 1))
            wait_if(pe, a_copied, it * GROUP + (before + r - 1))
            nc.tensor.transpose(bank[4 + q][0:P, 0:SLOTS], sel[:, r % NSEL, :], ident[:, :])\
                .then_inc(a_turned, 1)

        def copy_turned(act, it, r, before):
            act.wait_ge(a_turned, it * GROUP + (before + r + 1))
            wait_if(act, expanded, it * GROUP + (before + r + 1 - NPS))
            q = r % 2
            nc.scalar.activation(turned_sel[r % NPS], bank[4 + q][0:P, 0:SLOTS], ACT.Copy)\
                .then_inc(a_copied, 1)

        def expand(pe, own_rows, tile, it, r, before, nbank):
            pe.wait_ge(a_copied, it * GROUP + (before + r + 1))
            wait_if(pe, zed, it * GROUP + (before + r + 1 - nbank))
            nc.tensor.matmul(bank[r % nbank][:, 0:D + 1], turned_sel[r % NPS], at(own_rows, tile, 0, D + 1),
                             start=True, stop=True).then_inc(expanded, 1)

        def add_rows(dve, width, it, r, uses, before, nbank):
            dve.wait_ge(expanded, it * GROUP + (before + r + 1))
            dve.wait_ge(arrived[r % GROUP], arrival(it, r, uses))
            z = gathered(width, r, 0, D + 1)
            nc.vector.tensor_tensor(z, bank[r % nbank][:, 0:D + 1], z, ALU.add).then_inc(zed, 1)

        def take_relu(act, width, it, r, before):
            act.wait_ge(zed, it * GROUP + (before + r + 1))
            z = gathered(width, r, 0, D)
            nc.scalar.activation(z, z, ACT.Relu).then_inc(relued, 1)

        def take_score(dve, width, it, r, before):
            dve.wait_ge(relued, it * GROUP + (before + r + 1))
            z = gathered(width, r, 0, D + 1)
            c = r % GROUP
            nc.vector.tensor_tensor_reduce(out=z, in0=z, in1=wa_b[:, :], scale=1.0, scalar=0.0, op0=ALU.mult,
                                           op1=ALU.add, accum_out=escore[:, c:c + 1]).then_inc(scored, 1)

        WPT = D + 1
        QUAD = 4
        o = GROUP * WPT
        grid = [acc[:, 4 + q, D + 1:D + 1 + P] for q in range(NPS)]
        neg_loc = flat[:, o:o + CHUNKS]
        cmax = flat[0:P, o + CHUNKS:o + 2 * CHUNKS]
        csum = flat[0:P, o + 2 * CHUNKS:o + 3 * CHUNKS]
        cneg = flat[0:P, o + 3 * CHUNKS:o + 4 * CHUNKS]
        squared, gridded, g_turned, maxed, negged, g_summed, flipped = (sem(f"grid_{s}") for s in (
            "squared", "gridded", "turned", "maxed", "negged", "summed", "flipped"))
        uses1 = passes[0]
        passes[0] += STEPS
        with nc.Block() as block:
            @block.gpsimd
            def _(pool):
                gathers(pool, table_pt, WPT, dst_idx, uses1, scored, 0)

            @block.tensor
            def _(pe):
                tile = [None]

                def turn_grid(it, r):
                    q, k = r // QUAD % 2, r % QUAD
                    pe.wait_ge(gridded, it * GROUP + (r + 1))
                    if k == 0:
                        wait_if(pe, g_summed, it * GROUP + (r - QUAD))
                    nc.tensor.transpose(bank[6 + q][0:P, k * SLOTS:(k + 1) * SLOTS], grid[r % NPS], ident[:, :])\
                        .then_inc(g_turned, 1)

                def step(it, r):
                    if valid(it, r + 2):
                        turn(pe, it, r + 2, 0)
                    if valid(it, r):
                        if r % 2 == 0:
                            tile[0] = tile_of(pe, src_tile_i, it, r)
                        expand(pe, acc, tile[0], it, r, 0, NPS)
                    if valid(it, r - 4):
                        turn_grid(it, r - 4)
                run_steps(pe, 2, 4, step)

            @block.scalar
            def _(act):
                def make_grid(it, r):
                    wait_if(act, g_turned, it * GROUP + (r + 1 - NPS))
                    nc.scalar.activation(grid[r % NPS], iota_n[:, 0:P], ACT.Square,
                                         bias=col(neg_loc, it * GROUP + r, 1, 128)).then_inc(squared, 1)
                    act.wait_ge(scored, it * GROUP + (r + 1))
                    act.wait_ge(squared, it * GROUP + (r + 1))
                    nc.scalar.activation(grid[r % NPS], grid[r % NPS], ACT.Identity, scale=LOW,
                                         bias=escore[:, r % GROUP:r % GROUP + 1]).then_inc(gridded, 1)

                def exps(it, r):
                    act.wait_ge(negged, it * (GROUP // QUAD) + (r // QUAD + 1))
                    for k in range(QUAD):
                        g = bank[6 + r // QUAD % 2][0:P, k * SLOTS:(k + 1) * SLOTS]
                        c = it * GROUP + (r - (QUAD - 1) + k)
                        nc.scalar.activation(g, g, ACT.Exp, bias=col(cneg, c), scale=1.0, accum_out=col(csum, c))\
                            .then_inc(g_summed, 1)

                act.wait_ge(flipped, 1)

                def step(it, r):
                    if valid(it, r + 2):
                        copy_turned(act, it, r + 2, 0)
                    if valid(it, r):
                        take_relu(act, WPT, it, r, 0)
                    if valid(it, r - 2):
                        make_grid(it, r - 2)
                    if valid(it, r - 6) and (r - 6) % QUAD == QUAD - 1:
                        exps(it, r - 6)
                run_steps(act, 2, 7, step)

            @block.vector
            def _(dve):
                nc.vector.tensor_scalar(neg_loc, src_loc[:, :], -1.0, None, ALU.mult).then_inc(flipped, 1)

                def build(it, r):
                    wait_if(dve, a_turned, it * GROUP + (r + 1 - NSEL))
                    build_selector(dve, src_loc, None, it, r).then_inc(a_built, 1)

                def score(it, r):
                    wait_if(dve, gridded, it * GROUP + (r + 1 - GROUP))
                    take_score(dve, WPT, it, r, 0)

                def largest(it, r):
                    dve.wait_ge(g_turned, it * GROUP + (r + 1))
                    c = it * GROUP + (r - (QUAD - 1))
                    nc.vector.tensor_reduce(
                        col(cmax, c, QUAD), bank[6 + r // QUAD % 2][0:P, :].rearrange("p (a b) -> p a b", a=QUAD),
                        AX.X, ALU.max).then_inc(maxed, 1)
                    dve.wait_ge(maxed, it * (GROUP // QUAD) + (r // QUAD + 1))
                    nc.vector.tensor_scalar(col(cneg, c, QUAD), col(cmax, c, QUAD), -1.0, None, ALU.mult)\
                        .then_inc(negged, 1)

                def step(it, r):
                    if valid(it, r + 4):
                        build(it, r + 4)
                    if valid(it, r):
                        add_rows(dve, WPT, it, r, uses1, 0, NPS)
                    if valid(it, r - 1):
                        score(it, r - 1)
                    if valid(it, r - 5) and (r - 5) % QUAD == QUAD - 1:
                        largest(it, r - 5)
                run_steps(dve, 4, 6, step)

        pmax, psum_, pm, member, work = (flat[0:P, k * PAIRS:(k + 1) * PAIRS] for k in range(5))
        first = cmax.rearrange("p (a b) -> p a b", b=2)[:, :, 0]
        second = cmax.rearrange("p (a b) -> p a b", b=2)[:, :, 1]
        cexp = flat[0:P, 6 * PAIRS:8 * PAIRS]
        step_, exp_ready, exp_done = sem("comb_step"), sem("comb_exp_ready"), sem("comb_exp_done")
        total = small[0:P, 5, :]
        with nc.Block() as block:
            @block.vector
            def _(dve):
                done = [0]

                def link(ins):
                    done[0] += 1
                    ins.then_inc(step_, 1)
                    dve.wait_ge(step_, done[0])

                link(nc.vector.tensor_tensor(pmax, first, second, ALU.max))
                with dve.Fori(0, TILES) as t:
                    nc.vector.tensor_scalar(work, src_tile[0:P, :], col(iota_n, t), LOW, ALU.not_equal, ALU.mult)\
                        .then_inc(step_, 1)
                    dve.wait_ge(step_, t * 3 + (done[0] + 1))
                    nc.vector.tensor_tensor(work, work, pmax, ALU.add).then_inc(step_, 1)
                    dve.wait_ge(step_, t * 3 + (done[0] + 2))
                    nc.vector.tensor_reduce(col(top, t), work, AX.X, ALU.max).then_inc(step_, 1)
                    dve.wait_ge(step_, t * 3 + (done[0] + 3))
                done[0] += 3 * TILES
                link(nc.vector.memset(pm, 0.0))
                with dve.Fori(0, TILES) as t:
                    nc.vector.tensor_scalar(work, src_tile[0:P, :], col(iota_n, t), col(top, t), ALU.is_equal, ALU.mult)\
                        .then_inc(step_, 1)
                    dve.wait_ge(step_, t * 2 + (done[0] + 1))
                    nc.vector.tensor_tensor(pm, pm, work, ALU.add).then_inc(step_, 1)
                    dve.wait_ge(step_, t * 2 + (done[0] + 2))
                done[0] += 2 * TILES
                ce = cexp.rearrange("p (a b) -> p a b", b=2)
                link(nc.vector.tensor_tensor(ce[:, :, 0], first, pm, ALU.subtract))
                nc.vector.tensor_tensor(ce[:, :, 1], second, pm, ALU.subtract).then_inc(exp_ready, 1)
                dve.wait_ge(exp_done, 1)
                link(nc.vector.tensor_tensor(cexp, cexp, csum, ALU.mult))
                link(nc.vector.tensor_tensor(psum_, ce[:, :, 0], ce[:, :, 1], ALU.add))
                with dve.Fori(0, TILES) as t:
                    nc.vector.tensor_scalar(member, src_tile[0:P, :], col(iota_n, t), None, ALU.is_equal)\
                        .then_inc(step_, 1)
                    dve.wait_ge(step_, t * 3 + (done[0] + 1))
                    nc.vector.tensor_tensor(work, member, psum_, ALU.mult).then_inc(step_, 1)
                    dve.wait_ge(step_, t * 3 + (done[0] + 2))
                    nc.vector.tensor_reduce(col(total, t), work, AX.X, ALU.add).then_inc(step_, 1)
                    dve.wait_ge(step_, t * 3 + (done[0] + 3))
                done[0] += 3 * TILES
                link(nc.vector.tensor_scalar(total, total, 1e-30, None, ALU.max))
                link(nc.vector.reciprocal(total, total))
                nc.vector.tensor_tensor(rstd, rstd, total, ALU.mult)
                nc.vector.tensor_tensor(nmr, nmr, total, ALU.mult)

            @block.scalar
            def _(act):
                act.wait_ge(exp_ready, 1)
                nc.scalar.activation(cexp, cexp, ACT.Exp).then_inc(exp_done, 1)

        top_copied, ps_stored, h_made, h_stored = (sem(f"source_{s}") for s in (
            "top_copied", "ps_stored", "h_made", "h_stored"))
        with nc.Block() as block:
            @block.vector
            def _(dve):
                nc.vector.tensor_copy(acc[0:P, :, D + 1], top[0:P, :]).then_inc(top_copied, 1)
                dve.wait_ge(ps_stored, 16)
                nc.vector.memset(acc[0:P, :, 0:D], 0.0)

            @block.sync
            def _(sp):
                sp.wait_ge(top_copied, 1)
                sp.dma_start(table_src.rearrange("(t p) f -> p t f", p=P)[:, :, 0:D + 2], acc[0:P, :, 0:D + 2])                    .then_inc(ps_stored, 16)
                sp.wait_ge(ps_stored, 16)
                with sp.Fori(0, TILES) as t:
                    sp.wait_ge(h_made, t + 1)
                    sp.dma_start(node_rows(table_src, t, D + 2, 2 * D + 2), at(acc, t, D, 2 * D)).then_inc(h_stored, 16)
                sp.wait_ge(h_stored, 16 * TILES)

            @block.scalar
            def _(act):
                act.wait_ge(ps_stored, 16)
                with act.Fori(0, TILES) as t:
                    nc.scalar.activation(at(acc, t, D, 2 * D), at(x, t, 0, D), ACT.Relu, bias=col(nmr, t),
                                         scale=col(rstd, t)).then_inc(h_made, 1)

        WSRC = 2 * D + 2
        drop, lowered, exped, weighed = (sem(f"weigh_{s}") for s in ("drop", "lowered", "exped", "weighed"))
        gap = [cols[:, q:q + 1] for q in range(8)]
        uses2, before = passes[0], sums[0]
        passes[0] += STEPS
        before2 = before // 2
        with nc.Block() as block:
            @block.gpsimd
            def _(pool):
                gathers(pool, table_src, WSRC, src_idx, uses2, summed, before)

            @block.tensor
            def _(pe):
                tile = [None]

                def multiply(it, r):
                    q = r // 2 % 2
                    pe.wait_ge(weighed, it * GROUP + (r + 1))
                    if r % 2 == 0:
                        wait_if(pe, added, it * (GROUP // 2) + (before2 + r // 2 - 1))
                    nc.tensor.matmul(bank[6 + q][0:P, 0:D], sel[:, r % NSEL, :], gathered(WSRC, r, D + 2, 2 * D + 2),
                                     start=(r % 2 == 0), stop=(r % 2 == 1)).then_inc(summed, 1)

                def step(it, r):
                    if valid(it, r + 1):
                        turn(pe, it, r + 1, CHUNKS)
                    if valid(it, r):
                        if r % 2 == 0:
                            tile[0] = tile_of(pe, dst_tile_i, it, r)
                        expand(pe, hbuf, tile[0], it, r, CHUNKS, NPS)
                    if valid(it, r - 3):
                        multiply(it, r - 3)
                run_steps(pe, 1, 3, step)

            @block.scalar
            def _(act):
                def weigh(it, r):
                    g = gap[r % 8]
                    act.wait_ge(lowered, it * GROUP + (r + 1))
                    nc.scalar.activation(g, g, ACT.Exp).then_inc(exped, 1)
                    act.wait_ge(exped, it * GROUP + (r + 1))
                    h = gathered(WSRC, r, D + 2, 2 * D + 2)
                    nc.scalar.activation(h, h, ACT.Copy, scale=g).then_inc(weighed, 1)

                def step(it, r):
                    if valid(it, r + 1):
                        copy_turned(act, it, r + 1, CHUNKS)
                    if valid(it, r):
                        take_relu(act, WSRC, it, r, CHUNKS)
                    if valid(it, r - 2):
                        weigh(it, r - 2)
                run_steps(act, 1, 2, step)

            @block.vector
            def _(dve):
                def build(it, r):
                    wait_if(dve, summed, it * GROUP + (before + r + 1 - NSEL))
                    build_selector(dve, dst_loc, None, it, r).then_inc(a_built, 1)

                def score(it, r):
                    take_score(dve, WSRC, it, r, CHUNKS)
                    dve.wait_ge(scored, it * GROUP + (CHUNKS + r + 1))
                    wait_if(dve, weighed, it * GROUP + (r + 1 - 8))
                    c = r % GROUP
                    nc.vector.tensor_scalar(gap[r % 8], escore[:, c:c + 1], gathered(WSRC, r, D + 1, D + 2), 0.0,
                                            ALU.subtract, ALU.min).then_inc(lowered, 1)

                def add(it, r):
                    tile = tile_of(dve, dst_tile_i, it, r)
                    dve.wait_ge(summed, it * GROUP + (before + r + 1))
                    wait_if(dve, added, it * (GROUP // 2) + (before2 + r // 2))
                    row = at(acc, tile, 0, D)
                    nc.vector.tensor_tensor(row, bank[6 + r // 2 % 2][0:P, 0:D], row, ALU.add).then_inc(added, 1)

                def step(it, r):
                    if valid(it, r + 2):
                        build(it, r + 2)
                    if valid(it, r):
                        add_rows(dve, WSRC, it, r, uses2, CHUNKS, NPS)
                    if valid(it, r - 1):
                        score(it, r - 1)
                    if valid(it, r - 4) and r % 2 == 1:
                        add(it, r - 4)
                run_steps(dve, 2, 5, step)

        project("l3q", acc, 2, wfc, D, bfc_r, add_to_x, on_scalar=False, store=(out, x, D))


_INS = ["x", "src", "dst", "edge_weight", "L0_gnn_weight", "L0_gnn_bias", "L1_gnn_gamma1", "L1_gnn_beta1",
        "L1_gnn_gamma2", "L1_gnn_beta2", "L1_gnn_Wm1", "L1_gnn_bm1", "L1_gnn_W1", "L1_gnn_b1", "L1_gnn_W2",
        "L1_gnn_b2", "L1_gnn_Wm2", "L1_gnn_bm2", "L1_gnn_Ws", "L1_gnn_bs", "L2_gnn_W1", "L2_gnn_b1",
        "L2_gnn_W2", "L2_gnn_b2", "L3_gnn_W_s", "L3_gnn_W_t", "L3_gnn_W_attn", "L3_gnn_W_fc", "L3_gnn_b_fc"]


def kernel(**inputs):
    import numpy as _np
    import concourse.bacc as _bacc
    from concourse import mybir as _mybir
    from concourse.bass_utils import run_bass_kernel_spmd as _run

    nc = _bacc.Bacc("TRN2", target_bir_lowering=False, num_devices=1)
    arrays, args = {}, []
    for name in _INS:
        a = _np.ascontiguousarray(inputs[name])
        arrays[f"in_{name}"] = a
        args.append(nc.dram_tensor(f"in_{name}", a.shape, _mybir.dt.from_np(a.dtype), kind="ExternalInput").ap())
    args.append(nc.dram_tensor("out_x", (NODES, D), _mybir.dt.float32, kind="ExternalOutput").ap())
    gnn(nc, *args)
    r = _run(nc, [arrays], core_ids=[0])
    return r.results[0]["out_x"]
```

```python
import concourse.bass as bass
from concourse import mybir
from contextlib import ExitStack

F32 = mybir.dt.float32
I32 = mybir.dt.int32
ALU = mybir.AluOpType
ACT = mybir.ActivationFunctionType
AX = mybir.AxisListType

NODES = 3125
EDGES = 50000
D = 256
H = 512
P = 125
TILES = NODES // P
COLS = EDGES // P
SLOTS = 128
GROUP = 16
HALF = GROUP // 2
PAIR = 2 * SLOTS
CHUNKS = 2 * (EDGES // PAIR + TILES)
PAIRS = CHUNKS // 2
STEPS = -(-CHUNKS // GROUP)
NPS = 4
NSEL = 8
REC = 4
EPS = 1e-5
ROUND = 12582912.0
LOW = -float(2 ** 100)


def wait_if(eng, sem, value):
    if not isinstance(value, int) or value > 0:
        eng.wait_ge(sem, value)


def peeled(eng, n, body):
    body(0)
    with eng.Fori(1, n - 1) as i:
        body(i)
    body(n - 1)


def valid(it, r):
    return not isinstance(it, int) or 0 <= it * GROUP + r < CHUNKS


def run_steps(eng, ahead, behind, step, aside=None):
    for r in range(GROUP - ahead, GROUP):
        step(-1, r)
    for r in range(GROUP):
        if aside is not None:
            aside(0, r)
        step(0, r)
    if aside is not None:
        with eng.Fori(1, TILES) as it:
            for r in range(GROUP):
                aside(it, r)
                step(it, r)
    with eng.Fori(1 if aside is None else TILES, STEPS - 1) as it:
        for r in range(GROUP):
            step(it, r)
    for r in range(GROUP):
        step(STEPS - 1, r)
    for r in range(behind):
        step(STEPS, r)


def over_tiles(eng, body):
    body(0, 0)
    body(1, 1)
    with eng.Fori(1, TILES // 2) as i:
        body(i * 2, 0)
        body(i * 2 + 1, 1)
    body(TILES - 1, 0)


def at(buf, i, lo, hi, parts=P):
    if isinstance(i, int):
        return buf[0:parts, i, lo:hi]
    return buf[0:parts, bass.ds(i, 1), lo:hi].rearrange("p a f -> p (a f)")


def col(buf, i, n=1, parts=P):
    if isinstance(i, int):
        return buf[0:parts, i:i + n]
    return buf[0:parts, bass.ds(i, n)]


def gnn(nc, x_in, src_in, dst_in, ew_in, L0_W, L0_b, g1, be1, g2, be2, Wm1, bm1, W1, b1, W2, b2, Wm2, bm2,
        Ws, bs, L2_W1, L2_b1, L2_W2, L2_b2, L3_Ws, L3_Wt, L3_wa, L3_Wfc, L3_bfc, out):
    ctx = ExitStack()
    with ctx:
        def sb(name, shape, dt=F32):
            return ctx.enter_context(nc.sbuf_tensor(name, shape, dt))

        def sem(name):
            return ctx.enter_context(nc.semaphore(name))

        def dram(name, shape):
            return nc.dram_tensor(name, shape, F32, kind="Internal").ap()

        bank = [ctx.enter_context(nc.psum_tensor(f"bank{i}", [128, 512], F32)) for i in range(8)]

        table0 = dram("table0", (NODES, D))
        table1 = dram("table1", (NODES, D + 1))
        table2 = dram("table2", (NODES, H))
        table3 = dram("table3", (NODES, D))
        table4 = dram("table4", (NODES, D))
        table_pt = dram("table_pt", (NODES, D + 2))
        table_src = dram("table_src", (NODES, 2 * D + 3))
        records_d = dram("records_d", (SLOTS * CHUNKS, REC))
        records_s = dram("records_s", (SLOTS * CHUNKS, REC))

        x = sb("x", [128, TILES, D])
        acc = sb("acc", [128, TILES, H])
        hbuf = sb("hbuf", [128, TILES, D + 2])
        flat = sb("G", [128, GROUP * (2 * D + 3)])[:, :]
        hflat = hbuf[:, :, :].rearrange("p a b -> p (a b)")
        aflat = acc[:, :, :].rearrange("p a b -> p (a b)")
        sel = sb("sel", [128, NSEL, P])
        rec_s = aflat[:, 0:CHUNKS * REC].rearrange("p (c k) -> p c k", k=REC)
        rec_d = hflat[:, 0:CHUNKS * REC].rearrange("p (c k) -> p c k", k=REC)
        src_idx = sb("src_idx", [128, CHUNKS], I32)
        dst_loc = sb("dst_loc", [128, CHUNKS])
        ew = sb("ew", [128, CHUNKS])
        dst_idx = sb("dst_idx", [128, CHUNKS], I32)
        src_loc = sb("src_loc", [128, CHUNKS])
        ew_s = sb("ew_s", [128, CHUNKS])
        dst_tile = flat[:, 7792:7792 + PAIRS]
        dst_tile_i = sb("dst_tile_i", [1, PAIRS], I32)
        src_tile_i = sb("src_tile_i", [1, PAIRS], I32)
        src_tile = sb("src_tile", [128, PAIRS])
        stage = sb("stage", [128, 2, HALF], I32)
        stage_rec = sb("stage_rec", [128, 2, HALF * REC])
        iota_n = sb("iota_n", [128, CHUNKS])
        ident = sb("ident", [128, 128])
        ones = sb("ones", [128, 128])
        upper = sb("upper", [128, 128])
        stats = sb("stats", [128, TILES, 6])
        cell = sb("cell", [128, GROUP])
        small = sb("small", [128, 12, TILES])
        rstd, nmr, dis1, dis2, deg, mean = (small[0:P, k, :] for k in (0, 1, 2, 3, 4, 11))
        top = sb("top", [128, TILES])
        escore = sb("escore", [128, GROUP])
        w0 = sb("w0", [128, 2, D])
        wsk = sb("wsk", [128, 2, D])
        w11 = sb("w11", [128, 2, H])
        w2 = sb("w2", [128, 4, H])
        wm2 = sb("wm2", [128, 4, D])
        l2w1 = sb("l2w1", [128, 2, D])
        l2w2 = sb("l2w2", [128, 2, D])
        wst = sb("wst", [128, 2, 2 * D])
        wfc = sb("wfc", [128, 2, D])
        wa_b = sb("wa_b", [128, D + 2])
        wlin = sb("wlin", [128, 2, 4])
        b0_r = sb("b0_r", [1, D])
        bs_r = sb("bs_r", [1, D])
        b11_r = sb("b11_r", [2, H])
        b2_r = sb("b2_r", [1, H])
        bm2_r = sb("bm2_r", [1, D])
        l2b1_r = sb("l2b1_r", [1, D])
        l2b2_r = sb("l2b2_r", [1, D])
        bfc_r = sb("bfc_r", [1, D])
        cols = sb("cols", [128, 24])

        arrived = [sem(f"arrived{r}") for r in range(GROUP)]
        passes = [0]

        def node_rows(table, t, lo, hi):
            if isinstance(t, int):
                return table[t * P:(t + 1) * P, lo:hi]
            return table[bass.ds(t * P, P), lo:hi]

        wm1_raw = aflat[:, 0:1024].rearrange("p (k n) -> p k n", k=2)
        w1_raw = aflat[:, 1024:3072].rearrange("p (k n) -> p k n", k=4)
        wm1_t = aflat[:, 3072:4096].rearrange("p (k n) -> p k n", k=4)
        w3_raw = aflat[:, 4096:5632].rearrange("p (m k n) -> p m k n", m=3, k=2)
        g1_c, be1_c, g2_c, be2_c, bm1_c = cols[:, 0:2], cols[:, 2:4], cols[:, 4:8], cols[:, 8:12], cols[:, 12:16]
        wa_c = cols[:, 20:22]
        dst_i = flat[0:P, 0:400].bitcast(I32)
        src_i = flat[0:P, 400:800].bitcast(I32)
        wgt = flat[0:P, 800:1200]
        node_f = flat[0:P, 1200:1600]
        hi = flat[0:P, 1600:2000]
        tmp = flat[0:P, 2000:2400]
        mask = flat[0:P, 2400:2800]
        rank = flat[0:P, 2800:3200]
        slot = flat[0:P, 3200:3600]
        rec_in_s = aflat[0:P, 6000:7600].rearrange("p (c k) -> p c k", k=REC)
        adr_s = aflat[0:P, 7600:8000].bitcast(I32)
        hot_node = aflat[0:P, 8000:8000 + NPS * P].rearrange("p (a b) -> p a b", a=NPS)
        hot_tile = aflat[0:P, 8600:8600 + NPS * 2 * TILES].rearrange("p (a b) -> p a b", a=NPS)
        adr_d = flat[0:P, 3600:4000].bitcast(I32)
        rec_in = flat[0:P, 4000:5600].rearrange("p (c k) -> p c k", k=REC)
        ones_e = flat[0:P, 5600:6000]
        five_masks = aflat[0:P, 9100:9100 + 5 * COLS].rearrange("p (a b) -> p a b", a=5)
        rec_pad = flat[:, 6000:6000 + CHUNKS * REC].rearrange("p (c k) -> p c k", k=REC)
        count = small[0:P, 5, :]
        start = small[0:P, 6, :]
        bucket_c = small[0:TILES, 7, 0:1]
        first_c = small[0:TILES, 8, 0:1]
        diag = small[0:TILES, 9, 0:TILES]
        atleast = aflat[0:TILES, 8800:8800 + PAIRS]

        loaded_x, loaded_e, loaded_w = sem("loaded_x"), sem("loaded_e"), sem("loaded_w")
        const_ready, pad_ready, pad_stored = sem("const_ready"), sem("pad_ready"), sem("pad_stored")
        setup_tr, setup_tc, setup_mm, setup_w = sem("setup_tr"), sem("setup_tc"), sem("setup_mm"), sem("setup_w")

        weights = [(w0, L0_W, 2), (wsk, Ws, 2), (w2, W2, 4), (wm2, Wm2, 4), (l2w1, L2_W1, 2), (l2w2, L2_W2, 2),
                   (wm1_raw, Wm1, 2), (w1_raw, W1, 4), (w3_raw[:, 0, :, :], L3_Ws, 2), (w3_raw[:, 1, :, :], L3_Wt, 2),
                   (w3_raw[:, 2, :, :], L3_Wfc, 2)]
        rows = [(b0_r[0:1, :], L0_b), (bs_r[0:1, :], bs), (b11_r[1:2, :], b1), (b2_r[0:1, :], b2), (bm2_r[0:1, :], bm2),
                (l2b1_r[0:1, :], L2_b1), (l2b2_r[0:1, :], L2_b2), (bfc_r[0:1, :], L3_bfc)]
        columns = [(g1_c, g1), (be1_c, be1), (g2_c, g2), (be2_c, be2), (bm1_c, bm1), (wa_c, L3_wa.rearrange("a n -> (a n)"))]
        n_loads = len(weights) + len(rows) + len(columns) + 1

        bm_c = cols[:, 16:20]
        blocks = [(wm1_raw[:, i, 128 * j:128 * (j + 1)], wm1_t[:, j, 128 * i:128 * (i + 1)])
                  for j in range(4) for i in range(2)]
        for m, (dest, off) in enumerate(((wst, 0), (wst, D), (wfc, 0))):
            blocks += [(w3_raw[:, m, i, 128 * j:128 * (j + 1)], dest[:, j, off + 128 * i:off + 128 * (i + 1)])
                       for i in range(2) for j in range(2)]
        nb = len(blocks)

        def prepare_weights_pe(pe):
            pe.wait_ge(loaded_w, 16 * n_loads)
            pe.wait_ge(const_ready, 5)
            for n, (a, _o) in enumerate(blocks):
                wait_if(pe, setup_tc, n - 1)
                nc.tensor.transpose(bank[n % 2][:, 0:128], a, ident[:, :]).then_inc(setup_tr, 1)
            pe.wait_ge(setup_tc, nb)
            for i in range(2):
                for j in range(4):
                    last = nc.tensor.matmul(bank[2 + i][:, :], wm1_t[:, j, 128 * i:128 * (i + 1)], w1_raw[:, j, :],
                                            start=(j == 0), stop=(j == 3))
            last.then_inc(setup_mm, 1)
            for j in range(4):
                for i in range(2):
                    last = nc.tensor.matmul(bank[4][:, j:j + 1], wm1_raw[:, i, 128 * j:128 * (j + 1)],
                                            be1_c[:, i:i + 1], start=(i == 0), stop=(i == 1))
            last.then_inc(setup_mm, 1)
            for j in range(4):
                last = nc.tensor.matmul(bank[5][0:1, 0:D], be2_c[:, j:j + 1], wm2[:, j, :],
                                        start=(j == 0), stop=(j == 3))
            last.then_inc(setup_mm, 1)
            for m in range(2):
                for i in range(2):
                    for j in range(2):
                        last = nc.tensor.matmul(bank[7][:, 2 * i + m:2 * i + m + 1],
                                                w3_raw[:, m, j, 128 * i:128 * (i + 1)],
                                                wa_c[:, j:j + 1], start=(j == 0), stop=(j == 1))
            last.then_inc(setup_mm, 1)
            pe.wait_ge(setup_w, 3)
            for j in range(4):
                last = nc.tensor.matmul(bank[6][0:1, :], bm_c[:, j:j + 1], w1_raw[:, j, :],
                                        start=(j == 0), stop=(j == 3))
            last.then_inc(setup_mm, 1)

        def prepare_weights_dve(dve):
            for n, (_a, o) in enumerate(blocks):
                dve.wait_ge(setup_tr, n + 1)
                nc.vector.tensor_copy(o, bank[n % 2][:, 0:128]).then_inc(setup_tc, 1)
            dve.wait_ge(setup_mm, 2)
            for i in range(2):
                nc.vector.tensor_scalar(w11[:, i, :], bank[2 + i][:, :], g1_c[:, i:i + 1], None, ALU.mult)\
                    .then_inc(setup_w, 1)
            nc.vector.tensor_tensor(bm_c, bank[4][:, 0:4], bm1_c, ALU.add).then_inc(setup_w, 1)
            dve.wait_ge(setup_mm, 3)
            nc.vector.tensor_tensor(bm2_r[0:1, :], bank[5][0:1, 0:D], bm2_r[0:1, :], ALU.add)
            for j in range(4):
                nc.vector.tensor_scalar(wm2[:, j, :], wm2[:, j, :], g2_c[:, j:j + 1], None, ALU.mult)
            dve.wait_ge(setup_mm, 4)
            lin = bank[7][:, 0:4].rearrange("p (a b) -> p a b", a=2)
            nc.vector.tensor_scalar(wlin[:, :, 0:4:2], lin, 0.2, None, ALU.mult)
            nc.vector.tensor_scalar(wlin[:, :, 1:4:2], lin, -0.2, None, ALU.mult)
            nc.vector.tensor_scalar(wa_b[:, 0:D], wa_b[:, 0:D], 0.8, None, ALU.mult)
            nc.vector.memset(wa_b[:, D:D + 1], 1.0)
            nc.vector.memset(wa_b[:, D + 1:D + 2], -1.0)
            dve.wait_ge(setup_mm, 5)
            nc.vector.tensor_copy(b11_r[0:1, :], bank[6][0:1, :])

        def slots_by(nodes_i, name, local, address, tile_of_pair, tile_i):
            step = sem(f"{name}_step")
            counted, summed, passed = sem(f"{name}_counted"), sem(f"{name}_summed"), sem(f"{name}_passed")

            def on_dve(dve):
                done = [0]

                def link(ins):
                    done[0] += 1
                    ins.then_inc(step, 1)
                    dve.wait_ge(step, done[0])

                link(nc.vector.tensor_copy(node_f, nodes_i))
                link(nc.vector.tensor_scalar(tmp, node_f, 1.0 / P, 0.5 / P - 0.5, ALU.mult, ALU.add))
                link(nc.vector.tensor_scalar(tmp, tmp, ROUND, None, ALU.add))
                link(nc.vector.tensor_scalar(hi, tmp, ROUND, None, ALU.subtract))
                nc.vector.scalar_tensor_tensor(local, hi, -float(P), node_f, ALU.mult, ALU.add)
                for b in range(0, TILES, 5):
                    for k in range(5):
                        nc.vector.tensor_scalar(five_masks[:, k, :], hi, float(b + k), None, ALU.is_equal)\
                            .then_inc(step, 1)
                    done[0] += 5
                    dve.wait_ge(step, done[0])
                    link(nc.vector.tensor_reduce(count[:, b:b + 5], five_masks, AX.X, ALU.add))
                dve.sem_inc(counted, 1)
                dve.wait_ge(summed, 1)
                link(nc.vector.tensor_scalar(bucket_c, bank[0][0:TILES, 0:1], 1.0 / PAIR,
                                             (PAIR - 1.0) / PAIR - 0.5 + 0.5 / PAIR, ALU.mult, ALU.add))
                link(nc.vector.tensor_scalar(bucket_c, bucket_c, ROUND, None, ALU.add))
                nc.vector.tensor_scalar(bucket_c, bucket_c, ROUND, None, ALU.subtract).then_inc(counted, 1)
                dve.wait_ge(summed, 2)
                link(nc.vector.tensor_copy(first_c, bank[1][0:TILES, 0:1]))
                nc.vector.tensor_scalar(diag, ident[0:TILES, 0:TILES], first_c, float(PAIR), ALU.mult, ALU.mult)\
                    .then_inc(counted, 1)
                nc.vector.tensor_scalar(atleast, iota_n[0:TILES, 0:PAIRS], first_c, None, ALU.is_ge)\
                    .then_inc(counted, 1)
                dve.wait_ge(summed, 3)
                link(nc.vector.tensor_scalar(start, bank[2][0:P, 0:TILES], -1.0, None, ALU.add))
                dve.wait_ge(summed, 4)
                link(nc.vector.tensor_scalar(tile_of_pair, bank[3][:, 0:PAIRS], -1.0, None, ALU.add))
                nc.vector.tensor_copy(tile_i[0:1, :], tile_of_pair[0:1, :])

                masks, ranks, base = (mask, tmp), (rank, node_f), done[0]

                def make_mask(b, q):
                    if not isinstance(b, int) or b > 1:
                        dve.wait_ge(step, b * 3 + (base - 2))
                    nc.vector.tensor_copy(cell[0:P, q:q + 1], col(start, b))
                    nc.vector.tensor_scalar(masks[q], hi, col(iota_n, b), None, ALU.is_equal).then_inc(step, 1)

                def bucket(b, q):
                    dve.wait_ge(step, b * 3 + base + (1 if isinstance(b, int) and b == 0 else 0))
                    nc.vector.tensor_tensor_scan(ranks[q], ones_e, masks[q], cell[0:P, q:q + 1], ALU.mult, ALU.add)\
                        .then_inc(step, 1)
                    if not isinstance(b, int) or b < TILES - 1:
                        make_mask(b + 1, 1 - q)
                    dve.wait_ge(step, b * 3 + (base + 2))
                    dve.sem_inc(passed, 1)
                    nc.vector.copy_predicated(slot, masks[q].bitcast(I32), ranks[q]).then_inc(step, 1)
                make_mask(0, 0)
                over_tiles(dve, bucket)
                done[0] += 3 * TILES
                dve.wait_ge(step, done[0])
                link(nc.vector.tensor_scalar(tmp, slot, 1.0 / SLOTS, 0.5 / SLOTS - 0.5, ALU.mult, ALU.add))
                link(nc.vector.tensor_scalar(tmp, tmp, ROUND, None, ALU.add))
                link(nc.vector.tensor_scalar(tmp, tmp, ROUND, None, ALU.subtract))
                link(nc.vector.scalar_tensor_tensor(slot, tmp, -float(SLOTS), slot, ALU.mult, ALU.add))
                for a in address:
                    link(nc.vector.scalar_tensor_tensor(a, slot, float(CHUNKS), tmp, ALU.mult, ALU.add))

            def on_pe(pe):
                pe.wait_ge(counted, 1)
                nc.tensor.matmul(bank[0][0:TILES, 0:1], count, ones[0:P, 0:1], start=True, stop=True)\
                    .then_inc(summed, 1)
                pe.wait_ge(counted, 2)
                nc.tensor.matmul(bank[1][0:TILES, 0:1], upper[0:TILES, 0:TILES], bucket_c, start=True, stop=True)\
                    .then_inc(summed, 1)
                pe.wait_ge(counted, 4)
                nc.tensor.matmul(bank[2][0:P, 0:TILES], upper[0:P, 0:P], count, start=True, stop=False)
                nc.tensor.matmul(bank[2][0:P, 0:TILES], ones[0:TILES, 0:P], diag, start=False, stop=True)\
                    .then_inc(summed, 1)
                nc.tensor.matmul(bank[3][:, 0:PAIRS], ones[0:TILES, :], atleast, start=True, stop=True)\
                    .then_inc(summed, 1)
            return on_dve, on_pe

        source_slots_dve, source_slots_pe = slots_by(src_i, "by_src", rec_in_s[:, :, 1], (adr_s,), src_tile[:, :], src_tile_i)
        target_slots_dve, target_slots_pe = slots_by(dst_i, "by_dst", rec_in[:, :, 1], (adr_d,), dst_tile, dst_tile_i)

        def norm_vector(dve, src, width, seen, rooted, scale, own):
            n = 0
            if src is not None:
                with dve.Fori(0, TILES) as t:
                    nc.vector.bn_stats(at(stats, t, 0, 6), at(src, t, 0, width)).then_inc(own, 1)
                dve.wait_ge(own, TILES)
                n = TILES
            a_, b_ = stats[0:P, :, 1], stats[0:P, :, 4]
            sq_a, sq_b = stats[0:P, :, 2], stats[0:P, :, 5]
            nc.vector.tensor_tensor(nmr, a_, b_, ALU.subtract).then_inc(own, 1)
            nc.vector.tensor_tensor(rstd, sq_a, sq_b, ALU.add).then_inc(own, 1)
            nc.vector.tensor_tensor(mean, a_, b_, ALU.add).then_inc(own, 1)
            dve.wait_ge(own, n + 3)
            nc.vector.scalar_tensor_tensor(nmr, nmr, 0.25, nmr, ALU.mult, ALU.mult).then_inc(own, 1)
            nc.vector.tensor_scalar(rstd, rstd, 1.0 / width, EPS, ALU.mult, ALU.add).then_inc(own, 1)
            dve.wait_ge(own, n + 5)
            nc.vector.tensor_tensor(rstd, rstd, nmr, ALU.add).then_inc(seen, 1)
            dve.wait_ge(rooted, 1)
            nc.vector.reciprocal(rstd, rstd).then_inc(own, 1)
            dve.wait_ge(own, n + 6)
            if scale is not None:
                nc.vector.tensor_tensor(rstd, rstd, scale, ALU.mult).then_inc(own, 1)
                dve.wait_ge(own, n + 7)
            nc.vector.scalar_tensor_tensor(nmr, mean, -0.5, rstd, ALU.mult, ALU.mult).then_inc(seen, 1)

        def norm_root(act, seen, rooted):
            act.wait_ge(seen, 1)
            nc.scalar.activation(rstd, rstd, ACT.Sqrt).then_inc(rooted, 1)
            act.wait_ge(seen, 2)

        def norm_scalar(act, src, dest, width, func, seen, rooted, applied):
            norm_root(act, seen, rooted)
            with act.Fori(0, TILES // 5) as i:
                for k in range(5):
                    t = i * 5 + k
                    nc.scalar.activation(at(dest, t, 0, width), at(src, t, 0, width), func,
                                         bias=col(nmr, t), scale=col(rstd, t)).then_inc(applied, 1)

        def layer_norm(name, src, dest, width, func, scale=None, store=None, next_stats=False):
            own, seen, rooted, applied, stored = (sem(f"{name}_{s}") for s in ("own", "seen", "rooted", "applied", "stored"))
            with nc.Block() as block:
                @block.vector
                def _(dve):
                    norm_vector(dve, None, width, seen, rooted, scale, own)
                    if next_stats:
                        with dve.Fori(0, TILES) as t:
                            dve.wait_ge(applied, t + 1)
                            nc.vector.bn_stats(at(stats, t, 0, 6), at(dest, t, 0, width))

                @block.scalar
                def _(act):
                    norm_scalar(act, src, dest, width, func, seen, rooted, applied)

                if store is not None:
                    @block.sync
                    def _(sp):
                        table, buf, w = store
                        with sp.Fori(0, TILES) as t:
                            sp.wait_ge(applied, t + 1)
                            sp.dma_start(node_rows(table, t, 0, w), at(buf, t, 0, w)).then_inc(stored, 16)
                        sp.wait_ge(stored, 16 * TILES)

        rec_staged, scatter_go = sem("scatter_staged"), sem("scatter_go")
        sent = [sem("scatter_sent0"), sem("scatter_sent1")]
        rec_built = sem("rec_built")
        own, seen, rooted, applied, stored = (sem(f"ln0_{s}") for s in ("own", "seen", "rooted", "applied", "stored"))
        hot, counted_in = sem("hot"), sem("counted_in")
        deg_own, deg_root = sem("deg_own"), sem("deg_root")
        low_deg = small[0:P, 10, :]
        n_groups = COLS // HALF
        slots_used, source_scattered, rec_s_loaded = sem("slots_used"), sem("source_scattered"), sem("rec_s_loaded")
        with nc.Block() as block:
            @block.gpsimd
            def _(pool):
                nc.gpsimd.iota(iota_n[:, :], [[1, CHUNKS]], base=0, channel_multiplier=0,
                               allow_small_or_imprecise_dtypes=True).then_inc(const_ready, 1)
                nc.gpsimd.memset(ones[:, :], 1.0).then_inc(const_ready, 1)
                nc.gpsimd.memset(ones_e, 1.0).then_inc(const_ready, 1)
                pool.wait_ge(const_ready, 3)
                nc.gpsimd.affine_select(out=ident[:, :], in_=ones[:, :], compare_op=ALU.is_equal, fill=0.0,
                                        base=0, pattern=[[-1, 128]], channel_multiplier=1).then_inc(const_ready, 1)
                nc.gpsimd.affine_select(out=upper[:, :], in_=ones[:, :], compare_op=ALU.is_gt, fill=0.0,
                                        base=0, pattern=[[1, 128]], channel_multiplier=-1).then_inc(const_ready, 1)

                def scatter(records, before):
                    def step(it):
                        for h in range(2):
                            g = it * 2 + h
                            pool.wait_ge(rec_staged, g * 2 + (4 * before + 2))
                            pool.sem_inc(scatter_go, 1)
                            for r in range(HALF):
                                pool.indirect_dma_start(
                                    records, bass.IndirectOffsetOnAxis(ap=stage[0:P, h, r:r + 1], axis=0),
                                    stage_rec[0:P, h, r * REC:(r + 1) * REC], None).then_inc(sent[h], 16)
                    peeled(pool, n_groups // 2, step)
                pool.wait_ge(pad_stored, 32)
                scatter(records_s, 0)
                for h in range(2):
                    pool.wait_ge(sent[h], 16 * COLS // 2)
                pool.sem_inc(source_scattered, 1)
                scatter(records_d, n_groups // 2)
                for h in range(2):
                    pool.wait_ge(sent[h], 2 * 16 * COLS // 2)

            @block.vector
            def _(dve):
                for k, value in enumerate((0.0, -1.0, 0.0, 0.0)):
                    nc.vector.memset(rec_pad[:, :, k], value).then_inc(pad_ready, 1)
                dve.wait_ge(loaded_e, 48)
                dve.wait_ge(const_ready, 5)
                nc.vector.tensor_copy(rec_in_s[:, :, 0], dst_i).then_inc(rec_built, 1)
                nc.vector.tensor_copy(rec_in_s[:, :, 2], wgt).then_inc(rec_built, 1)
                nc.vector.memset(rec_in_s[:, :, 3], 0.0).then_inc(rec_built, 1)
                source_slots_dve(dve)
                dve.sem_inc(rec_built, 1)
                nc.vector.tensor_copy(rec_in[:, :, 0], src_i).then_inc(rec_built, 1)
                nc.vector.tensor_copy(rec_in[:, :, 2], wgt).then_inc(rec_built, 1)
                nc.vector.memset(rec_in[:, :, 3], 0.0).then_inc(rec_built, 1)
                dve.wait_ge(pad_stored, 32)
                target_slots_dve(dve)
                dve.sem_inc(rec_built, 1)
                dve.sem_inc(slots_used, 1)
                dve.wait_ge(loaded_x, 16)
                norm_vector(dve, x, D, seen, rooted, None, own)
                dve.wait_ge(loaded_w, 16 * n_loads)
                prepare_weights_dve(dve)

                def hots(c, q):
                    wait_if(dve, counted_in, c - (NPS - 1))
                    nc.vector.tensor_scalar(hot_node[:, q, :], iota_n[0:P, 0:P], at(rec_in, c, 1, 2), None, ALU.is_equal)
                    nc.vector.tensor_scalar(hot_tile[:, q, 0:TILES], iota_n[0:P, 0:TILES], col(hi, c), col(wgt, c),
                                            ALU.is_equal, ALU.mult)
                    nc.vector.tensor_scalar(hot_tile[:, q, TILES:2 * TILES], iota_n[0:P, 0:TILES], col(hi, c), None,
                                            ALU.is_equal).then_inc(hot, 1)

                def four(i):
                    for q in range(NPS):
                        hots(i * NPS + q, q)
                peeled(dve, COLS // NPS, four)

                dve.wait_ge(counted_in, COLS)
                done = 0
                for n, dis in enumerate((dis2, dis1)):
                    nc.vector.tensor_scalar(dis, bank[5][0:P, n * TILES:(n + 1) * TILES], 1.0, None, ALU.add)\
                        .then_inc(deg_own, 1)
                    dve.wait_ge(deg_own, done + 1)
                    nc.vector.tensor_scalar(low_deg, dis, 0.0, None, ALU.is_gt).then_inc(deg_own, 1)
                    nc.vector.tensor_scalar(deg, dis, 1e-30, None, ALU.max).then_inc(deg_own, 1)
                    dve.wait_ge(deg_root, n + 1)
                    nc.vector.reciprocal(deg, deg).then_inc(deg_own, 1)
                    dve.wait_ge(deg_own, done + 4)
                    nc.vector.tensor_tensor(dis, deg, low_deg, ALU.mult).then_inc(deg_own, 1)
                    dve.wait_ge(deg_own, done + 5)
                    done += 5
                dve.wait_ge(rec_s_loaded, 16)
                for k, field in enumerate((dst_idx, src_loc, ew_s)):
                    nc.vector.tensor_copy(field[:, :], rec_s[:, :, k])

            @block.tensor
            def _(pe):
                pe.wait_ge(const_ready, 5)
                source_slots_pe(pe)
                target_slots_pe(pe)
                pe.wait_ge(slots_used, 1)
                prepare_weights_pe(pe)

                def add_column(c, q, start, stop):
                    pe.wait_ge(hot, c + 1)
                    nc.tensor.matmul(bank[5][0:P, 0:2 * TILES], hot_node[:, q, :], hot_tile[:, q, :],
                                     start=start, stop=stop).then_inc(counted_in, 1)

                def four(i):
                    for q in range(NPS):
                        add_column(i * NPS + q, q, isinstance(i, int) and i * NPS + q == 0,
                                   isinstance(i, int) and i * NPS + q == COLS - 1)
                peeled(pe, COLS // NPS, four)

            @block.scalar
            def _(act):
                for tile, b in rows:
                    act.dma_start(tile, b.rearrange("(a n) -> a n", a=1)).then_inc(loaded_w, 16)
                for tile, b in columns:
                    act.dma_start(tile, b.rearrange("(k p) -> p k", p=128),
                                  allow_slow_non_contiguous=True).then_inc(loaded_w, 16)
                act.dma_start(wa_b[:, 0:D], L3_wa.broadcast_to([128, D])).then_inc(loaded_w, 16)

                def stage_records(address, rec_flat, before):
                    def step(it):
                        for h in range(2):
                            wait_if(act, sent[h], it * (16 * HALF) + before * (16 * HALF))
                            g = it * 2 + h
                            nc.scalar.activation(stage[0:P, h, :], col(address, g * HALF, HALF), ACT.Copy)\
                                .then_inc(rec_staged, 1)
                            nc.scalar.activation(stage_rec[0:P, h, :], col(rec_flat, g * (HALF * REC), HALF * REC),
                                                 ACT.Copy).then_inc(rec_staged, 1)
                    peeled(act, n_groups // 2, step)
                act.wait_ge(rec_built, 4)
                stage_records(adr_s, aflat[:, 6000:7600], 0)
                act.wait_ge(loaded_x, 16)
                norm_scalar(act, x, hbuf, D, ACT.Relu, seen, rooted, applied)
                act.wait_ge(rec_built, 8)
                stage_records(adr_d, flat[:, 4000:5600], n_groups // 2)
                for n in range(2):
                    act.wait_ge(deg_own, 5 * n + 3)
                    nc.scalar.activation(deg, deg, ACT.Sqrt).then_inc(deg_root, 1)

            @block.sync
            def _(sp):
                sp.dma_start(dst_i, dst_in.rearrange("(p c) -> p c", p=P)).then_inc(loaded_e, 16)
                sp.dma_start(src_i, src_in.rearrange("(p c) -> p c", p=P)).then_inc(loaded_e, 16)
                sp.dma_start(wgt, ew_in.rearrange("(p c) -> p c", p=P)).then_inc(loaded_e, 16)
                sp.dma_start(x[0:P, :, :], x_in.rearrange("(t p) f -> p t f", p=P)).then_inc(loaded_x, 16)
                for tile, w, k in weights:
                    sp.dma_start(tile[:, :, :], w.rearrange("(k p) n -> p k n", k=k)).then_inc(loaded_w, 16)
                sp.wait_ge(pad_ready, REC)
                for records in (records_s, records_d):
                    sp.dma_start(records.rearrange("(p c) k -> p c k", p=SLOTS), rec_pad).then_inc(pad_stored, 16)
                with sp.Fori(0, TILES) as t:
                    sp.wait_ge(applied, t + 1)
                    sp.dma_start(node_rows(table0, t, 0, D), at(hbuf, t, 0, D)).then_inc(stored, 16)
                sp.wait_ge(stored, 16 * TILES)
                sp.wait_ge(source_scattered, 1)
                sp.wait_ge(deg_own, 1)
                sp.dma_start(rec_s, records_s.rearrange("(p c) k -> p c k", p=SLOTS)).then_inc(rec_s_loaded, 16)
                sp.wait_ge(rec_s_loaded, 16)

        def gathered(width, r, lo=0, hi_=None):
            r = r % GROUP
            return flat[:, r * width + lo:r * width + (width if hi_ is None else hi_)]

        def arrival(it, r, uses):
            whole = CHUNKS // GROUP if r % GROUP >= CHUNKS % GROUP else STEPS
            return it * 16 + 16 * (uses * whole + 1 + r // GROUP)

        staged, go = sem("gather_staged"), sem("gather_go")

        def stage_indices(eng, copy, index, it, h, released, before):
            wait_if(eng, released, it * GROUP + (before + h * HALF - HALF))
            copy(stage[:, h, :], col(index, it * GROUP + h * HALF, HALF, 128)).then_inc(staged, 1)

        def stage_on_scalar(act, index, released, before):
            def step(it):
                for h in range(2):
                    if valid(it, h * HALF):
                        stage_indices(act, lambda o, i: nc.scalar.activation(o, i, ACT.Copy), index, it, h,
                                      released, before)
            peeled(act, STEPS, step)

        def gathers(pool, table, width, index, uses, released, before, stage_here=True):
            def step(it):
                for h in range(2):
                    if not valid(it, h * HALF):
                        continue
                    if stage_here:
                        stage_indices(pool, nc.gpsimd.tensor_copy, index, it, h, released, before)
                    pool.wait_ge(staged, it * 2 + (CHUNKS // HALF * uses + h + 1))
                    pool.sem_inc(go, 1)
                    for r in range(h * HALF, (h + 1) * HALF):
                        pool.indirect_dma_start(
                            gathered(width, r), None, table,
                            bass.IndirectOffsetOnAxis(ap=stage[:, h, r - h * HALF:r - h * HALF + 1], axis=0))\
                            .then_inc(arrived[r], 16)
            peeled(pool, STEPS, step)

        built, summed, added = sem("built"), sem("summed"), sem("added")
        sums = [0]

        def build_selector(dve, local, weight, it, r):
            c = it * GROUP + r
            if weight is None:
                return nc.vector.tensor_scalar(sel[:, r % NSEL, :], iota_n[:, 0:P], col(local, c, 1, 128), None,
                                               ALU.is_equal)
            return nc.vector.tensor_scalar(sel[:, r % NSEL, :], iota_n[:, 0:P], col(local, c, 1, 128),
                                           col(weight, c, 1, 128), ALU.is_equal, ALU.mult)

        def tile_of(eng, tile_i, it, r):
            return eng.value_load(col(tile_i, it * (GROUP // 2) + r // 2, 1, 1), min_val=0, max_val=TILES - 1)

        bias_spread, bias_added, rec_d_loaded = sem("bias_spread"), sem("bias_added"), sem("rec_d_loaded")
        spreads = [0]

        def spread_biases(pe, biases, free_bank):
            spreads[0] += 1
            for i, row in enumerate(biases):
                last = nc.tensor.matmul(bank[free_bank][0:P, 0:D], ones[0:1, 0:P], row, start=(i == 0),
                                        stop=(i == len(biases) - 1))
            last.then_inc(bias_spread, 1)

        def add_biases(dve, free_bank):
            dve.wait_ge(bias_spread, spreads[0])
            row = bank[free_bank][0:P, 0:D].rearrange("p (a b) -> p a b", a=1).broadcast_to([P, TILES, D])
            nc.vector.tensor_tensor(x[0:P, :, :], x[0:P, :, :], row, ALU.add).then_inc(bias_added, 1)

        def sum_over_edges(table, width, weight=None, by_source=False, biases=(), first=False, aside=None):
            index, local, tile_i = (dst_idx, src_loc, src_tile_i) if by_source else (src_idx, dst_loc, dst_tile_i)
            uses, before = passes[0], sums[0]
            passes[0] += 1
            sums[0] += CHUNKS
            before2 = before // 2

            with nc.Block() as block:
                @block.gpsimd
                def _(pool):
                    gathers(pool, table, width, index, uses, summed, before, stage_here=aside is not None)

                @block.tensor
                def _(pe):
                    def step(it, r):
                        if not valid(it, r):
                            return
                        q = r // 2 % NPS
                        pe.wait_ge(built, it * GROUP + (before + r + 1))
                        if r % 2 == 0:
                            wait_if(pe, added, it * (GROUP // 2) + (before2 + r // 2 + 1 - NPS))
                        pe.wait_ge(arrived[r], arrival(it, r, uses))
                        nc.tensor.matmul(bank[q][0:P, 0:width], sel[:, r % NSEL, :], gathered(width, r),
                                         start=(r % 2 == 0), stop=(r % 2 == 1)).then_inc(summed, 1)
                    if biases:
                        spread_biases(pe, biases, 7)
                    run_steps(pe, 0, 0, step, aside and (lambda it, r: aside[0](pe, it, r)))

                @block.scalar
                def _(act):
                    if aside is not None:
                        aside[2](act)
                    else:
                        stage_on_scalar(act, index, summed, before)

                if first:
                    @block.sync
                    def _(sp):
                        sp.dma_start(rec_d, records_d.rearrange("(p c) k -> p c k", p=SLOTS)).then_inc(rec_d_loaded, 16)

                @block.vector
                def _(dve):
                    def build(it, r):
                        wait_if(dve, summed, it * GROUP + (before + r + 1 - NSEL))
                        build_selector(dve, local, weight, it, r).then_inc(built, 1)

                    def add(it, r):
                        pair = it * (GROUP // 2) + (before2 + r // 2)
                        tile = tile_of(dve, tile_i, it, r)
                        dve.wait_ge(summed, it * GROUP + (before + r + 1))
                        wait_if(dve, added, pair)
                        row = at(acc, tile, 0, width)
                        nc.vector.tensor_tensor(row, bank[r // 2 % NPS][0:P, 0:width], row, ALU.add).then_inc(added, 1)

                    def step(it, r):
                        if valid(it, r + 4):
                            build(it, r + 4)
                        if valid(it, r) and r % 2 == 1:
                            add(it, r)
                    if first:
                        nc.vector.memset(acc[0:P, :, 0:D], 0.0)
                        dve.wait_ge(rec_d_loaded, 16)
                        for k, field in enumerate((src_idx, dst_loc, ew)):
                            nc.vector.tensor_copy(field[:, :], rec_d[:, :, k])
                    if biases:
                        add_biases(dve, 7)
                    run_steps(dve, 4, 0, step, aside and (lambda it, r: aside[1](dve, it, r)))

        xt = flat[:, 0:2 * H].rearrange("p (a b) -> p a b", a=2)
        tile_in = sb("tile_in", [128, 2, H + 2])

        turned, copied, multiplied, finished, ready = (sem(f"tiles_{s}") for s in (
            "turned", "copied", "multiplied", "finished", "ready"))
        projected = [0]

        def project(name, src, kt, w, n, bias, finish, on_scalar, aug=None, scale=None, store=None,
                    narrow=None, stats_of=None, touch=None, norm=None):
            width = 128 * kt + (1 if aug is not None else 0)
            base = projected[0]
            projected[0] += TILES
            if store is not None:
                stored = sem(f"{name}_stored")
            if touch is not None:
                touched = sem(f"{name}_touched")
            if norm is not None:
                own, seen, rooted = (sem(f"{name}_{s}") for s in ("own", "seen", "rooted"))
            copy = nc.vector if on_scalar else nc.scalar
            with nc.Block() as block:
                @block.tensor
                def _(pe):
                    def turn(t, q):
                        pe.wait_ge(ready, t + (base + 1))
                        wait_if(pe, copied, t + (base - 1))
                        for k in range(kt):
                            last = nc.tensor.transpose(bank[q][:, k * P:(k + 1) * P], tile_in[0:P, q, 128 * k:128 * (k + 1)],
                                                       ident[0:P, 0:P])
                        if aug is not None:
                            last = nc.tensor.transpose(bank[q][0:2, kt * P:(kt + 1) * P], tile_in[0:P, q, 128 * kt:128 * kt + 2],
                                                       ident[0:P, 0:P])
                        last.then_inc(turned, 1)

                    def multiply(t, q):
                        pe.wait_ge(copied, t + (base + 1))
                        wait_if(pe, finished, t + (base - 1))
                        o = bank[2 + q][0:P, 0:n]
                        for k in range(kt):
                            last = nc.tensor.matmul(o, xt[:, q, k * P:(k + 1) * P], w[:, k, 0:n], start=(k == 0),
                                                    stop=(k == kt - 1 and bias is None and aug is None))
                        if bias is not None:
                            last = nc.tensor.matmul(o, ones[0:1, 0:P], bias[0:1, 0:n], start=False, stop=True)
                        if aug is not None:
                            last = nc.tensor.matmul(o, xt[0:2, q, kt * P:(kt + 1) * P], aug[0:2, 0:n],
                                                    start=False, stop=True)
                        if narrow is not None:
                            for k in range(kt):
                                last = nc.tensor.matmul(bank[4 + q][0:P, 0:4], xt[:, q, k * P:(k + 1) * P],
                                                        narrow[0][:, k, :], start=(k == 0), stop=(k == kt - 1))
                        last.then_inc(multiplied, 1)

                    turn(0, 0)
                    turn(1, 1)
                    multiply(0, 0)
                    with pe.Fori(1, TILES // 2) as i:
                        turn(i * 2, 0)
                        multiply(i * 2 - 1, 1)
                        turn(i * 2 + 1, 1)
                        multiply(i * 2, 0)
                    turn(TILES - 1, 0)
                    multiply(TILES - 2, 1)
                    multiply(TILES - 1, 0)

                def copy_tile(eng, t, q):
                    eng.wait_ge(turned, t + (base + 1))
                    wait_if(eng, multiplied, t + (base - 1))
                    parts = ([(128, 0, kt * P)] if kt else []) + ([(2, kt * P, (kt + 1) * P)] if aug is not None else [])
                    for n_part, lo, hi_ in parts:
                        if on_scalar:
                            last = nc.vector.tensor_copy(xt[0:n_part, q, lo:hi_], bank[q][0:n_part, lo:hi_])
                        else:
                            last = nc.scalar.activation(xt[0:n_part, q, lo:hi_], bank[q][0:n_part, lo:hi_], ACT.Copy)
                    last.then_inc(copied, 1)

                def finish_tile(eng, t, q):
                    eng.wait_ge(multiplied, t + (base + 1))
                    if narrow is not None:
                        narrow[1](t, bank[4 + q][0:P, 0:4])
                    finish(t, bank[2 + q][0:P, 0:n]).then_inc(finished, 1)

                def scale_tile(dve, t, q):
                    wait_if(dve, turned, t + (base - 1))
                    nc.vector.tensor_scalar(tile_in[0:P, q, 0:width], at(src, t, 0, width), col(scale, t), None,
                                            ALU.mult).then_inc(ready, 1)

                def norm_tile(act, t, q):
                    wait_if(act, turned, t + (base - 1))
                    nc.scalar.activation(tile_in[0:P, q, 0:width], at(src, t, 0, width), norm,
                                         bias=col(nmr, t), scale=col(rstd, t)).then_inc(ready, 1)

                def feed_and_handle(eng, feed, handle):
                    def pair(i):
                        for q in range(2):
                            feed(eng, i * 2 + (q + 2), q)
                            handle(eng, i * 2 + q, q)
                    feed(eng, 0, 0)
                    feed(eng, 1, 1)
                    pair(0)
                    with eng.Fori(1, TILES // 2 - 1) as i:
                        pair(i)
                    feed(eng, TILES - 1, 0)
                    handle(eng, TILES - 3, 0)
                    handle(eng, TILES - 2, 1)
                    handle(eng, TILES - 1, 0)

                @block.vector
                def _(dve):
                    lag = 2 if on_scalar else 1

                    def take_stats(t):
                        dve.wait_ge(finished, t + (base + 1))
                        nc.vector.bn_stats(at(stats, t, 0, 6), at(stats_of[0], t, 0, stats_of[1]))

                    def touch_tile(t):
                        dve.wait_ge(finished, t + (base + 1))
                        touch(t).then_inc(touched, 1)

                    later = take_stats if stats_of is not None else touch_tile if touch is not None else None

                    def handle(dve, t, q):
                        (copy_tile if on_scalar else finish_tile)(dve, t, q)
                        if later is not None and (not isinstance(t, int) or t >= lag):
                            later(t - lag)

                    def last_ones():
                        if later is not None:
                            for t in range(TILES - lag, TILES):
                                later(t)

                    if norm is not None:
                        norm_vector(dve, None, width, seen, rooted, None, own)
                    if scale is None:
                        over_tiles(dve, lambda t, q: handle(dve, t, q))
                    else:
                        feed_and_handle(dve, scale_tile, handle)
                    last_ones()

                if scale is None and norm is None:
                    @block.gpsimd
                    def _(pool):
                        def copy_in(t, q):
                            wait_if(pool, turned, t + (base - 1))
                            nc.gpsimd.tensor_copy(tile_in[0:P, q, 0:width], at(src, t, 0, width)).then_inc(ready, 1)
                        over_tiles(pool, copy_in)

                @block.scalar
                def _(act):
                    handle = finish_tile if on_scalar else copy_tile
                    if norm is None:
                        over_tiles(act, lambda t, q: handle(act, t, q))
                    else:
                        norm_root(act, seen, rooted)
                        feed_and_handle(act, norm_tile, handle)

                if store is not None:
                    @block.sync
                    def _(sp):
                        with sp.Fori(0, TILES) as t:
                            if touch is not None:
                                sp.wait_ge(touched, t + 1)
                            else:
                                sp.wait_ge(finished, t + (base + 1))
                            table, buf, w_ = store
                            dest = node_rows(table, t, 0, w_)
                            sp.dma_start(dest, at(buf, t, 0, w_)).then_inc(stored, 16)
                        sp.wait_ge(stored, 16 * TILES)

        def add_to_x(t, o):
            return nc.vector.tensor_tensor(at(x, t, 0, D), o, at(x, t, 0, D), ALU.add)

        sum_over_edges(table0, D, weight=ew_s, by_source=True, biases=(b0_r[0:1, :],), first=True)
        project("l0p", acc, 2, w0, D, None, add_to_x, on_scalar=False, stats_of=(x, D))

        layer_norm("ln1", x, hbuf, D, ACT.Relu, next_stats=True)

        def skip_path():
            base = projected[0]
            projected[0] += TILES
            h_tile, h_turned = tile_in[0:P, 0, 0:D], tile_in[:, 1, 0:2 * P]

            def on_pe(pe, t, r):
                if r == 4:
                    pe.wait_ge(ready, t + (base + 1))
                    for k in range(2):
                        last = nc.tensor.transpose(bank[5][:, k * P:(k + 1) * P], h_tile[:, 128 * k:128 * (k + 1)],
                                                   ident[0:P, 0:P])
                    last.then_inc(turned, 1)
                if r == 10:
                    pe.wait_ge(copied, t + (base + 1))
                    wait_if(pe, finished, t + base)
                    for k in range(2):
                        last = nc.tensor.matmul(bank[6][0:P, 0:D], h_turned[:, k * P:(k + 1) * P], wsk[:, k, :],
                                                start=(k == 0), stop=(k == 1))
                    last.then_inc(multiplied, 1)

            def on_dve(dve, t, r):
                if r == 14:
                    dve.wait_ge(multiplied, t + (base + 1))
                    add_to_x(t, bank[6][0:P, 0:D]).then_inc(finished, 1)

            def on_act(act):
                with act.Fori(0, TILES) as t:
                    act.wait_ge(turned, t + base)
                    nc.scalar.activation(h_tile, at(hbuf, t, 0, D), ACT.Copy).then_inc(ready, 1)
                    act.wait_ge(turned, t + (base + 1))
                    act.wait_ge(multiplied, t + base)
                    nc.scalar.activation(h_turned, bank[5][:, 0:2 * P], ACT.Copy).then_inc(copied, 1)
            return on_pe, on_dve, on_act
        with nc.Block() as block:
            @block.vector
            def _(dve):
                nc.vector.tensor_copy(acc[0:P, :, D], dis1)
                nc.vector.memset(tile_in[:, :, D + 1:D + 2], 1.0)
        layer_norm("ln1b", hbuf, acc, D, ACT.Identity, scale=dis1, store=(table1, acc, D + 1))
        sum_over_edges(table1, D + 1, aside=skip_path())
        project("l1p", acc, 2, w11, H, None,
                lambda t, o: nc.scalar.activation(at(acc, t, 0, H), o, ACT.Gelu), on_scalar=True,
                aug=b11_r, scale=dis1, store=(table2, acc, H),
                touch=lambda t: nc.vector.tensor_scalar(at(acc, t, 0, H), at(acc, t, 0, H), col(dis1, t), None, ALU.mult))


        sum_over_edges(table2, H, biases=(bs_r[0:1, :], bm2_r[0:1, :]))
        project("l1q", acc, 4, w2, H, b2_r,
                lambda t, o: nc.scalar.activation(at(acc, t, 0, H), o, ACT.Gelu), on_scalar=True,
                scale=dis1, stats_of=(acc, H))
        project("l1o", acc, 4, wm2, D, None, add_to_x, on_scalar=False, stats_of=(x, D), norm=ACT.Identity)

        layer_norm("ln3", x, acc, D, ACT.Relu, scale=dis2, store=(table3, acc, D))
        sum_over_edges(table3, D, weight=ew, biases=(l2b2_r[0:1, :],))
        project("l2p", acc, 2, l2w1, D, l2b1_r,
                lambda t, o: nc.scalar.activation(at(acc, t, 0, D), o, ACT.Copy, scale=col(dis2, t)),
                on_scalar=True, scale=dis2, store=(table4, acc, D),
                touch=lambda t: nc.vector.scalar_tensor_tensor(
                    at(acc, t, 0, D), at(acc, t, 0, D), 0.01, at(acc, t, 0, D), ALU.mult, ALU.max))
        sum_over_edges(table4, D, weight=ew)
        project("l2q", acc, 2, l2w2, D, None, add_to_x, on_scalar=False, scale=dis2, stats_of=(x, D))


        def keep_projections(t, o):
            nc.scalar.activation(at(acc, t, 0, D), o[:, 0:D], ACT.Copy)
            return nc.scalar.activation(at(hbuf, t, 0, D), o[:, D:2 * D], ACT.Copy)

        def keep_narrow(t, o):
            nc.scalar.activation(at(acc, t, D, D + 2), o[:, 0:2], ACT.Copy)
            nc.scalar.activation(at(hbuf, t, D, D + 2), o[:, 2:4], ACT.Copy)
        project("l3p", x, 2, wst, 2 * D, None, keep_projections, on_scalar=True, norm=ACT.Relu,
                narrow=(wlin, keep_narrow), store=(table_pt, hbuf, D + 2))

        WPT = D + 2
        turned_sel = [acc[0:P, q, WPT:WPT + SLOTS] for q in range(NPS)]
        a_built, a_turned, a_copied, expanded, zed, scored = (sem(f"att_{s}") for s in (
            "built", "turned", "copied", "expanded", "zed", "scored"))

        own_sel = [acc[:, 2 * NPS + q // 2, WPT + q % 2 * P:WPT + (q % 2 + 1) * P] for q in range(GROUP)]

        def build_own(local, it, r):
            return nc.vector.tensor_scalar(own_sel[r % GROUP], iota_n[:, 0:P], col(local, it * GROUP + r, 1, 128),
                                           None, ALU.is_equal).then_inc(a_built, 1)

        def turn(pe, it, r, before):
            pe.wait_ge(a_built, it * GROUP + (before + r + 1))
            nc.tensor.transpose(bank[4 + r % 2][0:P, 0:SLOTS], own_sel[r % GROUP], ident[:, :]).then_inc(a_turned, 1)

        def copy_turned(act, it, r, before):
            act.wait_ge(a_turned, it * GROUP + (before + r + 1))
            wait_if(act, expanded, it * GROUP + (before + r + 1 - NPS))
            nc.scalar.activation(turned_sel[r % NPS], bank[4 + r % 2][0:P, 0:SLOTS], ACT.Copy).then_inc(a_copied, 1)

        def expand(pe, own_rows, tile, it, r, uses, before):
            pe.wait_ge(a_copied, it * GROUP + (before + r + 1))
            pe.wait_ge(arrived[r % GROUP], arrival(it, r, uses))
            wait_if(pe, zed, it * GROUP + (before + r + 1 - NPS))
            nc.tensor.matmul(bank[r % NPS][:, 0:WPT], turned_sel[r % NPS], at(own_rows, tile, 0, WPT),
                             start=True, stop=True).then_inc(expanded, 1)

        def add_rows(dve, width, it, r, before):
            dve.wait_ge(expanded, it * GROUP + (before + r + 1))
            z = gathered(width, r, 0, WPT)
            nc.vector.tensor_tensor(z, bank[r % NPS][:, 0:WPT], z, ALU.add).then_inc(zed, 1)

        def take_score(dve, width, it, r, before):
            dve.wait_ge(zed, it * GROUP + (before + r + 1))
            z = gathered(width, r, 0, WPT)
            c = r % GROUP
            nc.vector.scalar_tensor_tensor(z, z, 0.0, wa_b[:, :], ALU.max, ALU.mult, accum_out=escore[:, c:c + 1])\
                .then_inc(scored, 1)

        QUAD = 4
        o = flat.shape[1] - 4 * CHUNKS
        grid = [acc[:, NPS + q, WPT:WPT + P] for q in range(NPS)]
        neg_loc = flat[:, o:o + CHUNKS]
        cmax = flat[0:P, o + CHUNKS:o + 2 * CHUNKS]
        csum = flat[0:P, o + 2 * CHUNKS:o + 3 * CHUNKS]
        cneg = flat[0:P, o + 3 * CHUNKS:o + 4 * CHUNKS]
        squared, gridded, g_turned, maxed, negged, g_summed, flipped = (sem(f"grid_{s}") for s in (
            "squared", "gridded", "turned", "maxed", "negged", "summed", "flipped"))
        uses1 = passes[0]
        passes[0] += 1
        with nc.Block() as block:
            @block.gpsimd
            def _(pool):
                gathers(pool, table_pt, WPT, dst_idx, uses1, scored, 0)

            @block.tensor
            def _(pe):
                tile = [None]

                def turn_grid(it, r):
                    q, k = r // QUAD % 2, r % QUAD
                    pe.wait_ge(gridded, it * GROUP + (r + 1))
                    if k == 0:
                        wait_if(pe, g_summed, it * GROUP + (r - QUAD))
                    nc.tensor.transpose(bank[6 + q][0:P, k * SLOTS:(k + 1) * SLOTS], grid[r % NPS], ident[:, :])\
                        .then_inc(g_turned, 1)

                def step(it, r):
                    if valid(it, r + 1):
                        if r % 2 == 1 or r == 0:
                            tile[0] = tile_of(pe, src_tile_i, it, r + 1)
                        expand(pe, acc, tile[0], it, r + 1, uses1, 0)
                    if valid(it, r + 3):
                        turn(pe, it, r + 3, 0)
                    if valid(it, r - 4):
                        turn_grid(it, r - 4)
                run_steps(pe, 3, 4, step)

            @block.scalar
            def _(act):
                def square(it, r):
                    wait_if(act, g_turned, it * GROUP + (r + 1 - NPS))
                    nc.scalar.activation(grid[r % NPS], iota_n[:, 0:P], ACT.Square,
                                         bias=col(neg_loc, it * GROUP + r, 1, 128)).then_inc(squared, 1)

                def make_grid(it, r):
                    act.wait_ge(scored, it * GROUP + (r + 1))
                    act.wait_ge(squared, it * GROUP + (r + 1))
                    nc.scalar.activation(grid[r % NPS], grid[r % NPS], ACT.Identity, scale=LOW,
                                         bias=escore[:, r % GROUP:r % GROUP + 1]).then_inc(gridded, 1)

                def exps(it, r, k):
                    if k == 0:
                        act.wait_ge(negged, it * (GROUP // QUAD) + (r // QUAD + 1))
                    g = bank[6 + r // QUAD % 2][0:P, k * SLOTS:(k + 1) * SLOTS]
                    c = it * GROUP + (r - (QUAD - 1) + k)
                    nc.scalar.activation(g, g, ACT.Exp, bias=col(cneg, c), scale=1.0, accum_out=col(csum, c))\
                        .then_inc(g_summed, 1)

                act.wait_ge(flipped, 1)

                def step(it, r):
                    if valid(it, r + 2):
                        copy_turned(act, it, r + 2, 0)
                    if valid(it, r - 1):
                        square(it, r - 1)
                    if valid(it, r - 3):
                        make_grid(it, r - 3)
                    half = (r - 1) % QUAD
                    if half < 2 and valid(it, r - 6 - half):
                        exps(it, r - 6 - half, 2 * half)
                        exps(it, r - 6 - half, 2 * half + 1)
                run_steps(act, 2, 8, step)

            @block.vector
            def _(dve):
                nc.vector.tensor_scalar(neg_loc, src_loc[:, :], -1.0, None, ALU.mult).then_inc(flipped, 1)

                def score(it, r):
                    wait_if(dve, gridded, it * GROUP + (r + 1 - GROUP))
                    take_score(dve, WPT, it, r, 0)

                def largest(it, r):
                    dve.wait_ge(g_turned, it * GROUP + (r + 1))
                    c = it * GROUP + (r - (QUAD - 1))
                    nc.vector.tensor_reduce(
                        col(cmax, c, QUAD), bank[6 + r // QUAD % 2][0:P, :].rearrange("p (a b) -> p a b", a=QUAD),
                        AX.X, ALU.max).then_inc(maxed, 1)

                def negate(it, r):
                    dve.wait_ge(maxed, it * (GROUP // QUAD) + (r // QUAD + 1))
                    c = it * GROUP + (r - (QUAD - 1))
                    nc.vector.tensor_scalar(col(cneg, c, QUAD), col(cmax, c, QUAD), -1.0, None, ALU.mult)\
                        .then_inc(negged, 1)

                def step(it, r):
                    if valid(it, r - 5) and (r - 5) % QUAD == QUAD - 1:
                        largest(it, r - 5)
                    if valid(it, r + 5):
                        build_own(src_loc, it, r + 5)
                    if valid(it, r - 5) and (r - 5) % QUAD == QUAD - 1:
                        negate(it, r - 5)
                    if valid(it, r):
                        add_rows(dve, WPT, it, r, 0)
                    if valid(it, r - 1):
                        score(it, r - 1)
                run_steps(dve, 5, 6, step)

        outside = flat[0:P, 0:TILES * PAIRS].rearrange("p (t k) -> p t k", t=TILES)
        pmax, psum_, pm = (flat[0:P, TILES * PAIRS + k * PAIRS:TILES * PAIRS + (k + 1) * PAIRS] for k in range(3))
        work = acc[0:P, :, WPT:WPT + PAIRS]
        cexp = neg_loc[0:P, :]
        chunks_of = lambda buf: [buf.rearrange("p (a b) -> p a b", b=2)[:, :, k] for k in range(2)]
        over_all = lambda row: row.rearrange("p (a b) -> p a b", a=1).broadcast_to([P, TILES, PAIRS])
        per_tile = lambda c: c.rearrange("p (a b) -> p a b", b=1).broadcast_to([P, TILES, PAIRS])
        step_, exp_ready, exp_done = sem("comb_step"), sem("comb_exp_ready"), sem("comb_exp_done")
        top_copied, scales_ready, ps_stored, h_made, h_stored = (sem(f"source_{s}") for s in (
            "top_copied", "scales_ready", "ps_stored", "h_made", "h_stored"))
        total = small[0:P, 5, :]
        with nc.Block() as block:
            @block.vector
            def _(dve):
                done = [0]

                def link(ins):
                    done[0] += 1
                    ins.then_inc(step_, 1)
                    dve.wait_ge(step_, done[0])

                (max0, max1), (sum0, sum1) = chunks_of(cmax), chunks_of(cexp)
                with dve.Fori(0, TILES) as t:
                    nc.vector.tensor_scalar(at(outside, t, 0, PAIRS), src_tile[0:P, :], col(iota_n, t), LOW,
                                            ALU.not_equal, ALU.mult).then_inc(step_, 1)
                done[0] += TILES
                link(nc.vector.tensor_tensor(pmax, max0, max1, ALU.max))
                link(nc.vector.tensor_tensor(work, outside, over_all(pmax), ALU.add))
                link(nc.vector.tensor_reduce(top[0:P, :], work, AX.X, ALU.max))
                link(nc.vector.scalar_tensor_tensor(work, outside, 0.0, per_tile(top[0:P, :]), ALU.is_equal, ALU.mult))
                link(nc.vector.tensor_reduce(pm, work.rearrange("p t k -> p k t"), AX.X, ALU.add))
                link(nc.vector.tensor_tensor(sum0, max0, pm, ALU.subtract))
                nc.vector.tensor_tensor(sum1, max1, pm, ALU.subtract).then_inc(exp_ready, 1)
                dve.wait_ge(ps_stored, 16)
                nc.vector.tensor_copy(acc[0:P, :, D - 1], top[0:P, :]).then_inc(top_copied, 1)
                dve.wait_ge(exp_done, 1)
                link(nc.vector.tensor_tensor(cexp, cexp, csum, ALU.mult))
                link(nc.vector.tensor_tensor(psum_, sum0, sum1, ALU.add))
                link(nc.vector.scalar_tensor_tensor(work, outside, 0.0, over_all(psum_), ALU.is_equal, ALU.mult))
                link(nc.vector.tensor_reduce(total, work, AX.X, ALU.add))
                link(nc.vector.tensor_scalar(total, total, 1e-30, None, ALU.max))
                link(nc.vector.reciprocal(total, total))
                nc.vector.tensor_tensor(rstd, rstd, total, ALU.mult).then_inc(scales_ready, 1)
                nc.vector.tensor_tensor(nmr, nmr, total, ALU.mult).then_inc(scales_ready, 1)
                nc.vector.memset(acc[0:P, :, 0:D - 1], 0.0)
                dve.wait_ge(h_stored, 16 * TILES)
                nc.vector.memset(acc[0:P, :, D - 1:D], 0.0)

            @block.sync
            def _(sp):
                sp.dma_start(table_src.rearrange("(t p) f -> p t f", p=P)[:, :, 0:WPT], acc[0:P, :, 0:WPT])\
                    .then_inc(ps_stored, 16)
                sp.wait_ge(top_copied, 1)
                with sp.Fori(0, TILES) as t:
                    sp.wait_ge(h_made, t + 1)
                    sp.dma_start(node_rows(table_src, t, WPT, WPT + 1 + D), at(acc, t, D - 1, 2 * D))\
                        .then_inc(h_stored, 16)
                sp.wait_ge(h_stored, 16 * TILES)

            @block.scalar
            def _(act):
                act.wait_ge(exp_ready, 1)
                nc.scalar.activation(cexp, cexp, ACT.Exp).then_inc(exp_done, 1)
                act.wait_ge(scales_ready, 2)
                with act.Fori(0, TILES // 5) as i:
                    for k in range(5):
                        t = i * 5 + k
                        nc.scalar.activation(at(acc, t, D, 2 * D), at(x, t, 0, D), ACT.Relu, bias=col(nmr, t),
                                             scale=col(rstd, t)).then_inc(h_made, 1)

        WSRC = WPT + 1 + D
        lowered, exped, weighed = (sem(f"weigh_{s}") for s in ("lowered", "exped", "weighed"))
        uses2, before = passes[0], sums[0]
        passes[0] += 1
        before2 = before // 2
        with nc.Block() as block:
            @block.gpsimd
            def _(pool):
                gathers(pool, table_src, WSRC, src_idx, uses2, summed, before)

            @block.tensor
            def _(pe):
                tile = [None]

                def multiply(it, r):
                    q = r // 2 % 2
                    pe.wait_ge(weighed, it * GROUP + (r + 1))
                    if r % 2 == 0:
                        wait_if(pe, added, it * (GROUP // 2) + (before2 + r // 2 - 1))
                    nc.tensor.matmul(bank[6 + q][0:P, 0:D], own_sel[r % GROUP],
                                     gathered(WSRC, r, WPT + 1, WPT + 1 + D),
                                     start=(r % 2 == 0), stop=(r % 2 == 1)).then_inc(summed, 1)

                def step(it, r):
                    if valid(it, r + 1):
                        if r % 2 == 1 or r == 0:
                            tile[0] = tile_of(pe, dst_tile_i, it, r + 1)
                        expand(pe, hbuf, tile[0], it, r + 1, uses2, CHUNKS)
                    if valid(it, r + 3):
                        turn(pe, it, r + 3, CHUNKS)
                    if valid(it, r - 4):
                        multiply(it, r - 4)
                spread_biases(pe, (bfc_r[0:1, :],), 7)
                pe.wait_ge(bias_added, spreads[0])
                run_steps(pe, 3, 4, step)

            @block.scalar
            def _(act):
                def lower(it, r):
                    e = escore[:, r % GROUP:r % GROUP + 1]
                    act.wait_ge(scored, it * GROUP + (CHUNKS + r + 1))
                    nc.scalar.activation(e, e, ACT.Relu, bias=gathered(WSRC, r, WPT, WPT + 1), scale=-1.0)\
                        .then_inc(lowered, 1)

                def exponential(it, r):
                    e = escore[:, r % GROUP:r % GROUP + 1]
                    act.wait_ge(lowered, it * GROUP + (r + 1))
                    nc.scalar.activation(e, e, ACT.Exp, scale=-1.0).then_inc(exped, 1)

                def weigh(it, r):
                    act.wait_ge(exped, it * GROUP + (r + 1))
                    h = gathered(WSRC, r, WPT + 1, WPT + 1 + D)
                    nc.scalar.activation(h, h, ACT.Copy, scale=escore[:, r % GROUP:r % GROUP + 1]).then_inc(weighed, 1)

                def step(it, r):
                    if valid(it, r - 2):
                        lower(it, r - 2)
                    if valid(it, r + 2):
                        copy_turned(act, it, r + 2, CHUNKS)
                    if valid(it, r - 2):
                        exponential(it, r - 2)
                    if valid(it, r - 3):
                        weigh(it, r - 3)
                run_steps(act, 2, 3, step)

            @block.vector
            def _(dve):
                def add(it, r, tile):
                    dve.wait_ge(summed, it * GROUP + (before + r + 1))
                    wait_if(dve, added, it * (GROUP // 2) + (before2 + r // 2))
                    row = at(acc, tile, 0, D)
                    nc.vector.tensor_tensor(row, bank[6 + r // 2 % 2][0:P, 0:D], row, ALU.add).then_inc(added, 1)

                def step(it, r):
                    if valid(it, r + 4):
                        build_own(dst_loc, it, r + 4)
                    if valid(it, r):
                        add_rows(dve, WSRC, it, r, CHUNKS)
                    if valid(it, r - 1):
                        take_score(dve, WSRC, it, r - 1, CHUNKS)
                    if valid(it, r - 5) and r % 2 == 0:
                        add(it, r - 5, tile_of(dve, dst_tile_i, it, r - 5))
                add_biases(dve, 7)
                run_steps(dve, 4, 6, step)

        project("l3q", acc, 2, wfc, D, None, add_to_x, on_scalar=False, store=(out, x, D))


_INS = ["x", "src", "dst", "edge_weight", "L0_gnn_weight", "L0_gnn_bias", "L1_gnn_gamma1", "L1_gnn_beta1",
        "L1_gnn_gamma2", "L1_gnn_beta2", "L1_gnn_Wm1", "L1_gnn_bm1", "L1_gnn_W1", "L1_gnn_b1", "L1_gnn_W2",
        "L1_gnn_b2", "L1_gnn_Wm2", "L1_gnn_bm2", "L1_gnn_Ws", "L1_gnn_bs", "L2_gnn_W1", "L2_gnn_b1",
        "L2_gnn_W2", "L2_gnn_b2", "L3_gnn_W_s", "L3_gnn_W_t", "L3_gnn_W_attn", "L3_gnn_W_fc", "L3_gnn_b_fc"]


def kernel(**inputs):
    import numpy as _np
    import concourse.bacc as _bacc
    from concourse import mybir as _mybir
    from concourse.bass_utils import run_bass_kernel_spmd as _run

    nc = _bacc.Bacc("TRN2", target_bir_lowering=False, num_devices=1)
    arrays, args = {}, []
    for name in _INS:
        a = _np.ascontiguousarray(inputs[name])
        arrays[f"in_{name}"] = a
        args.append(nc.dram_tensor(f"in_{name}", a.shape, _mybir.dt.from_np(a.dtype), kind="ExternalInput").ap())
    args.append(nc.dram_tensor("out_x", (NODES, D), _mybir.dt.float32, kind="ExternalOutput").ap())
    gnn(nc, *args)
    r = _run(nc, [arrays], core_ids=[0])
    return r.results[0]["out_x"]
```
